# Optimizing a Trainium2 kernel written in Bass

```python
import numpy as np
import jax
import jax.numpy as jnp

def _softmax(x, axis=-1):
    return jax.nn.softmax(x, axis=axis)

def _gelu(x):
    return jax.nn.gelu(x, approximate=True)

def _silu(x):
    return jax.nn.silu(x)

def _sigmoid(x):
    return jax.nn.sigmoid(x)

def _layernorm(x, axis=-1, eps=1e-05):
    m = jnp.mean(x, axis=axis, keepdims=True)
    v = jnp.var(x, axis=axis, keepdims=True)
    return (x - m) / jnp.sqrt(v + eps)

def _scatter_add(tgt, idx, src, axis=0):
    return tgt.at[idx].add(src)

def _segment_sum(src, seg, n):
    return jax.ops.segment_sum(src, seg, n)
kernel_name = 'mk_seq_postln_d1_jaxref_r4_9d5e8f'

def setup_inputs(seed: int=0):
    np.random.seed(seed)
    _w = jnp.asarray

    def _L0_attn_setup():
        import jax, jax.numpy as jnp
        import numpy as np
        B, S, HID = (1, 1024, 512)
        NH, D = (16, 128)
        RATIO, TOPK, WIN = (4, 8, 128)
        ROPE_DIM = D // 2
        EPS = 1e-06
        NEG = -1e+30

        def rmsnorm(x, w):
            return x * jax.lax.rsqrt(jnp.mean(x * x, axis=-1, keepdims=True) + EPS) * w

        def apply_rope(x, pos):
            half = ROPE_DIM // 2
            inv = 1.0 / 10000.0 ** (jnp.arange(half, dtype=x.dtype) * (2.0 / ROPE_DIM))
            ang = pos.astype(x.dtype)[:, None] * inv[None, :]
            cos, sin = (jnp.cos(ang), jnp.sin(ang))
            x1, x2, rest = (x[..., :half], x[..., half:ROPE_DIM], x[..., ROPE_DIM:])
            return jnp.concatenate([x1 * cos - x2 * sin, x1 * sin + x2 * cos, rest], axis=-1)
        key = jax.random.key(seed)
        ks = jax.random.split(key, 16)
        n = jax.random.normal
        s = 0.02
        return {'hidden_states': n(ks[0], (B, S, HID), jnp.float32), 'Wq': n(ks[1], (HID, NH * D)) * s, 'bq': jnp.zeros((NH * D,)), 'Wcmp': n(ks[2], (HID, 1)) * s, 'bcmp': jnp.zeros((1,)), 'Wk': n(ks[3], (HID, D)) * s, 'bk': jnp.zeros((D,)), 'Wv': n(ks[4], (HID, D)) * s, 'bv': jnp.zeros((D,)), 'Wlk': n(ks[5], (HID, NH * D)) * s, 'blk': jnp.zeros((NH * D,)), 'Wlv': n(ks[6], (HID, NH * D)) * s, 'blv': jnp.zeros((NH * D,)), 'qn_w': jnp.ones((D,)), 'kn_w': jnp.ones((D,)), 'Wo': n(ks[7], (NH * D, HID)) * s, 'bo': jnp.zeros((HID,))}
    _L0_attn_in = _L0_attn_setup()

    def _L0_ffn_setup():
        import jax, jax.numpy as jnp
        import numpy as np
        DIM = 512
        INTER = 352
        E = 16
        TOPK = 4
        G = 4
        TOPK_G = 2
        N_SHARED = 2
        ROUTE_SCALE = 1.0
        INIT_STD = 0.02
        B, S = (1, 512)
        key = jax.random.key(seed)
        ks = jax.random.split(key, 9)
        std = INIT_STD
        x = jax.random.normal(ks[0], (B, S, DIM), jnp.float32)
        gate_w = jax.random.normal(ks[1], (E, DIM), jnp.float32) * std
        expert_bias = jnp.zeros((E,), jnp.float32)
        w1 = jax.random.normal(ks[2], (E, DIM, INTER), jnp.float32) * std
        w3 = jax.random.normal(ks[3], (E, DIM, INTER), jnp.float32) * std
        w2 = jax.random.normal(ks[4], (E, INTER, DIM), jnp.float32) * std
        sh = N_SHARED * INTER
        sw1 = jax.random.normal(ks[5], (DIM, sh), jnp.float32) * std
        sw3 = jax.random.normal(ks[6], (DIM, sh), jnp.float32) * std
        sw2 = jax.random.normal(ks[7], (sh, DIM), jnp.float32) * std
        return {'x': x, 'gate_w': gate_w, 'expert_bias': expert_bias, 'w1': w1, 'w2': w2, 'w3': w3, 'sw1': sw1, 'sw2': sw2, 'sw3': sw3}
    _L0_ffn_in = _L0_ffn_setup()
    _d = {'L0_attn_hidden_states': _L0_attn_in['hidden_states'], 'L0_attn_Wq': _L0_attn_in['Wq'], 'L0_attn_bq': _L0_attn_in['bq'], 'L0_attn_Wcmp': _L0_attn_in['Wcmp'], 'L0_attn_bcmp': _L0_attn_in['bcmp'], 'L0_attn_Wk': _L0_attn_in['Wk'], 'L0_attn_bk': _L0_attn_in['bk'], 'L0_attn_Wv': _L0_attn_in['Wv'], 'L0_attn_bv': _L0_attn_in['bv'], 'L0_attn_Wlk': _L0_attn_in['Wlk'], 'L0_attn_blk': _L0_attn_in['blk'], 'L0_attn_Wlv': _L0_attn_in['Wlv'], 'L0_attn_blv': _L0_attn_in['blv'], 'L0_attn_qn_w': _L0_attn_in['qn_w'], 'L0_attn_kn_w': _L0_attn_in['kn_w'], 'L0_attn_Wo': _L0_attn_in['Wo'], 'L0_attn_bo': _L0_attn_in['bo'], 'L0_ffn_gate_w': _L0_ffn_in['gate_w'], 'L0_ffn_expert_bias': _L0_ffn_in['expert_bias'], 'L0_ffn_w1': _L0_ffn_in['w1'], 'L0_ffn_w2': _L0_ffn_in['w2'], 'L0_ffn_w3': _L0_ffn_in['w3'], 'L0_ffn_sw1': _L0_ffn_in['sw1'], 'L0_ffn_sw2': _L0_ffn_in['sw2'], 'L0_ffn_sw3': _L0_ffn_in['sw3']}
    _x0 = _d['L0_attn_hidden_states']
    _d['L0_attn_hidden_states'] = jax.random.normal(jax.random.fold_in(jax.random.key(seed), 1), (1, 2048, 512), dtype=_x0.dtype)
    del _x0
    return _d

def reference(L0_attn_hidden_states, L0_attn_Wq, L0_attn_bq, L0_attn_Wcmp, L0_attn_bcmp, L0_attn_Wk, L0_attn_bk, L0_attn_Wv, L0_attn_bv, L0_attn_Wlk, L0_attn_blk, L0_attn_Wlv, L0_attn_blv, L0_attn_qn_w, L0_attn_kn_w, L0_attn_Wo, L0_attn_bo, L0_ffn_gate_w, L0_ffn_expert_bias, L0_ffn_w1, L0_ffn_w2, L0_ffn_w3, L0_ffn_sw1, L0_ffn_sw2, L0_ffn_sw3):

    def _L0_attn_ref(hidden_states, Wq, bq, Wcmp, bcmp, Wk, bk, Wv, bv, Wlk, blk, Wlv, blv, qn_w, kn_w, Wo, bo):
        import jax, jax.numpy as jnp
        import numpy as np
        B, S, HID = (1, 1024, 512)
        NH, D = (16, 128)
        RATIO, TOPK, WIN = (4, 8, 128)
        ROPE_DIM = D // 2
        EPS = 1e-06
        NEG = -1e+30

        def rmsnorm(x, w):
            return x * jax.lax.rsqrt(jnp.mean(x * x, axis=-1, keepdims=True) + EPS) * w

        def apply_rope(x, pos):
            half = ROPE_DIM // 2
            inv = 1.0 / 10000.0 ** (jnp.arange(half, dtype=x.dtype) * (2.0 / ROPE_DIM))
            ang = pos.astype(x.dtype)[:, None] * inv[None, :]
            cos, sin = (jnp.cos(ang), jnp.sin(ang))
            x1, x2, rest = (x[..., :half], x[..., half:ROPE_DIM], x[..., ROPE_DIM:])
            return jnp.concatenate([x1 * cos - x2 * sin, x1 * sin + x2 * cos, rest], axis=-1)
        Bq, Sq, _ = hidden_states.shape
        C = Sq // RATIO
        scale = 1.0 / jnp.sqrt(jnp.float32(D))
        pos = jnp.arange(Sq)
        q = (hidden_states @ Wq + bq).reshape(Bq, Sq, NH, D).transpose(0, 2, 1, 3)
        q = apply_rope(rmsnorm(q, qn_w), pos)
        w_log = (hidden_states @ Wcmp + bcmp).reshape(Bq, C, RATIO)
        w_cmp = jax.nn.softmax(w_log, axis=-1)
        entries = jnp.einsum('bcr,bcrh->bch', w_cmp, hidden_states.reshape(Bq, C, RATIO, HID))
        block_ends = jnp.arange(1, C + 1) * RATIO - 1
        ck = apply_rope(rmsnorm(entries @ Wk + bk, kn_w), block_ends)
        cv = entries @ Wv + bv
        sc = jnp.einsum('bhsd,bcd->bhsc', q, ck) * scale
        causal = block_ends[None, None, None, :] <= pos[None, None, :, None]
        sc = jnp.where(causal, sc, NEG)
        tv, ti = jax.lax.top_k(sc, TOPK)
        sel = (tv > NEG / 2).astype(sc.dtype)
        m = jnp.max(tv, axis=-1, keepdims=True)
        e = jnp.exp(tv - m) * sel
        pw = e / jnp.maximum(e.sum(axis=-1, keepdims=True), 1e-09)
        v_g = cv[jnp.arange(Bq)[:, None, None, None], ti]
        ctx_sparse = jnp.einsum('bhsk,bhskd->bhsd', pw, v_g)
        lk = apply_rope(rmsnorm((hidden_states @ Wlk + blk).reshape(Bq, Sq, NH, D).transpose(0, 2, 1, 3), kn_w), pos)
        lv = (hidden_states @ Wlv + blv).reshape(Bq, Sq, NH, D).transpose(0, 2, 1, 3)
        nc = Sq // WIN
        qc = q.reshape(Bq, NH, nc, WIN, D)

        def windowize(x):
            prev = jnp.pad(x, ((0, 0), (0, 0), (WIN, 0), (0, 0)))[:, :, :-WIN].reshape(Bq, NH, nc, WIN, D)
            cur = x.reshape(Bq, NH, nc, WIN, D)
            return jnp.concatenate([prev, cur], axis=3)
        kw, vw = (windowize(lk), windowize(lv))
        i = jnp.arange(WIN)[:, None]
        j = jnp.arange(2 * WIN)[None, :]
        rel = i + WIN - j
        band = (rel >= 0) & (rel <= WIN)
        kpos_ok = jnp.arange(nc)[:, None, None] * WIN - WIN + j[None] >= 0
        mask = band[None] & kpos_ok
        sl = jnp.einsum('bhcqd,bhckd->bhcqk', qc, kw) * scale
        sl = jnp.where(mask[None, None], sl, NEG)
        pl = jax.nn.softmax(sl, axis=-1)
        ctx_local = jnp.einsum('bhcqk,bhckd->bhcqd', pl, vw).reshape(Bq, NH, Sq, D)
        merged = (ctx_sparse + ctx_local) * 0.5
        out = merged.transpose(0, 2, 1, 3).reshape(Bq, Sq, NH * D) @ Wo + bo
        return out

    def _L0_ffn_ref(x, gate_w, expert_bias, w1, w2, w3, sw1, sw2, sw3):
        import jax, jax.numpy as jnp
        import numpy as np
        DIM = 512
        INTER = 352
        E = 16
        TOPK = 4
        G = 4
        TOPK_G = 2
        N_SHARED = 2
        ROUTE_SCALE = 1.0
        INIT_STD = 0.02
        B, S = (1, 512)
        b, s, d = x.shape
        T = b * s
        xf = x.reshape(T, d)
        scores = jax.nn.sigmoid(xf @ gate_w.T)
        original_scores = scores
        scores = scores + expert_bias
        sg = scores.reshape(T, G, E // G)
        group_scores = sg.max(axis=-1)
        _, gidx = jax.lax.top_k(group_scores, TOPK_G)
        gmask = jnp.zeros((T, G), bool).at[jnp.arange(T)[:, None], gidx].set(True)
        masked = jnp.where(gmask[:, :, None], sg, -jnp.inf).reshape(T, E)
        _, idx = jax.lax.top_k(masked, TOPK)
        w = jnp.take_along_axis(original_scores, idx, axis=1)
        w = w / jnp.sum(w, axis=-1, keepdims=True)
        w = w * ROUTE_SCALE
        cw = jnp.zeros((T, E), x.dtype).at[jnp.arange(T)[:, None], idx].add(w)
        h = jax.nn.silu(jnp.einsum('td,edh->teh', xf, w1)) * jnp.einsum('td,edh->teh', xf, w3)
        y = jnp.einsum('teh,ehd,te->td', h, w2, cw)
        z = jax.nn.silu(xf @ sw1) * (xf @ sw3) @ sw2
        return (y + z).reshape(b, s, d)
    x = L0_attn_hidden_states
    x = _layernorm(x + _L0_attn_ref(x, L0_attn_Wq, L0_attn_bq, L0_attn_Wcmp, L0_attn_bcmp, L0_attn_Wk, L0_attn_bk, L0_attn_Wv, L0_attn_bv, L0_attn_Wlk, L0_attn_blk, L0_attn_Wlv, L0_attn_blv, L0_attn_qn_w, L0_attn_kn_w, L0_attn_Wo, L0_attn_bo), axis=-1)
    x = _layernorm(x + _L0_ffn_ref(x, L0_ffn_gate_w, L0_ffn_expert_bias, L0_ffn_w1, L0_ffn_w2, L0_ffn_w3, L0_ffn_sw1, L0_ffn_sw2, L0_ffn_sw3), axis=-1)
    return x

_drawn_inputs = setup_inputs


def setup_inputs(seed=0):
    import zlib

    import numpy as np

    out = dict(_drawn_inputs(seed))
    spreads = {'L0_attn_bq': (0.0, 0.372),
     'L0_attn_bk': (0.0, 0.375),
     'L0_attn_bv': (0.0, 0.1),
     'L0_attn_blk': (0.0, 0.8),
     'L0_attn_blv': (0.0, 0.1),
     'L0_attn_qn_w': (1.0, 0.6),
     'L0_attn_kn_w': (1.0, 0.6),
     'L0_attn_bo': (0.0, 0.1),
     'L0_ffn_expert_bias': (0.0, 0.416)}
    factors = {'L0_ffn_gate_w': 3.775, 'L0_ffn_w1': 2.803, 'L0_ffn_w2': 2.745, 'L0_ffn_w3': 2.745}
    for name, (base, spread) in spreads.items():
        noise = np.random.default_rng([zlib.crc32(name.encode()), seed]).standard_normal(out[name].shape)
        drawn = base * np.exp(spread * noise) if base else spread * noise
        out[name] = jnp.asarray(drawn.astype(out[name].dtype))
    for name, factor in factors.items():
        out[name] = (out[name] * factor).astype(out[name].dtype)
    return out
```

```python
from contextlib import ExitStack

import numpy as np

import concourse.bass as bass
from concourse import mybir

F32 = mybir.dt.float32
BF16 = mybir.dt.bfloat16
ALU = mybir.AluOpType
ACT = mybir.ActivationFunctionType
AX = mybir.AxisListType

P = 128
S = 2048
HID = 512
KC = HID // P
NH = 16
D = 128
NT = S // P
RATIO = 4
C = S // RATIO
CB = C // P
EPT = P // RATIO
TOPK = 8
ROT = D // 4
CH = 512
NCH = S // CH
TPC = CH // P
EPS = 1e-6
LN_EPS = 1e-5
NEG = -1e30
FLOOR = -1e29
TAKEN = 3e38
INTER = 352
HB = 3
E = 16
NSH = 2
EG = 4
G = E // EG
HEAD_COLS = 3 * KC * D + 2 + D


def hb_rows(b):
    return min(P, INTER - b * P)


def wait_for(eng, sem, count):
    if isinstance(count, int) and count <= 0:
        return
    eng.wait_ge(sem, count)


def build(nc, t):
    ctx = ExitStack()
    with ctx:
        def sb(name, shape, dt=F32, stack=ctx):
            return stack.enter_context(nc.sbuf_tensor(name, shape, dt))

        def sem(name, stack=ctx):
            return stack.enter_context(nc.semaphore(name))

        bank = [ctx.enter_context(nc.psum_tensor(f"bank{i}", [P, CH], F32)) for i in range(8)]

        xT = sb("xT", [P, KC, S])
        acc = sb("acc", [P, NT, HID])
        ident = sb("ident", [P, P])

        att = ExitStack()
        with att:
            attention(nc, t, bank, xT, acc, ident,
                      lambda n, s, d=F32: sb(n, s, d, att), lambda n: sem(n, att), sb)
        ffn = ExitStack()
        with ffn:
            feed_forward(nc, t, bank, xT, acc, ident,
                         lambda n, s, d=F32: sb(n, s, d, ffn), lambda n: sem(n, ffn))


def attention(nc, t, bank, xT, acc, ident, sb, sem, sb_for):
    cosk = sb("cosk", [P, S])
    cosq = sb("cosq", [P, S])
    sink = sb("sink", [2 * ROT, S])
    sinq = sb("sinq", [2 * ROT, S])
    norm_w = sb("norm_w", [P, 2])
    ckT = sb("ckT", [P, C])
    cv = sb("cv", [P, CB, D])
    half = sb("half", [P, CH])
    band = sb("band", [P, 2 * P])
    diag = sb("diag", [P, EPT], BF16)
    identb = sb("identb", [P, P], BF16)
    ones = sb("ones", [P, P])

    s1 = ExitStack()
    with s1:
        compress(nc, t, bank, xT, acc, ident, ones, half, band, diag, identb, cosk, cosq, sink, sinq,
                 norm_w, ckT, cv, lambda n, s, d=F32: sb_for(n, s, d, s1),
                 lambda n: s1.enter_context(nc.semaphore(n)))

    heads(nc, t, bank, xT, acc, ident, ones, half, band, diag, identb, cosk, cosq, sink, sinq, ckT, cv, sb, sem)


def compress(nc, t, bank, xT, acc, ident, ones, half, band, diag, identb, cosk, cosq, sink, sinq,
             norm_w, ckT, cv, sb, sem):
    wcmp = sb("wcmp", [P, KC])
    wcmp_rep = sb("wcmp_rep", [P, KC, P])
    bcmp = sb("bcmp", [P, 1])
    wk = sb("wk", [P, KC, D])
    wv = sb("wv", [P, KC, D])
    bk = sb("bk", [P, 1])
    bv = sb("bv", [P, D])
    bo = sb("bo", [P, HID])
    logit = sb("logit", [P, 2, CH])
    weight = sb("weight", [P, 2, CH])
    gmax = sb("gmax", [P, 2, P])
    gsum = sb("gsum", [P, 2, P])
    product = sb("product", [P, 2, CH])
    entT = sb("entT", [P, KC, C])
    square = sb("square", [P, C])
    ms = sb("ms", [P, C])
    rstd = sb("rstd", [P, C])
    turned = sb("turned", [2 * ROT, C])
    diag32 = sb("diag32", [P, EPT])

    x_in, c_in, r_in = sem("x_in"), sem("c_in"), sem("r_in")
    ready, logits, wlog, wmax, wexp, wnorm = (sem(n) for n in ("ready", "logits", "wlog", "wmax", "wexp", "wnorm"))
    ent, step, kproj, ksq, kssq, kms, krstd, vproj = (
        sem(n) for n in ("ent", "step", "kproj", "ksq", "kssq", "kms", "krstd", "vproj"))

    with nc.Block() as block:
        @block.sync
        def _(sp):
            for k in range(KC):
                sp.dma_start(xT[:, k, :], t["xT"][k * P:(k + 1) * P, :]).then_inc(x_in, 16)
            sp.dma_start(wk[:, :, :], t["Wk"].rearrange("(k p) d -> p k d", p=P)).then_inc(x_in, 16)
            sp.dma_start(wv[:, :, :], t["Wv"].rearrange("(k p) d -> p k d", p=P)).then_inc(x_in, 16)
            sp.dma_start(acc[:, :, :], t["x"].rearrange("(n p) d -> p n d", p=P)).then_inc(r_in, 16)
            sp.dma_start(bo[:, :], t["bo"].broadcast_to([P, HID])).then_inc(r_in, 16)

        @block.scalar
        def _(act):
            act.dma_start(wcmp[:, :], t["Wcmp"]).then_inc(c_in, 16)
            act.dma_start(bcmp[:, :], t["bcmp"].broadcast_to([P, 1])).then_inc(c_in, 16)
            act.dma_start(norm_w[:, :], t["norm_w"]).then_inc(c_in, 16)
            act.dma_start(bk[:, :], t["bk"]).then_inc(c_in, 16)
            act.dma_start(bv[:, :], t["bv"].broadcast_to([P, D])).then_inc(c_in, 16)
            act.dma_start(ident[:, :], t["ident"]).then_inc(c_in, 16)
            act.dma_start(band[:, :], t["band"]).then_inc(c_in, 16)
            act.dma_start(diag32[:, :], t["diag"]).then_inc(c_in, 16)
            act.dma_start(cosk[:, :], t["cos"]).then_inc(c_in, 16)
            act.dma_start(sink[:, :], t["sin"]).then_inc(c_in, 16)
            for c in range(NCH):
                act.wait_ge(wmax, 2 * (c + 1))
                act.activation(weight[:, c % 2, :], weight[:, c % 2, :], ACT.Exp).then_inc(wexp, 1)
            act.wait_ge(kproj, 1)
            act.activation(square[:, :], bank[4][:, :], ACT.Square, bias=bk[:, 0:1]).then_inc(ksq, 1)

        @block.tensor
        def _(pe):
            pe.wait_ge(x_in, 16 * (KC + 2))
            pe.wait_ge(ready, 1)
            for c in range(NCH):
                for k in range(KC):
                    mm = pe.matmul(bank[c][:, :], wcmp_rep[:, k, :], xT[:, k, c * CH:(c + 1) * CH],
                                   start=(k == 0), stop=(k == KC - 1))
                mm.then_inc(logits, 1)
            pe.wait_ge(ent, KC * NCH)
            for k in range(KC):
                mm = pe.matmul(bank[4][:, :], wk[:, k, :], entT[:, k, :], start=(k == 0), stop=(k == KC - 1))
            mm.then_inc(kproj, 1)
            for b in range(CB):
                for k in range(KC):
                    mm = pe.matmul(bank[5][:, b * D:(b + 1) * D], entT[:, k, b * P:(b + 1) * P], wv[:, k, :],
                                   start=(k == 0), stop=(k == KC - 1))
            mm.then_inc(vproj, 1)
            pe.wait_ge(ksq, 1)
            pe.matmul(bank[6][:, :], ones[:, :], square[:, :], start=True, stop=True).then_inc(kssq, 1)

        @block.gpsimd
        def _(pool):
            pool.memset(half[:, :], -0.5).then_inc(krstd, 1)
            pool.wait_ge(kms, 1)
            pool.wait_ge(krstd, 1)
            pool.tensor_tensor(rstd[:, :], ms[:, :], half[:, :], ALU.pow).then_inc(krstd, 1)

        @block.vector
        def _(dve):
            dve.wait_ge(c_in, 16 * 10)
            dve.memset(ones[:, :], 1.0)
            dve.tensor_copy(wcmp_rep[:, :, :], wcmp[:, :].unsqueeze(2).to_broadcast([P, KC, P])).then_inc(ready, 1)
            dve.tensor_copy(identb[:, :], ident[:, :])
            dve.tensor_copy(diag[:, :], diag32[:, :])
            for c in range(NCH):
                b = c % 2
                dve.wait_ge(logits, c + 1)
                dve.tensor_scalar(logit[:, b, :], bank[c][:, :], bcmp[:, 0:1], None, ALU.add).then_inc(wlog, 1)
                dve.wait_ge(wlog, c + 1)
                by4 = logit[:, b, :].rearrange("p (c r) -> p c r", r=RATIO)
                w4 = weight[:, b, :].rearrange("p (c r) -> p c r", r=RATIO)
                dve.tensor_reduce(gmax[:, b, :], by4, AX.X, ALU.max).then_inc(wmax, 1)
                dve.wait_ge(wmax, 2 * c + 1)
                dve.tensor_tensor(w4, by4, gmax[:, b, :].unsqueeze(2).to_broadcast([P, P, RATIO]),
                                  ALU.subtract).then_inc(wmax, 1)
                dve.wait_ge(wexp, c + 1)
                dve.tensor_reduce(gsum[:, b, :], w4, AX.X, ALU.add).then_inc(wnorm, 1)
                dve.wait_ge(wnorm, 3 * c + 1)
                dve.reciprocal(gsum[:, b, :], gsum[:, b, :]).then_inc(wnorm, 1)
                dve.wait_ge(wnorm, 3 * c + 2)
                dve.tensor_tensor(w4, w4, gsum[:, b, :].unsqueeze(2).to_broadcast([P, P, RATIO]),
                                  ALU.mult).then_inc(wnorm, 1)
                dve.wait_ge(wnorm, 3 * c + 3)
                for k in range(KC):
                    n = c * KC + k
                    dve.tensor_tensor(product[:, n % 2, :], xT[:, k, c * CH:(c + 1) * CH], weight[:, b, :],
                                      ALU.mult).then_inc(step, 1)
                    dve.wait_ge(step, n + 1)
                    dve.tensor_reduce(entT[:, k, c * P:(c + 1) * P],
                                      product[:, n % 2, :].rearrange("p (c r) -> p c r", r=RATIO),
                                      AX.X, ALU.add).then_inc(ent, 1)
            n0 = NCH * KC
            dve.tensor_scalar(cosq[:, :], cosk[:, :], norm_w[:, 1:2], None, ALU.mult).then_inc(step, 1)
            dve.tensor_scalar(sinq[:, :], sink[:, :], norm_w[0:2 * ROT, 1:2], None, ALU.mult).then_inc(step, 1)
            dve.wait_ge(step, n0 + 2)
            dve.tensor_scalar(cosk[:, :], cosk[:, :], norm_w[:, 0:1], None, ALU.mult).then_inc(step, 1)
            dve.tensor_scalar(sink[:, :], sink[:, :], norm_w[0:2 * ROT, 0:1], None, ALU.mult).then_inc(step, 1)
            dve.wait_ge(step, n0 + 4)
            dve.wait_ge(kproj, 1)
            dve.wait_ge(ksq, 1)
            ends = slice(RATIO - 1, S, RATIO)
            dve.scalar_tensor_tensor(turned[0:ROT, :], bank[4][ROT:2 * ROT, :], bk[ROT:2 * ROT, 0:1],
                                     sink[ROT:2 * ROT, ends], ALU.add, ALU.mult)
            dve.scalar_tensor_tensor(turned[ROT:2 * ROT, :], bank[4][0:ROT, :], bk[0:ROT, 0:1],
                                     sink[0:ROT, ends], ALU.add, ALU.mult).then_inc(step, 1)
            dve.scalar_tensor_tensor(ckT[:, :], bank[4][:, :], bk[:, 0:1], cosk[:, ends],
                                     ALU.add, ALU.mult).then_inc(step, 1)
            dve.wait_ge(step, n0 + 6)
            dve.tensor_tensor(ckT[0:2 * ROT, :], ckT[0:2 * ROT, :], turned[:, :], ALU.add).then_inc(step, 1)
            dve.wait_ge(kssq, 1)
            dve.tensor_scalar(ms[:, :], bank[6][:, :], 1.0 / D, EPS, ALU.mult, ALU.add).then_inc(kms, 1)
            dve.wait_ge(krstd, 2)
            dve.wait_ge(step, n0 + 7)
            dve.tensor_tensor(ckT[:, :], ckT[:, :], rstd[:, :], ALU.mult)
            dve.wait_ge(vproj, 1)
            dve.tensor_tensor(cv[:, :, :], bank[5][:, :].rearrange("p (b d) -> p b d", b=CB),
                              bv[:, :].unsqueeze(1).to_broadcast([P, CB, D]), ALU.add)
            dve.wait_ge(r_in, 32)
            dve.tensor_tensor(acc[:, :, :], acc[:, :, :], bo[:, :].unsqueeze(1).to_broadcast([P, NT, HID]), ALU.add)


def heads(nc, t, bank, xT, acc, ident, ones, half, band, diag, identb, cosk, cosq, sink, sinq, ckT, cv, sb, sem):
    wh = [sb(f"wh{i}", [P, HEAD_COLS]) for i in range(2)]
    wo = sb("wo", [P, 2, HID])
    kT = [sb(f"kT{i}", [P, S]) for i in range(2)]
    qT = [sb(f"qT{i}", [P, S]) for i in range(2)]
    v = [sb(f"v{i}", [P, NT, D]) for i in range(2)]
    turned = [sb(f"turned{i}", [2 * ROT, CH]) for i in range(2)]
    square = [sb(f"square{i}", [P, CH]) for i in range(2)]
    kms = sb("kms", [P, NT])
    qms = sb("qms", [P, NT])
    krstd = [sb(f"krstd{i}", [P, NT]) for i in range(2)]
    qfac = [sb(f"qfac{i}", [P, NT]) for i in range(2)]
    nfac = [sb(f"nfac{i}", [P, NT]) for i in range(2)]
    top = [sb(f"top{i}", [P, TOPK + 1]) for i in range(2)]
    nbias = [sb(f"nbias{i}", [P, 2]) for i in range(2)]
    total = [sb(f"total{i}", [P, 2]) for i in range(2)]
    share = [sb(f"share{i}", [P, 2]) for i in range(2)]
    taken = sb("taken", [P, C])
    prob = [sb(f"prob{i}", [P, C + 2 * P]) for i in range(2)]
    probT = sb("probT", [P, C + 2 * P])
    ctx_even = sb("ctx_even", [P, S])
    ctx_odd = sb("ctx_odd", [P, 2, P])

    b_score, b_local, b_turn_s, b_turn_l, b_unit, b_ctx, b_out = (
        bank[0], bank[1], bank[2], bank[3], (bank[4], bank[5]), bank[6], bank[7])
    SSQ = 2 * P

    w_in = [sem("w_in_even"), sem("w_in_odd")]
    wo_in = sem("wo_in")
    s_scores = sem("scores_done")
    s_ssq = sem("ssq_done")
    s_turn = sem("turn_done")
    s_unit = sem("unit_done")
    s_ctx = sem("ctx_done")
    s_out = sem("out_done")
    s_top = sem("top_done")
    s_bias = sem("bias_done")
    s_taken = sem("taken_done")
    s_total = sem("total_done")
    s_share = sem("share_done")
    s_uvec = sem("unit_vector")
    s_ms = sem("ms_done")
    s_nfac = sem("nfac_done")
    s_acc = sem("acc_done")
    s_exp = sem("exp_done")
    s_probT = sem("probT_done")
    s_square = sem("square_done")
    s_ctxc = sem("ctx_copied")
    s_prob = sem("prob_done")
    s_rope = sem("rope_done")
    s_rstd = sem("rstd_done")

    def weight(par, which, k):
        return wh[par][:, (which * KC + k) * D:(which * KC + k + 1) * D]

    def bias_col(par, which, rows=slice(0, P)):
        col = 3 * KC * D + which
        return wh[par][rows, col:col + 1]

    def blocks(tile):
        return tile // TPC + 1

    def width(tile):
        return EPT * (tile + 1)

    def local_cols(tile):
        return slice(0 if tile else P, 2 * P)

    def chunk(c):
        return slice(c * CH, (c + 1) * CH)

    def pe_unit(pe, h, par, u, of_kind):
        n = h * 16 + u
        dst = b_unit[u % 2]
        if u == 0:
            pe.wait_ge(w_in[par], of_kind * 16 + 16)
        wait_for(pe, s_uvec, n - 1)
        if u < 8:
            which, c = (1, u) if u < 4 else (0, u - 4)
            for k in range(KC):
                mm = pe.matmul(dst[:, :], weight(par, which, k), xT[:, k, chunk(c)],
                               start=(k == 0), stop=(k == KC - 1))
        elif u < 12:
            for i in range(TPC):
                tile = (u - 8) * TPC + i
                for k in range(KC):
                    mm = pe.matmul(dst[:, i * D:(i + 1) * D], xT[:, k, tile * P:(tile + 1) * P],
                                   weight(par, 2, k), start=(k == 0), stop=(k == KC - 1))
        else:
            pe.wait_ge(s_rstd, h * 2 + 1)
            for i in range(TPC):
                tile = (u - 12) * TPC + i
                mm = pe.transpose(dst[:, i * P:(i + 1) * P],
                                  krstd[par][:, tile:tile + 1].to_broadcast([P, P]), ident[:, :])
        mm.then_inc(s_unit, 1)

    def pe_ssq(pe, h, u):
        pe.wait_ge(s_square, h * 8 + (u + 1))
        for i in range(TPC):
            col = SSQ + TPC * u + i
            mm = pe.matmul(b_local[:, col:col + 1], square[u % 2][:, i * P:(i + 1) * P], ones[:, 0:1],
                           start=True, stop=True)
        if u % 4 == 3:
            mm.then_inc(s_ssq, 1)

    def pe_scores(pe, n, h, par, tile):
        if tile == 0:
            pe.wait_ge(s_uvec, n + 16)
            pe.wait_ge(s_rope, h * 8 + 8)
        w = width(tile)
        q = qT[par][:, tile * P:(tile + 1) * P]
        pe.matmul(b_score[:, 0:w], q, ckT[:, 0:w], start=True, stop=False)
        pe.matmul(b_score[:, w - EPT:w], identb[:, :], diag[:, :], start=False, stop=True)
        pe.matmul(b_local[:, local_cols(tile)], q, kT[par][:, max(tile - 1, 0) * P:(tile + 1) * P],
                  start=True, stop=True).then_inc(s_scores, 1)

    def pe_turn(pe, n, tile):
        pe.wait_ge(s_prob, n + 1)
        wait_for(pe, s_probT, n)
        pr = prob[tile % 2]
        for b in range(blocks(tile)):
            pe.transpose(b_turn_s[:, b * P:(b + 1) * P], pr[:, b * P:(b + 1) * P], ident[:, :])
        for b in ((0, 1) if tile else (1,)):
            mm = pe.transpose(b_turn_l[:, b * P:(b + 1) * P], pr[:, C + b * P:C + (b + 1) * P], ident[:, :])
        mm.then_inc(s_turn, 1)

    def pe_context(pe, n, par, tile):
        pe.wait_ge(s_probT, n + 1)
        wait_for(pe, s_ctxc, n)
        parts = [(cv[:, b, :], probT[:, b * P:(b + 1) * P]) for b in range(blocks(tile))]
        if tile:
            parts.append((v[par][:, tile - 1, :], probT[:, C:C + P]))
        parts.append((v[par][:, tile, :], probT[:, C + P:C + 2 * P]))
        for m, (val, pt) in enumerate(parts):
            mm = pe.matmul(b_ctx[:, 0:P], val, pt, start=(m == 0), stop=(m == len(parts) - 1))
        mm.then_inc(s_ctx, 1)

    def pe_out(pe, i, n, tile):
        if tile == 0:
            pe.wait_ge(wo_in, i * 16 + 16)
        pe.wait_ge(s_ctxc, n + 1)
        wait_for(pe, s_acc, i * 16 + tile)
        pe.matmul(b_out[:, :], ctx_even[:, tile * P:(tile + 1) * P], wo[:, 0, :], start=True, stop=False)
        pe.matmul(b_out[:, :], ctx_odd[:, tile % 2, :], wo[:, 1, :], start=False, stop=True).then_inc(s_out, 1)

    def pe_pair(pe, i, first=False, last=False):
        for j in range(2 * NT):
            n, par, tile = i * 32 + j, j // NT, j % NT
            nxt = i * 2 + (par + 1)
            units = not (last and par == 1)
            wait_for(pe, s_taken, n)
            wait_for(pe, s_exp, n)
            if units and 1 <= tile <= 8:
                pe_ssq(pe, nxt, tile - 1)
            pe_scores(pe, n, i * 2 + par, par, tile)
            if j or not first:
                pe_turn(pe, n - 1, (tile - 1) % NT)
            if units:
                pe_unit(pe, nxt, 1 - par, tile, i + par)
            if j >= NT + 2:
                pe_out(pe, i, n - 2, tile - 2)
            elif j < 2 and not first:
                pe_out(pe, i - 1, n - 2, NT - 2 + j)
            if j or not first:
                pe_context(pe, n - 1, par if tile else 1 - par, (tile - 1) % NT)

    def dve_ms(dve, h, which):
        dve.wait_ge(s_ssq, h * 2 + (which + 1))
        cols = slice(SSQ + NT * which, SSQ + NT * (which + 1))
        if which == 0:
            dve.tensor_scalar(kms[:, :], b_local[:, cols], 1.0 / D, EPS, ALU.mult, ALU.add).then_inc(s_ms, 1)
        else:
            dve.tensor_scalar(qms[:, :], b_local[:, cols], D * EPS, None, ALU.add).then_inc(s_ms, 1)

    def dve_unit(dve, h, par, u):
        n = h * 16 + u
        src = b_unit[u % 2]
        if u < 8:
            dve.wait_ge(s_square, h * 8 + (u + 1))
            which, c, cos, sin, dst = (1, u, cosk, sink, kT) if u < 4 else (0, u - 4, cosq, sinq, qT)
            if u >= 2:
                dve.wait_ge(s_rope, h * 8 + (u - 1))
            elif not (isinstance(h, int) and h == 0):
                dve.wait_ge(s_rope, h * 8 + (u - 1))
            lo, hi = slice(0, ROT), slice(ROT, 2 * ROT)
            dve.scalar_tensor_tensor(turned[u % 2][lo, :], src[hi, :], bias_col(par, which, hi),
                                     sin[hi, chunk(c)], ALU.add, ALU.mult)
            dve.scalar_tensor_tensor(turned[u % 2][hi, :], src[lo, :], bias_col(par, which, lo),
                                     sin[lo, chunk(c)], ALU.add, ALU.mult)
            dve.scalar_tensor_tensor(dst[par][:, chunk(c)], src[:, :], bias_col(par, which),
                                     cos[:, chunk(c)], ALU.add, ALU.mult).then_inc(s_uvec, 1)
        elif u < 12:
            dve.wait_ge(s_unit, n + 1)
            g = u - 8
            blv = wh[par][:, 3 * KC * D + 2:HEAD_COLS]
            dve.tensor_tensor(v[par][:, g * TPC:(g + 1) * TPC, :], src[:, :].rearrange("p (a d) -> p a d", a=TPC),
                              blv.unsqueeze(1).to_broadcast([P, TPC, D]), ALU.add).then_inc(s_uvec, 1)
        else:
            dve.wait_ge(s_unit, n + 1)
            dve.wait_ge(s_rope, h * 8 + 4)
            keys = kT[par][:, chunk(u - 12)]
            dve.tensor_tensor(keys, keys, src[:, :], ALU.mult).then_inc(s_uvec, 1)

    def dve_nfac(dve, h, par):
        dve.wait_ge(s_rstd, h * 2 + 2)
        dve.tensor_scalar(nfac[par][:, :], qfac[par][:, :], -1.0, None, ALU.mult).then_inc(s_nfac, 1)

    def dve_step(dve, i, n, par, tile, ms_of):
        b, w, lc = tile % 2, width(tile), local_cols(tile)
        dve.wait_ge(s_scores, n + 1)
        wait_for(dve, s_turn, n - 1)
        dve.memset(prob[b][:, w:blocks(tile) * P] if w < blocks(tile) * P else total[b][:, :], 0.0)
        if ms_of is not None:
            dve_ms(dve, ms_of, tile // 8)
        pl = prob[b][:, C:C + 2 * P]
        dve.tensor_tensor_reduce(pl[:, lc], b_local[:, lc], band[:, lc], 1.0, NEG, ALU.add, ALU.max,
                                 top[b][:, TOPK:TOPK + 1]).then_inc(s_top, 1)
        dve.max(top[b][:, 0:TOPK], b_score[:, 0:w]).then_inc(s_top, 1)
        dve.wait_ge(s_top, n * 2 + 2)
        if tile == 0:
            dve.wait_ge(s_nfac, i * 2 + (par + 1))
        dve.tensor_scalar(nbias[b][:, :], top[b][:, 0:TOPK + 1:TOPK], FLOOR, nfac[par][:, tile:tile + 1],
                          ALU.max, ALU.mult).then_inc(s_bias, 1)
        dve.match_replace(taken[:, 0:w], top[b][:, 0:TOPK], b_score[:, 0:w], TAKEN).then_inc(s_taken, 1)
        dve.wait_ge(s_exp, n + 1)
        dve.wait_ge(s_taken, n + 1)
        dve.scalar_tensor_tensor(prob[b][:, 0:w], taken[:, 0:w], TAKEN / 2, prob[b][:, 0:w], ALU.is_ge, ALU.mult,
                                 accum_out=total[b][:, 0:1]).then_inc(s_total, 1)
        dve.wait_ge(s_total, n * 2 + 1)
        dve.tensor_scalar(total[b][:, :], total[b][:, :], 1e-9, 2.0, ALU.max, ALU.mult).then_inc(s_total, 1)
        dve.wait_ge(s_total, n * 2 + 2)
        dve.reciprocal(share[b][:, :], total[b][:, :]).then_inc(s_share, 1)

    def dve_acc(dve, i, tile):
        dve.wait_ge(s_out, i * 16 + (tile + 1))
        dve.tensor_tensor(acc[:, tile, :], acc[:, tile, :], b_out[:, :], ALU.add).then_inc(s_acc, 1)

    def dve_pair(dve, i, first=False, last=False):
        for j in range(2 * NT):
            n, par, tile = i * 32 + j, j // NT, j % NT
            nxt = i * 2 + (par + 1)
            units = not (last and par == 1)
            dve_step(dve, i, n, par, tile, nxt if units and tile in (4, 8) else None)
            if units:
                dve_unit(dve, nxt, 1 - par, tile)
                if tile == 11:
                    dve_nfac(dve, nxt, 1 - par)
            if j >= NT + 2:
                dve_acc(dve, i, tile - 2)
            elif j < 2 and not first:
                dve_acc(dve, i - 1, NT - 2 + j)

    def act_square(act, h, par, u):
        act.wait_ge(s_unit, h * 16 + (u + 1))
        act.activation(square[u % 2][:, :], b_unit[u % 2][:, :], ACT.Square,
                       bias=bias_col(par, 1 if u < 4 else 0)).then_inc(s_square, 1)

    def act_probT(act, n, tile):
        act.wait_ge(s_turn, n + 1)
        w = blocks(tile) * P
        act.copy(probT[:, 0:w], b_turn_s[:, 0:w])
        lc = local_cols(tile)
        act.copy(probT[:, C:C + 2 * P][:, lc], b_turn_l[:, lc]).then_inc(s_probT, 1)

    def act_exp(act, n, par, tile):
        b, w = tile % 2, width(tile)
        act.wait_ge(s_bias, n + 1)
        pl = prob[b][:, C:C + 2 * P][:, local_cols(tile)]
        act.activation(pl, pl, ACT.Exp, bias=nbias[b][:, 1:2], scale=qfac[par][:, tile:tile + 1],
                       accum_out=total[b][:, 1:2])
        act.wait_ge(s_taken, n + 1)
        act.activation(prob[b][:, 0:w], b_score[:, 0:w], ACT.Exp, bias=nbias[b][:, 0:1],
                       scale=qfac[par][:, tile:tile + 1]).then_inc(s_exp, 1)

    def act_ctx(act, n, par, tile):
        act.wait_ge(s_ctx, n + 1)
        dst = ctx_odd[:, tile % 2, :] if par else ctx_even[:, tile * P:(tile + 1) * P]
        act.copy(dst, b_ctx[:, 0:P]).then_inc(s_ctxc, 1)

    def act_pair(act, i, first=False, last=False):
        for j in range(2 * NT):
            n, par, tile = i * 32 + j, j // NT, j % NT
            if j or not first:
                act_probT(act, n - 1, (tile - 1) % NT)
            act_exp(act, n, par, tile)
            if tile < 8 and not (last and par == 1):
                act_square(act, i * 2 + (par + 1), 1 - par, tile)
            if j or not first:
                act_ctx(act, n - 1, par if tile else 1 - par, (tile - 1) % NT)

    def pool_rope(pool, h, par, u):
        pool.wait_ge(s_uvec, h * 16 + (u + 1))
        dst = kT[par] if u < 4 else qT[par]
        part = dst[0:2 * ROT, chunk(u % 4)]
        pool.tensor_tensor(part, part, turned[u % 2][:, :], ALU.add).then_inc(s_rope, 1)

    def pool_rstd(pool, h, par, which):
        pool.wait_ge(s_ms, h * 2 + (which + 1))
        src, dst = (kms, krstd) if which == 0 else (qms, qfac)
        pool.tensor_tensor(dst[par][:, :], src[:, :], half[:, 0:NT], ALU.pow).then_inc(s_rstd, 1)

    def pool_prob(pool, n, tile):
        b, w = tile % 2, width(tile)
        pool.wait_ge(s_share, n + 1)
        pl = prob[b][:, C:C + 2 * P][:, local_cols(tile)]
        pool.tensor_tensor(pl, pl, share[b][:, 1:2].to_broadcast(list(pl.shape)), ALU.mult)
        pool.tensor_scalar(prob[b][:, 0:w], prob[b][:, 0:w], share[b][:, 0:1], 1.0, ALU.mult,
                           ALU.mult).then_inc(s_prob, 1)

    def pool_pair(pool, i, first=False, last=False):
        for j in range(2 * NT):
            n, par, tile = i * 32 + j, j // NT, j % NT
            nxt = i * 2 + (par + 1)
            units = not (last and par == 1)
            if units and tile in (4, 8):
                pool_rstd(pool, nxt, 1 - par, tile // 8)
            pool_prob(pool, n, tile)
            if units and tile < 8:
                pool_rope(pool, nxt, 1 - par, tile)

    NP = NH // 2
    with nc.Block() as block:
        @block.sync
        def _(sp):
            def load_head(h, par):
                wait_for(sp, s_uvec, h * 16 - 16)
                sp.dma_start(wh[par][:, :], t["wh"][h, :, :] if isinstance(h, int)
                             else t["wh"][bass.ds(h, 1), :, :].rearrange("o p c -> (o p) c")).then_inc(w_in[par], 16)

            def load_wo(i):
                wait_for(sp, s_out, i * 16)
                rows = t["Wo"][0:2 * D, :] if isinstance(i, int) and i == 0 else t["Wo"][bass.ds(i * (2 * D), 2 * D), :]
                sp.dma_start(wo[:, :, :], rows.rearrange("(a d) n -> d a n", a=2)).then_inc(wo_in, 16)

            load_head(0, 0)
            load_head(1, 1)
            load_wo(0)
            with sp.Fori(1, NP) as i:
                load_head(i * 2, 0)
                load_head(i * 2 + 1, 1)
                load_wo(i)

        @block.tensor
        def _(pe):
            for u in range(NT):
                pe_unit(pe, 0, 0, u, 0)
                if 1 <= u <= 8:
                    if u == 5:
                        pe.wait_ge(s_ms, 1)
                    pe_ssq(pe, 0, u - 1)
            pe.wait_ge(s_ms, 2)
            pe_pair(pe, 0, first=True)
            with pe.Fori(1, NP - 1) as i:
                pe_pair(pe, i)
            pe_pair(pe, NP - 1, last=True)
            n = NH * NT
            pe_turn(pe, n - 1, NT - 1)
            pe_out(pe, NP - 1, n - 2, NT - 2)
            pe_context(pe, n - 1, 1, NT - 1)
            pe_out(pe, NP - 1, n - 1, NT - 1)

        @block.vector
        def _(dve):
            for u in range(NT):
                dve_unit(dve, 0, 0, u)
                if u in (4, 8):
                    dve_ms(dve, 0, u // 8)
            dve_nfac(dve, 0, 0)
            dve_pair(dve, 0, first=True)
            with dve.Fori(1, NP - 1) as i:
                dve_pair(dve, i)
            dve_pair(dve, NP - 1, last=True)
            dve_acc(dve, NP - 1, NT - 2)
            dve_acc(dve, NP - 1, NT - 1)

        @block.scalar
        def _(act):
            for u in range(8):
                act_square(act, 0, 0, u)
            act_pair(act, 0, first=True)
            with act.Fori(1, NP - 1) as i:
                act_pair(act, i)
            act_pair(act, NP - 1, last=True)
            n = NH * NT
            act_probT(act, n - 1, NT - 1)
            act_ctx(act, n - 1, 1, NT - 1)

        @block.gpsimd
        def _(pool):
            for u in range(8):
                pool_rope(pool, 0, 0, u)
                if u == 4:
                    pool_rstd(pool, 0, 0, 0)
            pool_rstd(pool, 0, 0, 1)
            pool_pair(pool, 0, first=True)
            with pool.Fori(1, NP - 1) as i:
                pool_pair(pool, i)
            pool_pair(pool, NP - 1, last=True)


def feed_forward(nc, t, bank, x1T, acc, ident, sb, sem):
    NE = E + NSH
    stats = sb("stats", [P, 2, 6])
    mv = sb("mv", [P, NT, 2])
    rstd = sb("rstd2", [P, NT])
    neghalf = sb("neghalf", [P, NT])
    gateT = sb("gateT", [P, KC, E])
    ebias = sb("ebias", [P, E])
    sig = sb("sig", [P, NT, E])
    choice = sb("choice", [P, NT, E])
    gbest = sb("gbest", [P, NT, G])
    cmp = sb("cmp", [P, NT, E])
    grank = sb("grank", [P, NT, G])
    rank = sb("rank", [P, NT, E])
    cw = sb("cw", [P, NT, NE])
    csum = sb("csum", [P, NT])

    def norm(block_name, out_dram=None):
        st = ExitStack()
        with st:
            s_st, s_mv, s_eps, s_pow, s_half, s_done, s_store = (
                st.enter_context(nc.semaphore(f"{block_name}_{x}"))
                for x in ("stats", "mv", "eps", "pow", "half", "done", "store"))
            with nc.Block() as block:
                @block.vector
                def _(dve):
                    for n in range(NT):
                        dve.bn_stats(stats[:, n % 2, :], acc[:, n, :]).then_inc(s_st, 1)
                        dve.wait_ge(s_st, n + 1)
                        dve.bn_aggr(mv[:, n, :], stats[:, n % 2, :]).then_inc(s_mv, 1)
                    dve.wait_ge(s_mv, NT)
                    dve.tensor_scalar(rstd[:, :], mv[:, :, 1], LN_EPS, None, ALU.add).then_inc(s_eps, 1)
                    dve.wait_ge(s_pow, 1)
                    for n in range(NT):
                        dve.tensor_scalar(acc[:, n, :], acc[:, n, :], mv[:, n, 0:1], rstd[:, n:n + 1],
                                          ALU.subtract, ALU.mult).then_inc(s_done, 1)

                @block.gpsimd
                def _(pool):
                    pool.memset(neghalf[:, :], -0.5).then_inc(s_half, 1)
                    pool.wait_ge(s_half, 1)
                    pool.wait_ge(s_eps, 1)
                    pool.tensor_tensor(rstd[:, :], rstd[:, :], neghalf[:, :], ALU.pow).then_inc(s_pow, 1)

                if out_dram is not None:
                    @block.sync
                    def _(sp):
                        for n in range(NT):
                            sp.wait_ge(s_done, n + 1)
                            sp.dma_start(out_dram[n * P:(n + 1) * P, :], acc[:, n, :]).then_inc(s_store, 16)
                        sp.wait_ge(s_store, 16 * NT)

    norm("ln1")

    r = ExitStack()
    with r:
        g_in, turned, copied, logits, sigs, v = (r.enter_context(nc.semaphore(x)) for x in (
            "g_in", "x1_turned", "x1_copied", "gate_done", "sig_done", "router"))
        with nc.Block() as block:
            @block.sync
            def _(sp):
                sp.dma_start(gateT[:, :, :], t["gateT"].rearrange("(k p) e -> p k e", p=P)).then_inc(g_in, 16)
                sp.dma_start(ebias[:, :], t["ebias"].broadcast_to([P, E])).then_inc(g_in, 16)

            @block.tensor
            def _(pe):
                for n in range(NT):
                    if n >= 4:
                        pe.wait_ge(copied, n - 3)
                    for k in range(KC):
                        mm = pe.transpose(bank[n % 4][:, k * P:(k + 1) * P], acc[:, n, k * P:(k + 1) * P], ident[:, :])
                    mm.then_inc(turned, 1)
                pe.wait_ge(copied, NT)
                pe.wait_ge(g_in, 32)
                for n in range(NT):
                    for k in range(KC):
                        mm = pe.matmul(bank[4][:, n * E:(n + 1) * E], x1T[:, k, n * P:(n + 1) * P], gateT[:, k, :],
                                       start=(k == 0), stop=(k == KC - 1))
                mm.then_inc(logits, 1)

            @block.scalar
            def _(act):
                for n in range(NT):
                    act.wait_ge(turned, n + 1)
                    act.copy(x1T[:, :, n * P:(n + 1) * P],
                             bank[n % 4][:, :].rearrange("p (k t) -> p k t", k=KC)).then_inc(copied, 1)
                act.wait_ge(logits, 1)
                act.activation(sig[:, :, :], bank[4][:, 0:NT * E].rearrange("p (n e) -> p n e", e=E),
                               ACT.Sigmoid).then_inc(sigs, 1)

            @block.vector
            def _(dve):
                count = [0]

                def then(ins):
                    count[0] += 1
                    ins.then_inc(v, 1)
                    dve.wait_ge(v, count[0])

                dve.wait_ge(sigs, 1)
                dve.wait_ge(g_in, 32)
                then(dve.tensor_tensor(choice[:, :, :], sig[:, :, :], ebias[:, :].unsqueeze(1).to_broadcast([P, NT, E]),
                                       ALU.add))
                then(dve.tensor_reduce(gbest[:, :, :], choice[:, :, :].rearrange("p n (g e) -> p n g e", e=EG),
                                       AX.X, ALU.max))
                then(dve.memset(grank[:, :, :], 0.0))
                for g in range(G):
                    for o in range(G):
                        if o != g:
                            then(dve.tensor_tensor(cmp[:, :, 0:1], gbest[:, :, o:o + 1], gbest[:, :, g:g + 1],
                                                   ALU.is_ge if o < g else ALU.is_gt))
                            then(dve.tensor_tensor(grank[:, :, g:g + 1], grank[:, :, g:g + 1], cmp[:, :, 0:1], ALU.add))
                then(dve.tensor_scalar(grank[:, :, :], grank[:, :, :], 2.0, None, ALU.is_lt))
                gm = grank[:, :, :].unsqueeze(3).to_broadcast([P, NT, G, EG])
                c4 = choice[:, :, :].rearrange("p n (g e) -> p n g e", e=EG)
                then(dve.tensor_tensor(c4, c4, gm, ALU.mult))
                then(dve.tensor_scalar(grank[:, :, :], grank[:, :, :], -1.0, -NEG, ALU.add, ALU.mult))
                then(dve.tensor_tensor(c4, c4, gm, ALU.add))
                then(dve.memset(rank[:, :, :], 0.0))
                for o in range(E):
                    other = choice[:, :, o:o + 1]
                    if o + 1 < E:
                        m = E - o - 1
                        then(dve.tensor_tensor(cmp[:, :, o + 1:E], other.to_broadcast([P, NT, m]),
                                               choice[:, :, o + 1:E], ALU.is_ge))
                    if o:
                        then(dve.tensor_tensor(cmp[:, :, 0:o], other.to_broadcast([P, NT, o]),
                                               choice[:, :, 0:o], ALU.is_gt))
                    if o:
                        then(dve.tensor_tensor(rank[:, :, 0:o], rank[:, :, 0:o], cmp[:, :, 0:o], ALU.add))
                    if o + 1 < E:
                        then(dve.tensor_tensor(rank[:, :, o + 1:E], rank[:, :, o + 1:E], cmp[:, :, o + 1:E], ALU.add))
                then(dve.tensor_scalar(rank[:, :, :], rank[:, :, :], 4.0, None, ALU.is_lt))
                then(dve.tensor_tensor(sig[:, :, :], sig[:, :, :], rank[:, :, :], ALU.mult))
                then(dve.tensor_reduce(csum[:, :], sig[:, :, :], AX.X, ALU.add))
                then(dve.reciprocal(csum[:, :], csum[:, :]))
                then(dve.memset(cw[:, :, :], 1.0))
                then(dve.tensor_tensor(cw[:, :, 0:E], sig[:, :, :], csum[:, :].unsqueeze(2).to_broadcast([P, NT, E]),
                                       ALU.mult))

    e_ = ExitStack()
    with e_:
        w13 = [sb(f"w13_{i}", [P, 2, KC, INTER]) for i in range(2)]
        w2 = [sb(f"w2_{i}", [P, HB, HID]) for i in range(2)]
        gate = [sb(f"gate{i}", [P, CH]) for i in range(2)]
        hT = [sb(f"hT{i}", [P, HB, CH]) for i in range(2)]
        cwt = [sb(f"cwt{i}", [P, NT]) for i in range(2)]
        w_in = [e_.enter_context(nc.semaphore(x)) for x in ("ew_in_even", "ew_in_odd")]
        s_up, s_silu, s_h, s_y, s_sum, s_cw = (e_.enter_context(nc.semaphore(x)) for x in (
            "up_done", "silu_done", "h_done", "y_done", "sum_done", "cw_done"))
        UPS, DOWNS = NCH * HB, NT

        def pe_up(pe, e, par, c, b):
            q = c * HB + b
            n = e * UPS + q
            wait_for(pe, s_h, n - 1)
            rows = hb_rows(b)
            for w in range(2):
                for k in range(KC):
                    mm = pe.matmul(bank[2 * (q % 2) + w][0:rows, :], w13[par][:, w, k, b * P:b * P + rows],
                                   x1T[:, k, c * CH:(c + 1) * CH], start=(k == 0), stop=(k == KC - 1))
            mm.then_inc(s_up, 1)

        def pe_down(pe, e, par, c):
            pe.wait_ge(s_h, e * UPS + (c + 1) * HB)
            for i in range(TPC):
                m = c * TPC + i
                n = e * DOWNS + m
                wait_for(pe, s_sum, n - 3)
                for b in range(HB):
                    rows = hb_rows(b)
                    mm = pe.matmul(bank[4 + m % 4][:, :], hT[c % 2][0:rows, b, i * P:(i + 1) * P],
                                   w2[par][0:rows, b, :], start=(b == 0), stop=(b == HB - 1))
                mm.then_inc(s_y, 1)

        with nc.Block() as block:
            @block.sync
            def _(sp):
                def load(e, par):
                    wait_for(sp, s_y, e * DOWNS - DOWNS)
                    if isinstance(e, int):
                        a, b, c = t["w13"][e, :, :, :], t["w2"][e, 0:2 * P, :], t["w2"][e, 2 * P:INTER, :]
                    else:
                        a = t["w13"][bass.ds(e, 1), :, :, :].rearrange("o w k n -> (o w) k n")
                        b = t["w2"][bass.ds(e, 1), 0:2 * P, :].rearrange("o k n -> (o k) n")
                        c = t["w2"][bass.ds(e, 1), 2 * P:INTER, :].rearrange("o k n -> (o k) n")
                    for w in range(2):
                        sp.dma_start(w13[par][:, w, :, :], a[w, :, :].rearrange("(k p) n -> p k n", p=P)).then_inc(w_in[par], 16)
                    sp.dma_start(w2[par][:, 0:2, :], b.rearrange("(b p) n -> p b n", p=P)).then_inc(w_in[par], 16)
                    sp.dma_start(w2[par][0:INTER - 2 * P, 2, :], c).then_inc(w_in[par], 16)

                load(0, 0)
                load(1, 1)
                with sp.Fori(1, NE // 2) as i:
                    load(i * 2, 0)
                    load(i * 2 + 1, 1)

            @block.tensor
            def _(pe):
                def pair(i):
                    for par in range(2):
                        e = i * 2 + par
                        pe.wait_ge(w_in[par], i * 64 + 64)
                        for c in range(NCH):
                            for b in range(HB):
                                pe_up(pe, e, par, c, b)
                            pe_down(pe, e, par, c)

                pair(0)
                with pe.Fori(1, NE // 2) as i:
                    pair(i)

            @block.scalar
            def _(act):
                def pair(i):
                    for par in range(2):
                        e = i * 2 + par
                        for q in range(UPS):
                            rows = hb_rows(q % HB)
                            act.wait_ge(s_up, e * UPS + (q + 1))
                            act.activation(gate[q % 2][0:rows, :], bank[2 * (q % 2)][0:rows, :],
                                           ACT.Silu).then_inc(s_silu, 1)
                pair(0)
                with act.Fori(1, NE // 2) as i:
                    pair(i)

            @block.vector
            def _(dve):
                def pair(i):
                    for par in range(2):
                        e = i * 2 + par
                        dve.tensor_copy(cwt[par][:, :], cw[:, :, par:par + 1] if isinstance(i, int)
                                        else cw[:, :, bass.ds(e, 1)]).then_inc(s_cw, 1)
                        for c in range(NCH):
                            for b in range(HB):
                                q = c * HB + b
                                rows = hb_rows(b)
                                if b == 0:
                                    wait_for(dve, s_y, e * DOWNS + (c - 1) * TPC)
                                dve.wait_ge(s_silu, e * UPS + (q + 1))
                                dve.tensor_tensor(hT[c % 2][0:rows, b, :], gate[q % 2][0:rows, :],
                                                  bank[2 * (q % 2) + 1][0:rows, :], ALU.mult).then_inc(s_h, 1)
                            if c == 0:
                                dve.wait_ge(s_cw, e + 1)
                            for k in range(TPC):
                                m = c * TPC + k
                                dve.wait_ge(s_y, e * DOWNS + (m + 1))
                                dve.scalar_tensor_tensor(acc[:, m, :], bank[4 + m % 4][:, :], cwt[par][:, m:m + 1],
                                                         acc[:, m, :], ALU.mult, ALU.add).then_inc(s_sum, 1)

                pair(0)
                with dve.Fori(1, NE // 2) as i:
                    pair(i)

    norm("ln2", t["out"])


def kernel(**inputs):
    import concourse.bacc as bacc
    from concourse.bass_utils import run_bass_kernel_spmd as run

    a = {n.replace("L0_attn_", "").replace("L0_ffn_", "f_"): np.ascontiguousarray(x) for n, x in inputs.items()}
    x = a["hidden_states"][0]
    def by_head(w):
        return w.reshape(KC, P, NH, D).transpose(2, 1, 0, 3).reshape(NH, P, KC * D)
    wh = np.concatenate([
        by_head(a["Wq"]), by_head(a["Wlk"]), by_head(a["Wlv"]),
        a["bq"].reshape(NH, D, 1), a["blk"].reshape(NH, D, 1),
        np.broadcast_to(a["blv"].reshape(NH, 1, D), (NH, P, D)),
    ], axis=2)
    sh = NSH * INTER
    w1 = np.concatenate([a["f_w1"], a["f_sw1"].reshape(HID, NSH, INTER).transpose(1, 0, 2)])
    w3 = np.concatenate([a["f_w3"], a["f_sw3"].reshape(HID, NSH, INTER).transpose(1, 0, 2)])
    w2 = np.concatenate([a["f_w2"], a["f_sw2"].reshape(NSH, INTER, HID)])
    inv = np.float32(1.0) / np.float32(10000.0) ** (np.arange(ROT, dtype=np.float32) * np.float32(2.0 / (2 * ROT)))
    ang = np.arange(S, dtype=np.float32)[None, :] * inv.astype(np.float32)[:, None]
    cos, sin = np.cos(ang).astype(np.float32), np.sin(ang).astype(np.float32)
    cos_t = np.concatenate([cos, cos, np.ones((P - 2 * ROT, S), np.float32)])
    sin_t = np.concatenate([sin, -sin])
    q, k = np.arange(P)[:, None], np.arange(2 * P)[None, :]
    rel = q + P - k
    band = np.where((rel >= 0) & (rel <= P), 0.0, NEG).astype(np.float32)
    diag = np.where(np.arange(EPT)[None, :] * RATIO + RATIO - 1 <= q, 0.0, NEG).astype(np.float32)
    arrays = {
        "x": x, "xT": x.T, "Wcmp": a["Wcmp"].reshape(KC, P).T, "bcmp": a["bcmp"].reshape(1, 1), "Wk": a["Wk"], "Wv": a["Wv"],
        "norm_w": np.stack([a["kn_w"], a["qn_w"]], axis=1), "bk": a["bk"].reshape(D, 1), "bv": a["bv"].reshape(1, D),
        "bo": a["bo"].reshape(1, HID), "wh": wh, "Wo": a["Wo"], "gateT": a["f_gate_w"].T,
        "ebias": a["f_expert_bias"].reshape(1, E), "w13": np.stack([w1, w3], axis=1), "w2": w2,
        "ident": np.eye(P, dtype=np.float32), "cos": cos_t, "sin": sin_t, "band": band, "diag": diag,
    }
    arrays = {n: np.ascontiguousarray(v) for n, v in arrays.items()}
    nc = bacc.Bacc("TRN2", target_bir_lowering=False, num_devices=1)
    t = {n: nc.dram_tensor(f"in_{n}", v.shape, F32, kind="ExternalInput").ap() for n, v in arrays.items()}
    out = nc.dram_tensor("out", [1, S, HID], F32, kind="ExternalOutput").ap()
    t["out"] = out[0, :, :]
    build(nc, t)
    r = run(nc, [{f"in_{n}": v for n, v in arrays.items()}], core_ids=[0])
    return r.results[0]["out"]
```

```python
from contextlib import ExitStack

import numpy as np

import concourse.bass as bass
from concourse import mybir

F32 = mybir.dt.float32
F32R = mybir.dt.float32r
BF16 = mybir.dt.bfloat16
I32 = mybir.dt.int32
U32 = mybir.dt.uint32
ALU = mybir.AluOpType
ACT = mybir.ActivationFunctionType
AX = mybir.AxisListType

P = 128
S = 2048
HID = 512
KC = HID // P
NH = 16
D = 128
NT = S // P
RATIO = 4
C = S // RATIO
CB = C // P
EPT = P // RATIO
TOPK = 8
ROT = D // 4
CH = 512
NCH = S // CH
TPC = CH // P
EPS = 1e-6
LN_EPS = 1e-5
NEG = -1e30
FLOOR = -1e29
TAKEN = 3e38
INTER = 352
HB = 3
E = 16
NSH = 2
EG = 4
G = E // EG
PICK = 4
PICK_G = 2
MAXT = PICK * NT + E + 2
WCOLS = 2 * KC * INTER + HB * HID
HEAD_COLS = 3 * KC * D + 2 + D


def hb_rows(b):
    return min(P, INTER - b * P)


def wait_for(eng, sem, count):
    if isinstance(count, int) and count <= 0:
        return
    eng.wait_ge(sem, count)


def build(nc, t):
    ctx = ExitStack()
    with ctx:
        def sb(name, shape, dt=F32, stack=ctx):
            return stack.enter_context(nc.sbuf_tensor(name, shape, dt))

        def sem(name, stack=ctx):
            return stack.enter_context(nc.semaphore(name))

        bank = [ctx.enter_context(nc.psum_tensor(f"bank{i}", [P, CH], F32)) for i in range(8)]

        acc = sb("acc", [P, NT, HID])
        ident = sb("ident", [P, P])

        xs = nc.dram_tensor("slots_in", [MAXT * P, HID], F32, kind="Internal").ap()
        ys = nc.dram_tensor("slots_out", [MAXT * P, HID], F32, kind="Internal").ap()
        zero_sem = sem("slots_zeroed")

        att = ExitStack()
        with att:
            xT = sb("xT", [P, KC, S], F32, att)
            attention(nc, t, bank, xT, acc, ident, (xs, ys), zero_sem,
                      lambda n, s, d=F32: sb(n, s, d, att), lambda n: sem(n, att), sb)
        feed_forward(nc, t, bank, acc, ident, xs, ys, [(zero_sem, 16 * (MAXT // 2 + (MAXT - PICK * NT) // 2))],
                     sb, sem)


def attention(nc, t, bank, xT, acc, ident, slots_dram, zero_sem, sb, sem, sb_for):
    cosk = sb("cosk", [P, S])
    cosq = sb("cosq", [P, S])
    sink = sb("sink", [2 * ROT, S])
    sinq = sb("sinq", [2 * ROT, S])
    norm_w = sb("norm_w", [P, 2])
    ckT = sb("ckT", [P, C])
    cv = sb("cv", [P, CB, D])
    half = sb("half", [P, CH])
    band = sb("band", [P, 2 * P])
    diag = sb("diag", [P, EPT], BF16)
    identb = sb("identb", [P, P], BF16)
    ones = sb("ones", [P, P])

    s1 = ExitStack()
    with s1:
        compress(nc, t, bank, xT, acc, ident, ones, half, band, diag, identb, cosk, cosq, sink, sinq,
                 norm_w, ckT, cv, lambda n, s, d=F32: sb_for(n, s, d, s1),
                 lambda n: s1.enter_context(nc.semaphore(n)))

    heads(nc, t, bank, xT, acc, ident, slots_dram, zero_sem, ones, half, band, diag, identb, cosk, cosq, sink, sinq, ckT, cv,
          sb, sem)


def compress(nc, t, bank, xT, acc, ident, ones, half, band, diag, identb, cosk, cosq, sink, sinq,
             norm_w, ckT, cv, sb, sem):
    wcmp = sb("wcmp", [P, KC])
    wcmp_rep = sb("wcmp_rep", [P, KC, P])
    bcmp = sb("bcmp", [P, 1])
    wk = sb("wk", [P, KC, D])
    wv = sb("wv", [P, KC, D])
    bk = sb("bk", [P, 1])
    bv = sb("bv", [P, D])
    bo = sb("bo", [P, HID])
    logit = sb("logit", [P, 2, CH])
    weight = sb("weight", [P, 2, CH])
    gmax = sb("gmax", [P, 2, P])
    gsum = sb("gsum", [P, 2, P])
    product = sb("product", [P, 2, CH])
    entT = sb("entT", [P, KC, C])
    square = sb("square", [P, C])
    ms = sb("ms", [P, C])
    rstd = sb("rstd", [P, C])
    turned = sb("turned", [2 * ROT, C])
    diag32 = sb("diag32", [P, EPT])

    x_in, c_in, r_in = sem("x_in"), sem("c_in"), sem("r_in")
    ready, logits, wlog, wmax, wexp, wnorm = (sem(n) for n in ("ready", "logits", "wlog", "wmax", "wexp", "wnorm"))
    ent, step, kproj, ksq, kssq, kms, krstd, vproj = (
        sem(n) for n in ("ent", "step", "kproj", "ksq", "kssq", "kms", "krstd", "vproj"))

    with nc.Block() as block:
        @block.sync
        def _(sp):
            for k in range(KC):
                sp.dma_start(xT[:, k, :], t["xT"][k * P:(k + 1) * P, :]).then_inc(x_in, 16)
            sp.dma_start(wk[:, :, :], t["Wk"].rearrange("(k p) d -> p k d", p=P)).then_inc(x_in, 16)
            sp.dma_start(wv[:, :, :], t["Wv"].rearrange("(k p) d -> p k d", p=P)).then_inc(x_in, 16)
            sp.dma_start(acc[:, :, :], t["x"].rearrange("(n p) d -> p n d", p=P)).then_inc(r_in, 16)
            sp.dma_start(bo[:, :], t["bo"].broadcast_to([P, HID])).then_inc(r_in, 16)

        @block.scalar
        def _(act):
            act.dma_start(wcmp[:, :], t["Wcmp"]).then_inc(c_in, 16)
            act.dma_start(bcmp[:, :], t["bcmp"].broadcast_to([P, 1])).then_inc(c_in, 16)
            act.dma_start(norm_w[:, :], t["norm_w"]).then_inc(c_in, 16)
            act.dma_start(bk[:, :], t["bk"]).then_inc(c_in, 16)
            act.dma_start(bv[:, :], t["bv"].broadcast_to([P, D])).then_inc(c_in, 16)
            act.dma_start(ident[:, :], t["ident"]).then_inc(c_in, 16)
            act.dma_start(band[:, :], t["band"]).then_inc(c_in, 16)
            act.dma_start(diag32[:, :], t["diag"]).then_inc(c_in, 16)
            act.dma_start(cosk[:, :], t["cos"]).then_inc(c_in, 16)
            act.dma_start(sink[:, :], t["sin"]).then_inc(c_in, 16)
            for c in range(NCH):
                act.wait_ge(wmax, 2 * (c + 1))
                act.activation(weight[:, c % 2, :], weight[:, c % 2, :], ACT.Exp).then_inc(wexp, 1)
            act.wait_ge(kproj, 1)
            act.activation(square[:, :], bank[4][:, :], ACT.Square, bias=bk[:, 0:1]).then_inc(ksq, 1)

        @block.tensor
        def _(pe):
            pe.wait_ge(x_in, 16 * (KC + 2))
            pe.wait_ge(ready, 1)
            for c in range(NCH):
                for k in range(KC):
                    mm = pe.matmul(bank[c][:, :], wcmp_rep[:, k, :], xT[:, k, c * CH:(c + 1) * CH],
                                   start=(k == 0), stop=(k == KC - 1))
                mm.then_inc(logits, 1)
            pe.wait_ge(ent, KC * NCH)
            for k in range(KC):
                mm = pe.matmul(bank[4][:, :], wk[:, k, :], entT[:, k, :], start=(k == 0), stop=(k == KC - 1))
            mm.then_inc(kproj, 1)
            for b in range(CB):
                for k in range(KC):
                    mm = pe.matmul(bank[5][:, b * D:(b + 1) * D], entT[:, k, b * P:(b + 1) * P], wv[:, k, :],
                                   start=(k == 0), stop=(k == KC - 1))
            mm.then_inc(vproj, 1)
            pe.wait_ge(ksq, 1)
            pe.matmul(bank[6][:, :], ones[:, :], square[:, :], start=True, stop=True).then_inc(kssq, 1)

        @block.gpsimd
        def _(pool):
            pool.memset(half[:, :], -0.5).then_inc(krstd, 1)
            pool.wait_ge(kms, 1)
            pool.wait_ge(krstd, 1)
            pool.tensor_tensor(rstd[:, :], ms[:, :], half[:, :], ALU.pow).then_inc(krstd, 1)

        @block.vector
        def _(dve):
            dve.wait_ge(c_in, 16 * 10)
            dve.memset(ones[:, :], 1.0)
            dve.tensor_copy(wcmp_rep[:, :, :], wcmp[:, :].unsqueeze(2).to_broadcast([P, KC, P])).then_inc(ready, 1)
            dve.tensor_copy(identb[:, :], ident[:, :])
            dve.tensor_copy(diag[:, :], diag32[:, :])
            for c in range(NCH):
                b = c % 2
                dve.wait_ge(logits, c + 1)
                dve.tensor_scalar(logit[:, b, :], bank[c][:, :], bcmp[:, 0:1], None, ALU.add).then_inc(wlog, 1)
                dve.wait_ge(wlog, c + 1)
                by4 = logit[:, b, :].rearrange("p (c r) -> p c r", r=RATIO)
                w4 = weight[:, b, :].rearrange("p (c r) -> p c r", r=RATIO)
                dve.tensor_reduce(gmax[:, b, :], by4, AX.X, ALU.max).then_inc(wmax, 1)
                dve.wait_ge(wmax, 2 * c + 1)
                dve.tensor_tensor(w4, by4, gmax[:, b, :].unsqueeze(2).to_broadcast([P, P, RATIO]),
                                  ALU.subtract).then_inc(wmax, 1)
                dve.wait_ge(wexp, c + 1)
                dve.tensor_reduce(gsum[:, b, :], w4, AX.X, ALU.add).then_inc(wnorm, 1)
                dve.wait_ge(wnorm, 3 * c + 1)
                dve.reciprocal(gsum[:, b, :], gsum[:, b, :]).then_inc(wnorm, 1)
                dve.wait_ge(wnorm, 3 * c + 2)
                dve.tensor_tensor(w4, w4, gsum[:, b, :].unsqueeze(2).to_broadcast([P, P, RATIO]),
                                  ALU.mult).then_inc(wnorm, 1)
                dve.wait_ge(wnorm, 3 * c + 3)
                for k in range(KC):
                    n = c * KC + k
                    dve.tensor_tensor(product[:, n % 2, :], xT[:, k, c * CH:(c + 1) * CH], weight[:, b, :],
                                      ALU.mult).then_inc(step, 1)
                    dve.wait_ge(step, n + 1)
                    dve.tensor_reduce(entT[:, k, c * P:(c + 1) * P],
                                      product[:, n % 2, :].rearrange("p (c r) -> p c r", r=RATIO),
                                      AX.X, ALU.add).then_inc(ent, 1)
            n0 = NCH * KC
            dve.tensor_scalar(cosq[:, :], cosk[:, :], norm_w[:, 1:2], None, ALU.mult).then_inc(step, 1)
            dve.tensor_scalar(sinq[:, :], sink[:, :], norm_w[0:2 * ROT, 1:2], None, ALU.mult).then_inc(step, 1)
            dve.wait_ge(step, n0 + 2)
            dve.tensor_scalar(cosk[:, :], cosk[:, :], norm_w[:, 0:1], None, ALU.mult).then_inc(step, 1)
            dve.tensor_scalar(sink[:, :], sink[:, :], norm_w[0:2 * ROT, 0:1], None, ALU.mult).then_inc(step, 1)
            dve.wait_ge(step, n0 + 4)
            dve.wait_ge(kproj, 1)
            dve.wait_ge(ksq, 1)
            ends = slice(RATIO - 1, S, RATIO)
            dve.scalar_tensor_tensor(turned[0:ROT, :], bank[4][ROT:2 * ROT, :], bk[ROT:2 * ROT, 0:1],
                                     sink[ROT:2 * ROT, ends], ALU.add, ALU.mult)
            dve.scalar_tensor_tensor(turned[ROT:2 * ROT, :], bank[4][0:ROT, :], bk[0:ROT, 0:1],
                                     sink[0:ROT, ends], ALU.add, ALU.mult).then_inc(step, 1)
            dve.scalar_tensor_tensor(ckT[:, :], bank[4][:, :], bk[:, 0:1], cosk[:, ends],
                                     ALU.add, ALU.mult).then_inc(step, 1)
            dve.wait_ge(step, n0 + 6)
            dve.tensor_tensor(ckT[0:2 * ROT, :], ckT[0:2 * ROT, :], turned[:, :], ALU.add).then_inc(step, 1)
            dve.wait_ge(kssq, 1)
            dve.tensor_scalar(ms[:, :], bank[6][:, :], 1.0 / D, EPS, ALU.mult, ALU.add).then_inc(kms, 1)
            dve.wait_ge(krstd, 2)
            dve.wait_ge(step, n0 + 7)
            dve.tensor_tensor(ckT[:, :], ckT[:, :], rstd[:, :], ALU.mult)
            dve.wait_ge(vproj, 1)
            dve.tensor_tensor(cv[:, :, :], bank[5][:, :].rearrange("p (b d) -> p b d", b=CB),
                              bv[:, :].unsqueeze(1).to_broadcast([P, CB, D]), ALU.add)
            dve.wait_ge(r_in, 32)
            dve.tensor_tensor(acc[:, :, :], acc[:, :, :], bo[:, :].unsqueeze(1).to_broadcast([P, NT, HID]), ALU.add)


def heads(nc, t, bank, xT, acc, ident, slots_dram, zero_sem, ones, half, band, diag, identb, cosk, cosq, sink, sinq, ckT, cv,
          sb, sem):
    wh = [sb(f"wh{i}", [P, HEAD_COLS]) for i in range(2)]
    wo = sb("wo", [P, 2, HID])
    kT = [sb(f"kT{i}", [P, S]) for i in range(2)]
    qT = [sb(f"qT{i}", [P, S]) for i in range(2)]
    v = [sb(f"v{i}", [P, NT, D]) for i in range(2)]
    turned = [sb(f"turned{i}", [2 * ROT, CH]) for i in range(2)]
    square = [sb(f"square{i}", [P, CH]) for i in range(2)]
    kms = sb("kms", [P, NT])
    qms = sb("qms", [P, NT])
    krstd = [sb(f"krstd{i}", [P, NT]) for i in range(2)]
    qfac = [sb(f"qfac{i}", [P, NT]) for i in range(2)]
    nfac = [sb(f"nfac{i}", [P, NT]) for i in range(2)]
    top = [sb(f"top{i}", [P, TOPK + 1]) for i in range(2)]
    nbias = [sb(f"nbias{i}", [P, 2]) for i in range(2)]
    total = [sb(f"total{i}", [P, 2]) for i in range(2)]
    share = [sb(f"share{i}", [P, 2]) for i in range(2)]
    taken = sb("taken", [P, C])
    prob = [sb(f"prob{i}", [P, C + 2 * P]) for i in range(2)]
    probT = sb("probT", [P, C + 2 * P])
    ctx_even = sb("ctx_even", [P, S])
    ctx_odd = sb("ctx_odd", [P, 2, P])

    b_score, b_local, b_turn_s, b_turn_l, b_unit, b_ctx, b_out = (
        bank[0], bank[1], bank[2], bank[3], (bank[4], bank[5]), bank[6], bank[7])
    SSQ = 2 * P

    zeros = sb("zeros", [P, 2 * HID])
    xs, ys = slots_dram
    s_zero = sem("zeros_made")
    w_in = [sem("w_in_even"), sem("w_in_odd")]
    wo_in = sem("wo_in")
    s_scores = sem("scores_done")
    s_ssq = sem("ssq_done")
    s_turn = sem("turn_done")
    s_unit = sem("unit_done")
    s_ctx = sem("ctx_done")
    s_out = sem("out_done")
    s_top = sem("top_done")
    s_bias = sem("bias_done")
    s_taken = sem("taken_done")
    s_total = sem("total_done")
    s_share = sem("share_done")
    s_uvec = sem("unit_vector")
    s_ms = sem("ms_done")
    s_nfac = sem("nfac_done")
    s_acc = sem("acc_done")
    s_exp = sem("exp_done")
    s_probT = sem("probT_done")
    s_square = sem("square_done")
    s_ctxc = sem("ctx_copied")
    s_prob = sem("prob_done")
    s_rope = sem("rope_done")
    s_rstd = sem("rstd_done")

    def weight(par, which, k):
        return wh[par][:, (which * KC + k) * D:(which * KC + k + 1) * D]

    def bias_col(par, which, rows=slice(0, P)):
        col = 3 * KC * D + which
        return wh[par][rows, col:col + 1]

    def blocks(tile):
        return tile // TPC + 1

    def width(tile):
        return EPT * (tile + 1)

    def local_cols(tile):
        return slice(0 if tile else P, 2 * P)

    def chunk(c):
        return slice(c * CH, (c + 1) * CH)

    def pe_unit(pe, h, par, u, of_kind):
        n = h * 16 + u
        dst = b_unit[u % 2]
        if u == 0:
            pe.wait_ge(w_in[par], of_kind * 16 + 16)
        wait_for(pe, s_uvec, n - 1)
        if u < 8:
            which, c = (1, u) if u < 4 else (0, u - 4)
            for k in range(KC):
                mm = pe.matmul(dst[:, :], weight(par, which, k), xT[:, k, chunk(c)],
                               start=(k == 0), stop=(k == KC - 1))
        elif u < 12:
            for i in range(TPC):
                tile = (u - 8) * TPC + i
                for k in range(KC):
                    mm = pe.matmul(dst[:, i * D:(i + 1) * D], xT[:, k, tile * P:(tile + 1) * P],
                                   weight(par, 2, k), start=(k == 0), stop=(k == KC - 1))
        else:
            pe.wait_ge(s_rstd, h * 2 + 1)
            for i in range(TPC):
                tile = (u - 12) * TPC + i
                mm = pe.transpose(dst[:, i * P:(i + 1) * P],
                                  krstd[par][:, tile:tile + 1].to_broadcast([P, P]), ident[:, :])
        mm.then_inc(s_unit, 1)

    def pe_ssq(pe, h, u):
        pe.wait_ge(s_square, h * 8 + (u + 1))
        for i in range(TPC):
            col = SSQ + TPC * u + i
            mm = pe.matmul(b_local[:, col:col + 1], square[u % 2][:, i * P:(i + 1) * P], ones[:, 0:1],
                           start=True, stop=True)
        if u % 4 == 3:
            mm.then_inc(s_ssq, 1)

    def pe_scores(pe, n, h, par, tile):
        if tile == 0:
            pe.wait_ge(s_uvec, n + 16)
            pe.wait_ge(s_rope, h * 8 + 8)
        w = width(tile)
        q = qT[par][:, tile * P:(tile + 1) * P]
        pe.matmul(b_score[:, 0:w], q, ckT[:, 0:w], start=True, stop=False)
        pe.matmul(b_score[:, w - EPT:w], identb[:, :], diag[:, :], start=False, stop=True)
        pe.matmul(b_local[:, local_cols(tile)], q, kT[par][:, max(tile - 1, 0) * P:(tile + 1) * P],
                  start=True, stop=True).then_inc(s_scores, 1)

    def pe_turn(pe, n, tile):
        pe.wait_ge(s_prob, n + 1)
        wait_for(pe, s_probT, n)
        pr = prob[tile % 2]
        for b in range(blocks(tile)):
            pe.transpose(b_turn_s[:, b * P:(b + 1) * P], pr[:, b * P:(b + 1) * P], ident[:, :])
        for b in ((0, 1) if tile else (1,)):
            mm = pe.transpose(b_turn_l[:, b * P:(b + 1) * P], pr[:, C + b * P:C + (b + 1) * P], ident[:, :])
        mm.then_inc(s_turn, 1)

    def pe_context(pe, n, par, tile):
        pe.wait_ge(s_probT, n + 1)
        wait_for(pe, s_ctxc, n)
        parts = [(cv[:, b, :], probT[:, b * P:(b + 1) * P]) for b in range(blocks(tile))]
        if tile:
            parts.append((v[par][:, tile - 1, :], probT[:, C:C + P]))
        parts.append((v[par][:, tile, :], probT[:, C + P:C + 2 * P]))
        for m, (val, pt) in enumerate(parts):
            mm = pe.matmul(b_ctx[:, 0:P], val, pt, start=(m == 0), stop=(m == len(parts) - 1))
        mm.then_inc(s_ctx, 1)

    def pe_out(pe, i, n, tile):
        if tile == 0:
            pe.wait_ge(wo_in, i * 16 + 16)
        pe.wait_ge(s_ctxc, n + 1)
        wait_for(pe, s_acc, i * 16 + tile)
        pe.matmul(b_out[:, :], ctx_even[:, tile * P:(tile + 1) * P], wo[:, 0, :], start=True, stop=False)
        pe.matmul(b_out[:, :], ctx_odd[:, tile % 2, :], wo[:, 1, :], start=False, stop=True).then_inc(s_out, 1)

    def pe_pair(pe, i, first=False, last=False):
        for j in range(2 * NT):
            n, par, tile = i * 32 + j, j // NT, j % NT
            nxt = i * 2 + (par + 1)
            units = not (last and par == 1)
            wait_for(pe, s_taken, n)
            wait_for(pe, s_exp, n)
            if units and 1 <= tile <= 8:
                pe_ssq(pe, nxt, tile - 1)
            pe_scores(pe, n, i * 2 + par, par, tile)
            if j or not first:
                pe_turn(pe, n - 1, (tile - 1) % NT)
            if units:
                pe_unit(pe, nxt, 1 - par, tile, i + par)
            if j >= NT + 2:
                pe_out(pe, i, n - 2, tile - 2)
            elif j < 2 and not first:
                pe_out(pe, i - 1, n - 2, NT - 2 + j)
            if j or not first:
                pe_context(pe, n - 1, par if tile else 1 - par, (tile - 1) % NT)

    def dve_ms(dve, h, which):
        dve.wait_ge(s_ssq, h * 2 + (which + 1))
        cols = slice(SSQ + NT * which, SSQ + NT * (which + 1))
        if which == 0:
            dve.tensor_scalar(kms[:, :], b_local[:, cols], 1.0 / D, EPS, ALU.mult, ALU.add).then_inc(s_ms, 1)
        else:
            dve.tensor_scalar(qms[:, :], b_local[:, cols], D * EPS, None, ALU.add).then_inc(s_ms, 1)

    def dve_unit(dve, h, par, u):
        n = h * 16 + u
        src = b_unit[u % 2]
        if u < 8:
            dve.wait_ge(s_square, h * 8 + (u + 1))
            which, c, cos, sin, dst = (1, u, cosk, sink, kT) if u < 4 else (0, u - 4, cosq, sinq, qT)
            if u >= 2:
                dve.wait_ge(s_rope, h * 8 + (u - 1))
            elif not (isinstance(h, int) and h == 0):
                dve.wait_ge(s_rope, h * 8 + (u - 1))
            lo, hi = slice(0, ROT), slice(ROT, 2 * ROT)
            dve.scalar_tensor_tensor(turned[u % 2][lo, :], src[hi, :], bias_col(par, which, hi),
                                     sin[hi, chunk(c)], ALU.add, ALU.mult)
            dve.scalar_tensor_tensor(turned[u % 2][hi, :], src[lo, :], bias_col(par, which, lo),
                                     sin[lo, chunk(c)], ALU.add, ALU.mult)
            dve.scalar_tensor_tensor(dst[par][:, chunk(c)], src[:, :], bias_col(par, which),
                                     cos[:, chunk(c)], ALU.add, ALU.mult).then_inc(s_uvec, 1)
        elif u < 12:
            dve.wait_ge(s_unit, n + 1)
            g = u - 8
            blv = wh[par][:, 3 * KC * D + 2:HEAD_COLS]
            dve.tensor_tensor(v[par][:, g * TPC:(g + 1) * TPC, :], src[:, :].rearrange("p (a d) -> p a d", a=TPC),
                              blv.unsqueeze(1).to_broadcast([P, TPC, D]), ALU.add).then_inc(s_uvec, 1)
        else:
            dve.wait_ge(s_unit, n + 1)
            dve.wait_ge(s_rope, h * 8 + 4)
            keys = kT[par][:, chunk(u - 12)]
            dve.tensor_tensor(keys, keys, src[:, :], ALU.mult).then_inc(s_uvec, 1)

    def dve_nfac(dve, h, par):
        dve.wait_ge(s_rstd, h * 2 + 2)
        dve.tensor_scalar(nfac[par][:, :], qfac[par][:, :], -1.0, None, ALU.mult).then_inc(s_nfac, 1)

    def dve_step(dve, i, n, par, tile, ms_of):
        b, w, lc = tile % 2, width(tile), local_cols(tile)
        dve.wait_ge(s_scores, n + 1)
        wait_for(dve, s_turn, n - 1)
        dve.memset(prob[b][:, w:blocks(tile) * P] if w < blocks(tile) * P else total[b][:, :], 0.0)
        if ms_of is not None:
            dve_ms(dve, ms_of, tile // 8)
        pl = prob[b][:, C:C + 2 * P]
        dve.tensor_tensor_reduce(pl[:, lc], b_local[:, lc], band[:, lc], 1.0, NEG, ALU.add, ALU.max,
                                 top[b][:, TOPK:TOPK + 1]).then_inc(s_top, 1)
        dve.max(top[b][:, 0:TOPK], b_score[:, 0:w]).then_inc(s_top, 1)
        dve.wait_ge(s_top, n * 2 + 2)
        if tile == 0:
            dve.wait_ge(s_nfac, i * 2 + (par + 1))
        dve.tensor_scalar(nbias[b][:, :], top[b][:, 0:TOPK + 1:TOPK], FLOOR, nfac[par][:, tile:tile + 1],
                          ALU.max, ALU.mult).then_inc(s_bias, 1)
        dve.match_replace(taken[:, 0:w], top[b][:, 0:TOPK], b_score[:, 0:w], TAKEN).then_inc(s_taken, 1)
        dve.wait_ge(s_exp, n + 1)
        dve.wait_ge(s_taken, n + 1)
        dve.scalar_tensor_tensor(prob[b][:, 0:w], taken[:, 0:w], TAKEN / 2, prob[b][:, 0:w], ALU.is_ge, ALU.mult,
                                 accum_out=total[b][:, 0:1]).then_inc(s_total, 1)
        dve.wait_ge(s_total, n * 2 + 1)
        dve.tensor_scalar(total[b][:, :], total[b][:, :], 1e-9, 2.0, ALU.max, ALU.mult).then_inc(s_total, 1)
        dve.wait_ge(s_total, n * 2 + 2)
        dve.reciprocal(share[b][:, :], total[b][:, :]).then_inc(s_share, 1)

    def dve_acc(dve, i, tile):
        dve.wait_ge(s_out, i * 16 + (tile + 1))
        dve.tensor_tensor(acc[:, tile, :], acc[:, tile, :], b_out[:, :], ALU.add).then_inc(s_acc, 1)

    def dve_pair(dve, i, first=False, last=False):
        for j in range(2 * NT):
            n, par, tile = i * 32 + j, j // NT, j % NT
            nxt = i * 2 + (par + 1)
            units = not (last and par == 1)
            dve_step(dve, i, n, par, tile, nxt if units and tile in (4, 8) else None)
            if units:
                dve_unit(dve, nxt, 1 - par, tile)
                if tile == 11:
                    dve_nfac(dve, nxt, 1 - par)
            if j >= NT + 2:
                dve_acc(dve, i, tile - 2)
            elif j < 2 and not first:
                dve_acc(dve, i - 1, NT - 2 + j)

    def act_square(act, h, par, u):
        act.wait_ge(s_unit, h * 16 + (u + 1))
        act.activation(square[u % 2][:, :], b_unit[u % 2][:, :], ACT.Square,
                       bias=bias_col(par, 1 if u < 4 else 0)).then_inc(s_square, 1)

    def act_probT(act, n, tile):
        act.wait_ge(s_turn, n + 1)
        w = blocks(tile) * P
        act.copy(probT[:, 0:w], b_turn_s[:, 0:w])
        lc = local_cols(tile)
        act.copy(probT[:, C:C + 2 * P][:, lc], b_turn_l[:, lc]).then_inc(s_probT, 1)

    def act_exp(act, n, par, tile):
        b, w = tile % 2, width(tile)
        act.wait_ge(s_bias, n + 1)
        pl = prob[b][:, C:C + 2 * P][:, local_cols(tile)]
        act.activation(pl, pl, ACT.Exp, bias=nbias[b][:, 1:2], scale=qfac[par][:, tile:tile + 1],
                       accum_out=total[b][:, 1:2])
        act.wait_ge(s_taken, n + 1)
        act.activation(prob[b][:, 0:w], b_score[:, 0:w], ACT.Exp, bias=nbias[b][:, 0:1],
                       scale=qfac[par][:, tile:tile + 1]).then_inc(s_exp, 1)

    def act_ctx(act, n, par, tile):
        act.wait_ge(s_ctx, n + 1)
        dst = ctx_odd[:, tile % 2, :] if par else ctx_even[:, tile * P:(tile + 1) * P]
        act.copy(dst, b_ctx[:, 0:P]).then_inc(s_ctxc, 1)

    def act_pair(act, i, first=False, last=False):
        for j in range(2 * NT):
            n, par, tile = i * 32 + j, j // NT, j % NT
            if j or not first:
                act_probT(act, n - 1, (tile - 1) % NT)
            act_exp(act, n, par, tile)
            if tile < 8 and not (last and par == 1):
                act_square(act, i * 2 + (par + 1), 1 - par, tile)
            if j or not first:
                act_ctx(act, n - 1, par if tile else 1 - par, (tile - 1) % NT)

    def pool_rope(pool, h, par, u):
        pool.wait_ge(s_uvec, h * 16 + (u + 1))
        dst = kT[par] if u < 4 else qT[par]
        part = dst[0:2 * ROT, chunk(u % 4)]
        pool.tensor_tensor(part, part, turned[u % 2][:, :], ALU.add).then_inc(s_rope, 1)

    def pool_rstd(pool, h, par, which):
        pool.wait_ge(s_ms, h * 2 + (which + 1))
        src, dst = (kms, krstd) if which == 0 else (qms, qfac)
        pool.tensor_tensor(dst[par][:, :], src[:, :], half[:, 0:NT], ALU.pow).then_inc(s_rstd, 1)

    def pool_prob(pool, n, tile):
        b, w = tile % 2, width(tile)
        pool.wait_ge(s_share, n + 1)
        pl = prob[b][:, C:C + 2 * P][:, local_cols(tile)]
        pool.tensor_tensor(pl, pl, share[b][:, 1:2].to_broadcast(list(pl.shape)), ALU.mult)
        pool.tensor_scalar(prob[b][:, 0:w], prob[b][:, 0:w], share[b][:, 0:1], 1.0, ALU.mult,
                           ALU.mult).then_inc(s_prob, 1)

    def pool_pair(pool, i, first=False, last=False):
        for j in range(2 * NT):
            n, par, tile = i * 32 + j, j // NT, j % NT
            nxt = i * 2 + (par + 1)
            units = not (last and par == 1)
            if units and tile in (4, 8):
                pool_rstd(pool, nxt, 1 - par, tile // 8)
            pool_prob(pool, n, tile)
            if units and tile < 8:
                pool_rope(pool, nxt, 1 - par, tile)

    NP = NH // 2
    with nc.Block() as block:
        @block.sync
        def _(sp):
            def load_head(h, par):
                wait_for(sp, s_uvec, h * 16 - 16)
                sp.dma_start(wh[par][:, :], t["wh"][h, :, :] if isinstance(h, int)
                             else t["wh"][bass.ds(h, 1), :, :].rearrange("o p c -> (o p) c")).then_inc(w_in[par], 16)

            def load_wo(i):
                wait_for(sp, s_out, i * 16)
                rows = t["Wo"][0:2 * D, :] if isinstance(i, int) and i == 0 else t["Wo"][bass.ds(i * (2 * D), 2 * D), :]
                sp.dma_start(wo[:, :, :], rows.rearrange("(a d) n -> d a n", a=2)).then_inc(wo_in, 16)

            load_head(0, 0)
            load_head(1, 1)
            load_wo(0)
            sp.wait_ge(s_zero, 1)
            for n in range(MAXT // 2):
                sp.dma_start(xs[n * 2 * P:(n + 1) * 2 * P, :].rearrange("(p a) d -> p (a d)", a=2),
                             zeros[:, :]).then_inc(zero_sem, 16)
            for n in range(PICK * NT // 2, MAXT // 2):
                sp.dma_start(ys[n * 2 * P:(n + 1) * 2 * P, :].rearrange("(p a) d -> p (a d)", a=2),
                             zeros[:, :]).then_inc(zero_sem, 16)
            with sp.Fori(1, NP) as i:
                load_head(i * 2, 0)
                load_head(i * 2 + 1, 1)
                load_wo(i)

        @block.tensor
        def _(pe):
            for u in range(NT):
                pe_unit(pe, 0, 0, u, 0)
                if 1 <= u <= 8:
                    if u == 5:
                        pe.wait_ge(s_ms, 1)
                    pe_ssq(pe, 0, u - 1)
            pe.wait_ge(s_ms, 2)
            pe_pair(pe, 0, first=True)
            with pe.Fori(1, NP - 1) as i:
                pe_pair(pe, i)
            pe_pair(pe, NP - 1, last=True)
            n = NH * NT
            pe_turn(pe, n - 1, NT - 1)
            pe_out(pe, NP - 1, n - 2, NT - 2)
            pe_context(pe, n - 1, 1, NT - 1)
            pe_out(pe, NP - 1, n - 1, NT - 1)

        @block.vector
        def _(dve):
            for u in range(NT):
                dve_unit(dve, 0, 0, u)
                if u in (4, 8):
                    dve_ms(dve, 0, u // 8)
            dve_nfac(dve, 0, 0)
            dve_pair(dve, 0, first=True)
            with dve.Fori(1, NP - 1) as i:
                dve_pair(dve, i)
            dve_pair(dve, NP - 1, last=True)
            dve_acc(dve, NP - 1, NT - 2)
            dve_acc(dve, NP - 1, NT - 1)

        @block.scalar
        def _(act):
            for u in range(8):
                act_square(act, 0, 0, u)
            act_pair(act, 0, first=True)
            with act.Fori(1, NP - 1) as i:
                act_pair(act, i)
            act_pair(act, NP - 1, last=True)
            n = NH * NT
            act_probT(act, n - 1, NT - 1)
            act_ctx(act, n - 1, 1, NT - 1)

        @block.gpsimd
        def _(pool):
            pool.memset(zeros[:, :], 0.0).then_inc(s_zero, 1)
            for u in range(8):
                pool_rope(pool, 0, 0, u)
                if u == 4:
                    pool_rstd(pool, 0, 0, 0)
            pool_rstd(pool, 0, 0, 1)
            pool_pair(pool, 0, first=True)
            with pool.Fori(1, NP - 1) as i:
                pool_pair(pool, i)
            pool_pair(pool, NP - 1, last=True)


def feed_forward(nc, t, bank, acc, ident, xs, ys, zeroed, sb_in, sem_in):
    whole = ExitStack()

    def sb(name, shape, dt=F32, stack=whole):
        return sb_in(name, shape, dt, stack)

    def sem(name, stack=whole):
        return sem_in(name, stack)

    with whole:
        slots = sb("slots", [P, NT, PICK], U32)
        pick_w = sb("pick_w", [P, NT, PICK])
        tile_expert = sb("tile_expert", [P, MAXT], I32)
        first_tile = sb("first_tile", [P, E], I32)
        pair_count = sb("pair_count", [P, 2], I32)
        mv = sb("mv", [P, NT, 2])
        rstd = sb("rstd2", [P, NT])
        neghalf = sb("neghalf", [P, NT])
        stats = sb("stats", [P, 2, 6])

        mid = ExitStack()
        with mid:
            whi = sb("whi", [P, 2, WCOLS], F32R, mid)
            wlo = sb("wlo", [P, 2, WCOLS], F32R, mid)
            first_norm_and_split(nc, t, acc, mv, rstd, neghalf, stats, whi, wlo,
                                 lambda n, s, d, k: sb(n, s, d, k), sem)
            route_and_shared(nc, t, bank, acc, ident, xs, zeroed, slots, pick_w, tile_expert, first_tile,
                             pair_count, whi, wlo, sb, sem)
            routed(nc, t, bank, ident, xs, ys, tile_expert, first_tile, pair_count, whi, wlo, sb, sem)
        combine(nc, t, acc, ys, slots, pick_w, mv, rstd, neghalf, stats, sb, sem)


def first_norm_and_split(nc, t, acc, mv, rstd, neghalf, stats, whi, wlo, sb, sem):
    st = ExitStack()
    with st:
        staged = sb("staged_shared", [P, WCOLS], F32, st)
        s_in, s_hi, s_lo, s_st, s_mv, s_eps, s_pow, s_half = (sem(x, st) for x in (
            "shared_in", "shared_hi", "shared_lo", "ln1_stats", "ln1_mv", "ln1_eps", "ln1_pow", "ln1_half"))
        with nc.Block() as block:
            @block.sync
            def _(sp):
                for s in range(NSH):
                    if s:
                        sp.wait_ge(s_lo, s)
                    sp.dma_start(staged[:, :], t["wexp"][E + s, :, :]).then_inc(s_in, 16)

            @block.gpsimd
            def _(pool):
                pool.memset(neghalf[:, :], -0.5).then_inc(s_half, 1)
                for s in range(NSH):
                    pool.wait_ge(s_in, 16 * (s + 1))
                    pool.tensor_copy(whi[:, s, :], staged[:, :]).then_inc(s_hi, 1)
                    if s == 0:
                        pool.wait_ge(s_half, 1)
                        pool.wait_ge(s_eps, 1)
                        pool.tensor_tensor(rstd[:, :], rstd[:, :], neghalf[:, :], ALU.pow).then_inc(s_pow, 1)
                    pool.wait_ge(s_hi, s + 1)
                    pool.tensor_tensor(wlo[:, s, :], staged[:, :], whi[:, s, :].bitcast(F32),
                                       ALU.subtract).then_inc(s_lo, 1)

            @block.vector
            def _(dve):
                for n in range(NT):
                    dve.bn_stats(stats[:, n % 2, :], acc[:, n, :]).then_inc(s_st, 1)
                    dve.wait_ge(s_st, n + 1)
                    dve.bn_aggr(mv[:, n, :], stats[:, n % 2, :]).then_inc(s_mv, 1)
                dve.wait_ge(s_mv, NT)
                dve.tensor_scalar(rstd[:, :], mv[:, :, 1], LN_EPS, None, ALU.add).then_inc(s_eps, 1)
                dve.wait_ge(s_pow, 1)
                for n in range(NT):
                    dve.tensor_scalar(acc[:, n, :], acc[:, n, :], mv[:, n, 0:1], rstd[:, n:n + 1],
                                      ALU.subtract, ALU.mult)


def three_products(pe, out, hi_lo_w, hi_lo_x, first, last):
    (wh_, wl_), (xh_, xl_) = hi_lo_w, hi_lo_x
    pe.matmul(out, wl_, xh_, start=first, stop=False)
    pe.matmul(out, wh_, xl_, start=False, stop=False)
    return pe.matmul(out, wh_, xh_, start=False, stop=last)


def w13_cols(w, k):
    at = (w * KC + k) * INTER
    return at, at + INTER


def w2_cols(b):
    at = 2 * KC * INTER + b * HID
    return at, at + HID


def route_and_shared(nc, t, bank, acc, ident, xs, zeroed, slots, pick_w, tile_expert, first_tile, pair_count,
                     whi, wlo, sb, sem):
    st = ExitStack()
    with st:
        raw = [sb(f"raw{i}", [P, KC, P], F32, st) for i in range(2)]
        gateT = sb("gateT", [P, KC, E], F32, st)
        ebias = sb("ebias", [P, E], F32, st)
        sig = sb("sig", [P, NT, E], F32, st)
        choice = sb("choice", [P, NT, E], F32, st)
        gbest = sb("gbest", [P, NT, G], F32, st)
        cmp = sb("cmp", [P, NT, E], F32, st)
        grank = sb("grank", [P, NT, G], F32, st)
        rank = sb("rank", [P, NT, E], F32, st)
        picked = sb("picked", [P, NT, E], F32, st)
        pickedb = sb("pickedb", [P, NT, E], BF16, st)
        trib = sb("trib", [P, 2, P], BF16, st)
        tri = sb("tri", [P, 2, P], F32, st)
        before = [sb(f"before{i}", [P, NT, E], F32, st) for i in range(2)]
        slotf = sb("slotf", [P, NT, E], F32, st)
        load = sb("load", [P, E], F32, st)
        ramp = sb("ramp", [P, MAXT], F32, st)
        tiles = [sb(f"tiles{i}", [P, E], F32, st) for i in range(2)]
        by16 = sb("by16", [P, E, E], F32, st)
        byt = sb("byt", [P, MAXT, E], F32, st)
        texp = sb("texp", [P, MAXT], F32, st)
        slot4 = sb("slot4", [P, NT, PICK], F32, st)
        csum = sb("csum", [P, NT], F32, st)
        xhi = [sb(f"xhi{i}", [P, KC, CH], F32R, st) for i in range(1)]
        xlo = [sb(f"xlo{i}", [P, KC, CH], F32R, st) for i in range(1)]
        gate = [sb(f"gate{i}", [P, CH], F32, st) for i in range(2)]
        hid = [sb(f"hid{i}", [P, CH], F32, st) for i in range(2)]
        hhi = sb("hhi", [P, NSH * HB, CH], F32R, st)
        hlo = sb("hlo", [P, NSH * HB, CH], F32R, st)

        g_in, s_turned, s_raw, s_logits, s_sig, s_r, s_pick, s_count, s_slots, s_scat = (sem(x, st) for x in (
            "gate_in", "x1_turned", "x1_raw", "gate_done", "sig_done", "router_step", "picked_done",
            "counts_done", "slots_done", "scatter_done"))
        s_xt, s_xhi, s_xlo, s_up, s_silu, s_hid, s_hhi, s_hlo, s_y, s_sum = (sem(x, st) for x in (
            "sh_xt", "sh_xhi", "sh_xlo", "sh_up", "sh_silu", "sh_hid", "sh_hhi", "sh_hlo", "sh_y", "sh_sum"))
        NB = NSH * HB

        with nc.Block() as block:
            @block.sync
            def _(sp):
                sp.dma_start(gateT[:, :, :], t["gateT"].rearrange("(k p) e -> p k e", p=P)).then_inc(g_in, 16)
                sp.dma_start(ebias[:, :], t["ebias"].broadcast_to([P, E])).then_inc(g_in, 16)
                sp.dma_start(tri[:, :, :], t["tri"]).then_inc(g_in, 16)
                sp.dma_start(ramp[:, :], t["ramp"].broadcast_to([P, MAXT])).then_inc(g_in, 16)

            @block.tensor
            def _(pe):
                pe.wait_ge(g_in, 64)

                def gate_logits(n):
                    pe.wait_ge(s_raw, n + 1)
                    for k in range(KC):
                        mm = pe.matmul(bank[7][:, n * E:(n + 1) * E], raw[n % 2][:, k, :], gateT[:, k, :],
                                       start=(k == 0), stop=(k == KC - 1))
                    return mm

                for n in range(NT):
                    if n >= 2:
                        pe.wait_ge(s_raw, n - 1)
                    for k in range(KC):
                        mm = pe.transpose(bank[5 + n % 2][:, k * P:(k + 1) * P], acc[:, n, k * P:(k + 1) * P], ident[:, :])
                    mm.then_inc(s_turned, 1)
                    if n:
                        gate_logits(n - 1)
                gate_logits(NT - 1).then_inc(s_logits, 1)

                def turn(c, k):
                    wait_for(pe, s_xlo, c * KC + k - 1)
                    for i in range(TPC):
                        mm = pe.transpose(bank[k % 2][:, i * P:(i + 1) * P], acc[:, c * TPC + i, k * P:(k + 1) * P],
                                          ident[:, :])
                    mm.then_inc(s_xt, 1)

                def up(c, q):
                    n = c * NB + q
                    s, b = divmod(q, HB)
                    rows = hb_rows(b)
                    if q == 0:
                        pe.wait_ge(s_xlo, (c + 1) * KC)
                    wait_for(pe, s_hid, n - 1)
                    for w in range(2):
                        for k in range(KC):
                            at = w13_cols(w, k)[0] + b * P
                            mm = three_products(pe, bank[2 + 2 * w + q % 2][0:rows, :],
                                                (whi[:, s, at:at + rows], wlo[:, s, at:at + rows]),
                                                (xhi[0][:, k, :], xlo[0][:, k, :]), k == 0, k == KC - 1)
                    mm.then_inc(s_up, 1)

                def down(c):
                    pe.wait_ge(s_hlo, (c + 1) * NB)
                    for i in range(TPC):
                        m = c * TPC + i
                        wait_for(pe, s_sum, m - 1)
                        for q in range(NB):
                            s, b = divmod(q, HB)
                            rows = hb_rows(b)
                            lo_, hi_ = w2_cols(b)
                            cols = slice(i * P, (i + 1) * P)
                            mm = three_products(pe, bank[6 + m % 2][:, :],
                                                (hhi[0:rows, q, cols], hlo[0:rows, q, cols]),
                                                (whi[0:rows, s, lo_:hi_], wlo[0:rows, s, lo_:hi_]),
                                                q == 0, q == NB - 1)
                        mm.then_inc(s_y, 1)

                pe.wait_ge(s_pick, 1)
                picks = pickedb[:, :, :].rearrange("p n e -> p (n e)")
                pe.matmul(bank[6][:, 0:NT * E], trib[:, 0, :], picks, start=True, stop=True)
                pe.matmul(bank[6][:, NT * E:2 * NT * E], trib[:, 1, :], picks, start=True, stop=True).then_inc(s_count, 1)
                pe.wait_ge(s_count, 2)
                for c in range(NCH):
                    for k in range(KC):
                        turn(c, k)
                    for q in range(NB):
                        up(c, q)
                    down(c)

            @block.scalar
            def _(act):
                for n in range(NT):
                    act.wait_ge(s_turned, n + 1)
                    act.copy(raw[n % 2][:, :, :], bank[5 + n % 2][:, :].rearrange("p (k t) -> p k t", k=KC)).then_inc(s_raw, 1)
                act.wait_ge(s_logits, 1)
                act.activation(sig[:, :, :], bank[7][:, 0:NT * E].rearrange("p (n e) -> p n e", e=E),
                               ACT.Sigmoid).then_inc(s_sig, 1)
                for c in range(NCH):
                    for k in range(KC):
                        act.wait_ge(s_xt, c * KC + k + 1)
                        wait_for(act, s_up, c * NB)
                        act.copy(xhi[0][:, k, :], bank[k % 2][:, :]).then_inc(s_xhi, 1)
                    for q in range(NB):
                        n = c * NB + q
                        rows = hb_rows(q % HB)
                        act.wait_ge(s_up, n + 1)
                        act.activation(gate[n % 2][0:rows, :], bank[2 + q % 2][0:rows, :], ACT.Silu).then_inc(s_silu, 1)
                        act.wait_ge(s_hid, n + 1)
                        wait_for(act, s_y, c * TPC)
                        act.copy(hhi[0:rows, q, :], hid[n % 2][0:rows, :]).then_inc(s_hhi, 1)

            @block.gpsimd
            def _(pool):
                pool.wait_ge(s_slots, 1)
                for z in zeroed:
                    pool.wait_ge(*z)
                for n in range(NT):
                    for k in range(PICK):
                        pool.indirect_dma_start(xs[:, :], bass.IndirectOffsetOnAxis(ap=slots[:, n, k:k + 1], axis=0),
                                                acc[:, n, :], None, bounds_check=MAXT * P - 1,
                                                oob_is_err=False).then_inc(s_scat, 16)
                pool.wait_ge(s_scat, 16 * NT * PICK)

            @block.vector
            def _(dve):
                count = [0]

                def then(ins):
                    count[0] += 1
                    ins.then_inc(s_r, 1)
                    dve.wait_ge(s_r, count[0])

                def prefix(bufs, total, axis_view):
                    a, shift = 0, 1
                    while shift < total:
                        x, y = axis_view(bufs[a]), axis_view(bufs[1 - a])
                        then(dve.tensor_copy(y[:, 0:shift, :], x[:, 0:shift, :]))
                        then(dve.tensor_tensor(y[:, shift:total, :], x[:, shift:total, :], x[:, 0:total - shift, :], ALU.add))
                        a, shift = 1 - a, 2 * shift
                    return bufs[a]

                dve.wait_ge(g_in, 64)
                then(dve.tensor_copy(trib[:, :, :], tri[:, :, :]))
                dve.wait_ge(s_sig, 1)
                then(dve.tensor_tensor(choice[:, :, :], sig[:, :, :], ebias[:, :].unsqueeze(1).to_broadcast([P, NT, E]),
                                       ALU.add))
                then(dve.tensor_reduce(gbest[:, :, :], choice[:, :, :].rearrange("p n (g e) -> p n g e", e=EG),
                                       AX.X, ALU.max))
                then(dve.memset(grank[:, :, :], 0.0))
                for o in range(G):
                    other = gbest[:, :, o:o + 1]
                    if o + 1 < G:
                        then(dve.tensor_tensor(cmp[:, :, o + 1:G], other.to_broadcast([P, NT, G - o - 1]),
                                               gbest[:, :, o + 1:G], ALU.is_ge))
                        then(dve.tensor_tensor(grank[:, :, o + 1:G], grank[:, :, o + 1:G], cmp[:, :, o + 1:G], ALU.add))
                    if o:
                        then(dve.tensor_tensor(cmp[:, :, 0:o], other.to_broadcast([P, NT, o]), gbest[:, :, 0:o], ALU.is_gt))
                        then(dve.tensor_tensor(grank[:, :, 0:o], grank[:, :, 0:o], cmp[:, :, 0:o], ALU.add))
                then(dve.tensor_scalar(grank[:, :, :], grank[:, :, :], float(PICK_G), None, ALU.is_lt))
                gm = grank[:, :, :].unsqueeze(3).to_broadcast([P, NT, G, EG])
                c4 = choice[:, :, :].rearrange("p n (g e) -> p n g e", e=EG)
                then(dve.tensor_tensor(c4, c4, gm, ALU.mult))
                then(dve.tensor_scalar(grank[:, :, :], grank[:, :, :], -1.0, -NEG, ALU.add, ALU.mult))
                then(dve.tensor_tensor(c4, c4, gm, ALU.add))
                then(dve.memset(rank[:, :, :], 0.0))
                for o in range(E):
                    other = choice[:, :, o:o + 1]
                    if o + 1 < E:
                        dve.tensor_tensor(cmp[:, :, o + 1:E], other.to_broadcast([P, NT, E - o - 1]),
                                          choice[:, :, o + 1:E], ALU.is_ge).then_inc(s_r, 1)
                        count[0] += 1
                    if o:
                        dve.tensor_tensor(cmp[:, :, 0:o], other.to_broadcast([P, NT, o]),
                                          choice[:, :, 0:o], ALU.is_gt).then_inc(s_r, 1)
                        count[0] += 1
                    dve.memset(cmp[:, :, o:o + 1], 0.0).then_inc(s_r, 1)
                    count[0] += 1
                    dve.wait_ge(s_r, count[0])
                    then(dve.tensor_tensor(rank[:, :, :], rank[:, :, :], cmp[:, :, :], ALU.add))
                then(dve.tensor_scalar(picked[:, :, :], rank[:, :, :], float(PICK), None, ALU.is_lt))
                dve.tensor_copy(pickedb[:, :, :], picked[:, :, :]).then_inc(s_pick, 1)
                then(dve.tensor_tensor(sig[:, :, :], sig[:, :, :], picked[:, :, :], ALU.mult))
                then(dve.tensor_reduce(csum[:, :], sig[:, :, :], AX.X, ALU.add))
                then(dve.reciprocal(csum[:, :], csum[:, :]))
                then(dve.tensor_tensor(sig[:, :, :], sig[:, :, :], csum[:, :].unsqueeze(2).to_broadcast([P, NT, E]),
                                       ALU.mult))
                dve.wait_ge(s_count, 1)
                ne = lambda b: b[:, :, :]
                within, sums = (bank[6][:, x * NT * E:(x + 1) * NT * E].rearrange("p (n e) -> p n e", e=E) for x in range(2))
                then(dve.tensor_copy(before[0][:, :, :], sums))
                full = prefix(before, NT, ne)
                then(dve.tensor_copy(load[:, :], full[:, NT - 1, :]))
                then(dve.tensor_tensor(full[:, :, :], full[:, :, :], sums, ALU.subtract))
                then(dve.tensor_tensor(full[:, :, :], full[:, :, :], within, ALU.add))
                dve.nop().then_inc(s_count, 1)
                then(dve.tensor_scalar(texp[:, 0:E], ramp[:, 0:E], float(P), None, ALU.mult))
                then(dve.tensor_tensor(by16[:, :, :], load[:, :].unsqueeze(2).to_broadcast([P, E, E]),
                                       texp[:, 0:E].unsqueeze(1).to_broadcast([P, E, E]), ALU.is_gt))
                then(dve.tensor_reduce(tiles[0][:, :], by16[:, :, :], AX.X, ALU.add))
                then(dve.tensor_scalar(tiles[0][:, :], tiles[0][:, :], 1.0, None, ALU.max))
                then(dve.tensor_copy(load[:, :], tiles[0][:, :]))
                upto = prefix(tiles, E, lambda b: b[:, :].unsqueeze(2))
                then(dve.tensor_scalar(texp[:, :], ramp[:, :], 2.0, upto[:, E - 1:E], ALU.mult, ALU.is_lt))
                then(dve.tensor_reduce(csum[:, 0:1], texp[:, :], AX.X, ALU.add))
                then(dve.tensor_scalar(csum[:, 1:2], csum[:, 0:1], 2.0, -2.0, ALU.mult, ALU.add))
                then(dve.tensor_copy(pair_count[:, :], csum[:, 0:2]))
                then(dve.tensor_tensor(upto[:, :], upto[:, :], load[:, :], ALU.subtract))
                then(dve.tensor_copy(first_tile[:, :], upto[:, :]))
                then(dve.tensor_tensor(byt[:, :, :], ramp[:, :].unsqueeze(2).to_broadcast([P, MAXT, E]),
                                       upto[:, :].unsqueeze(1).to_broadcast([P, MAXT, E]), ALU.is_ge))
                then(dve.tensor_reduce(texp[:, :], byt[:, :, :], AX.X, ALU.add))
                then(dve.tensor_scalar(texp[:, :], texp[:, :], -1.0, None, ALU.add))
                then(dve.tensor_copy(tile_expert[:, :], texp[:, :]))
                then(dve.tensor_scalar(upto[:, :], upto[:, :], float(P), None, ALU.mult))
                then(dve.tensor_tensor(slotf[:, :, :], full[:, :, :], upto[:, :].unsqueeze(1).to_broadcast([P, NT, E]),
                                       ALU.add))
                for k in range(PICK):
                    then(dve.tensor_scalar(cmp[:, :, :], rank[:, :, :], float(k), None, ALU.is_equal))
                    dve.tensor_tensor(choice[:, :, :], cmp[:, :, :], sig[:, :, :], ALU.mult)
                    then(dve.tensor_tensor(picked[:, :, :], cmp[:, :, :], slotf[:, :, :], ALU.mult))
                    dve.tensor_reduce(slot4[:, :, k:k + 1], picked[:, :, :], AX.X, ALU.add)
                    then(dve.tensor_reduce(pick_w[:, :, k:k + 1], choice[:, :, :], AX.X, ALU.add))
                dve.tensor_copy(slots[:, :, :], slot4[:, :, :]).then_inc(s_slots, 1)

                for c in range(NCH):
                    for k in range(KC):
                        dve.wait_ge(s_xhi, c * KC + k + 1)
                        dve.tensor_tensor(xlo[0][:, k, :], bank[k % 2][:, :], xhi[0][:, k, :].bitcast(F32),
                                          ALU.subtract).then_inc(s_xlo, 1)
                    for q in range(NB):
                        n = c * NB + q
                        rows = hb_rows(q % HB)
                        dve.wait_ge(s_silu, n + 1)
                        dve.tensor_tensor(hid[n % 2][0:rows, :], gate[n % 2][0:rows, :], bank[4 + q % 2][0:rows, :],
                                          ALU.mult).then_inc(s_hid, 1)
                        dve.wait_ge(s_hhi, n + 1)
                        dve.tensor_tensor(hlo[0:rows, q, :], hid[n % 2][0:rows, :], hhi[0:rows, q, :].bitcast(F32),
                                          ALU.subtract).then_inc(s_hlo, 1)
                    for i in range(TPC):
                        m = c * TPC + i
                        dve.wait_ge(s_y, m + 1)
                        if m == 0:
                            dve.wait_ge(s_scat, 16 * NT * PICK)
                        dve.tensor_tensor(acc[:, m, :], acc[:, m, :], bank[6 + m % 2][:, :], ALU.add).then_inc(s_sum, 1)


def routed(nc, t, bank, ident, xs, ys, tile_expert, first_tile, pair_count, whi, wlo, sb, sem):
    st = ExitStack()
    with st:
        staged = [sb(f"staged{i}", [P, WCOLS], F32, st) for i in range(2)]
        x = [sb(f"xslot{i}", [P, HID], F32, st) for i in range(2)]
        xhi = [sb(f"xshi{i}", [P, KC, P], F32R, st) for i in range(2)]
        xlo = [sb(f"xslo{i}", [P, KC, P], F32R, st) for i in range(2)]
        gate = [sb(f"sgate{i}", [P, INTER], F32, st) for i in range(2)]
        hid = [sb(f"shid{i}", [P, INTER], F32, st) for i in range(2)]
        hhi = sb("shhi", [P, HB, P], F32R, st)
        hlo = sb("shlo", [P, HB, P], F32R, st)
        y = [sb(f"yslot{i}", [P, HID], F32, st) for i in range(2)]

        st_in = [sem("staged_even", st), sem("staged_odd", st)]
        x_in = [sem("xslot_even", st), sem("xslot_odd", st)]
        y_out = [sem("yslot_even", st), sem("yslot_odd", st)]
        s_hi, s_w, s_xt, s_u1, s_u3, s_ht, s_dn, s_xhi, s_silu, s_hhi, s_y, s_xlo, s_h, s_hlo = (sem(n, st) for n in (
            "w_hi", "w_ready", "m_xt", "m_up1", "m_up3", "m_ht", "m_down", "m_xhi", "m_silu", "m_hhi", "m_y",
            "m_xlo", "m_h", "m_hlo"))
        b_xt, b_ht, b_u1, b_u3, b_dn = bank[0], bank[1], bank[2:4], bank[4:6], bank[6:8]

        def pairs(eng):
            return eng.value_load(pair_count[0:1, 0:1], min_val=E // 2, max_val=(MAXT - 2) // 2)

        def last_pair(eng):
            return eng.value_load(pair_count[0:1, 1:2], min_val=E - 2, max_val=MAXT - 4)

        with nc.Block() as block:
            @block.sync
            def _(sp):
                def row(g):
                    return g * P if isinstance(g, int) else sp.snap(g * P)

                def load(par, g):
                    r = row(g)
                    wait_for(sp, s_xt, g - 1)
                    sp.dma_start(x[par][:, :], xs[bass.ds(r, P), :]).then_inc(x_in[par], 16)

                def store(g, par):
                    r = row(g)
                    sp.wait_ge(s_y, g + 1)
                    sp.dma_start(ys[bass.ds(r, P), :], y[par][:, :]).then_inc(y_out[par], 16)

                n = pairs(sp)
                load(0, 0)
                load(1, 1)
                load(0, 2)
                load(1, 3)
                with sp.Fori(1, n) as i:
                    load(0, i * 2 + 2)
                    store(i * 2 - 2, 0)
                    load(1, i * 2 + 3)
                    store(i * 2 - 1, 1)
                m = last_pair(sp)
                store(m, 0)
                store(m + 1, 1)

            @block.gpsimd
            def _(pool):
                def stage(e, par):
                    src = t["wexp"][e, :, :] if isinstance(e, int) else t["wexp"][bass.ds(e, 1), :, :].rearrange("o p c -> (o p) c")
                    pool.dma_start(staged[par][:, :], src).then_inc(st_in[par], 16)

                def split(e, par, of_kind, free_at):
                    pool.wait_ge(st_in[par], of_kind * 16 + 16)
                    if free_at is not None:
                        pool.wait_ge(s_dn, free_at)
                    pool.tensor_copy(whi[:, par, :], staged[par][:, :]).then_inc(s_hi, 1)
                    pool.wait_ge(s_hi, e + 1)
                    pool.tensor_tensor(wlo[:, par, :], staged[par][:, :], whi[:, par, :].bitcast(F32),
                                       ALU.subtract).then_inc(s_w, 1)

                stage(0, 0)
                stage(1, 1)
                split(0, 0, 0, None)
                pool.wait_ge(s_w, 1)
                stage(2, 0)
                split(1, 1, 0, None)
                pool.wait_ge(s_w, 2)
                stage(3, 1)
                for e in range(2, E):
                    free_at = pool.value_load(first_tile[0:1, e - 1:e], min_val=1, max_val=MAXT)
                    split(e, e % 2, e // 2, free_at)
                    if e + 2 < E:
                        pool.wait_ge(s_w, e + 1)
                        stage(e + 2, e % 2)
                n = pairs(pool)
                for par in range(2):
                    pool.wait_ge(y_out[par], n * 16)
                    pool.wait_ge(x_in[par], n * 16 + 16)

            @block.tensor
            def _(pe):
                def turn(g, par, of_kind):
                    pe.wait_ge(x_in[par], of_kind * 16 + 16)
                    wait_for(pe, s_xlo, g)
                    for k in range(KC):
                        mm = pe.transpose(b_xt[:, k * P:(k + 1) * P], x[par][:, k * P:(k + 1) * P], ident[:, :])
                    mm.then_inc(s_xt, 1)

                def up(g, par, w, at):
                    if w == 0:
                        wait_for(pe, s_silu, g - 1)
                        pe.wait_ge(s_xlo, g + 1)
                    else:
                        wait_for(pe, s_h, g - 1)
                    dst = (b_u1, b_u3)[w][par][:, 0:INTER]
                    for k in range(KC):
                        cols = bass.ds(at + w13_cols(w, k)[0], INTER)
                        mm = three_products(pe, dst, (xhi[par][:, k, :], xlo[par][:, k, :]),
                                            (flat(whi)[:, cols], flat(wlo)[:, cols]), k == 0, k == KC - 1)
                    mm.then_inc((s_u1, s_u3)[w], 1)

                def turn_hidden(g, par):
                    pe.wait_ge(s_h, g + 1)
                    wait_for(pe, s_hlo, g)
                    for b in range(HB):
                        rows = hb_rows(b)
                        mm = pe.transpose(b_ht[0:rows, b * P:(b + 1) * P], hid[par][:, b * P:b * P + rows], ident[:, :])
                    mm.then_inc(s_ht, 1)

                def down(g, par, at):
                    pe.wait_ge(s_hlo, g + 1)
                    wait_for(pe, s_y, g - 1)
                    for b in range(HB):
                        rows = hb_rows(b)
                        cols = bass.ds(at + w2_cols(b)[0], HID)
                        mm = three_products(pe, b_dn[par][:, :], (hhi[0:rows, b, :], hlo[0:rows, b, :]),
                                            (flat(whi)[0:rows, cols], flat(wlo)[0:rows, cols]), b == 0, b == HB - 1)
                    mm.then_inc(s_dn, 1)

                def flat(w):
                    return w[:, :, :].rearrange("p s c -> p (s c)")

                def weights_at(g):
                    cell = tile_expert[0:1, g:g + 1] if isinstance(g, int) else tile_expert[0:1, bass.ds(g, 1)]
                    e = pe.value_load(cell, min_val=0, max_val=E - 1)
                    return e

                def step(g, par, i, first):
                    e = weights_at(g)
                    pe.wait_ge(s_w, e + 1)
                    at = (e % 2) * WCOLS
                    up(g, par, 0, at)
                    if not first:
                        turn_hidden(g - 1, 1 - par)
                    up(g, par, 1, at)
                    turn(g + 1, 1 - par, i + par)
                    if not first:
                        down(g - 1, 1 - par, (weights_at(g - 1) % 2) * WCOLS)

                n = pairs(pe)
                turn(0, 0, 0)
                step(0, 0, 0, True)
                step(1, 1, 0, False)
                with pe.Fori(1, n) as i:
                    step(i * 2, 0, i, False)
                    step(i * 2 + 1, 1, i, False)
                m = last_pair(pe)
                turn_hidden(m + 1, 1)
                down(m + 1, 1, (weights_at(m + 1) % 2) * WCOLS)

            @block.scalar
            def _(act):
                def x_high(g, par):
                    act.wait_ge(s_xt, g + 1)
                    act.copy(xhi[par][:, :, :], b_xt[:, :].rearrange("p (k t) -> p k t", k=KC)).then_inc(s_xhi, 1)

                def silu(g, par):
                    act.wait_ge(s_u1, g + 1)
                    act.activation(gate[par][:, :], b_u1[par][:, 0:INTER], ACT.Silu).then_inc(s_silu, 1)

                def h_high(g):
                    act.wait_ge(s_ht, g + 1)
                    act.copy(hhi[:, 0:2, :], b_ht[:, 0:2 * P].rearrange("p (b t) -> p b t", b=2))
                    rows = hb_rows(2)
                    act.copy(hhi[0:rows, 2, :], b_ht[0:rows, 2 * P:3 * P]).then_inc(s_hhi, 1)

                def y_copy(g, par, of_kind):
                    act.wait_ge(s_dn, g + 1)
                    wait_for(act, y_out[par], of_kind * 16)
                    act.copy(y[par][:, :], b_dn[par][:, :]).then_inc(s_y, 1)

                def step(g, par, i, first):
                    silu(g, par)
                    if not first:
                        h_high(g - 1)
                    x_high(g + 1, 1 - par)
                    if not first:
                        y_copy(g - 1, 1 - par, i if par else i - 1)

                n = pairs(act)
                x_high(0, 0)
                step(0, 0, 0, True)
                step(1, 1, 0, False)
                with act.Fori(1, n) as i:
                    step(i * 2, 0, i, False)
                    step(i * 2 + 1, 1, i, False)
                m = last_pair(act)
                h_high(m + 1)
                act.wait_ge(s_dn, m + 2)
                act.wait_ge(y_out[1], m * 8)
                act.copy(y[1][:, :], b_dn[1][:, :]).then_inc(s_y, 1)

            @block.vector
            def _(dve):
                def x_low(g, par):
                    dve.wait_ge(s_xhi, g + 1)
                    dve.tensor_tensor(xlo[par][:, :, :], b_xt[:, :].rearrange("p (k t) -> p k t", k=KC),
                                      xhi[par][:, :, :].bitcast(F32), ALU.subtract).then_inc(s_xlo, 1)

                def hidden(g, par):
                    dve.wait_ge(s_silu, g + 1)
                    dve.wait_ge(s_u3, g + 1)
                    dve.tensor_tensor(hid[par][:, :], gate[par][:, :], b_u3[par][:, 0:INTER], ALU.mult).then_inc(s_h, 1)

                def h_low(g):
                    dve.wait_ge(s_hhi, g + 1)
                    dve.tensor_tensor(hlo[:, 0:2, :], b_ht[:, 0:2 * P].rearrange("p (b t) -> p b t", b=2),
                                      hhi[:, 0:2, :].bitcast(F32), ALU.subtract)
                    rows = hb_rows(2)
                    dve.tensor_tensor(hlo[0:rows, 2, :], b_ht[0:rows, 2 * P:3 * P],
                                      hhi[0:rows, 2, :].bitcast(F32), ALU.subtract).then_inc(s_hlo, 1)

                def step(g, par, first):
                    if not first:
                        h_low(g - 1)
                    hidden(g, par)
                    x_low(g + 1, 1 - par)

                n = pairs(dve)
                x_low(0, 0)
                step(0, 0, True)
                step(1, 1, False)
                with dve.Fori(1, n) as i:
                    step(i * 2, 0, False)
                    step(i * 2 + 1, 1, False)
                h_low(last_pair(dve) + 1)


def combine(nc, t, acc, ys, slots, pick_w, mv, rstd, neghalf, stats, sb, sem):
    st = ExitStack()
    with st:
        got = [sb(f"got{i}", [P, PICK, HID], F32, st) for i in range(4)]
        s_got = [sem(f"got{i}", st) for i in range(4)]
        s_sum, s_st, s_mv, s_eps, s_pow, s_done, s_store = (sem(x, st) for x in (
            "ln2_sum", "ln2_stats", "ln2_mv", "ln2_eps", "ln2_pow", "ln2_done", "ln2_store"))
        with nc.Block() as block:
            @block.gpsimd
            def _(pool):
                def gather(n):
                    if n >= 4:
                        pool.wait_ge(s_sum, PICK * (n - 3))
                    for k in range(PICK):
                        pool.indirect_dma_start(got[n % 4][:, k, :], None, ys[:, :],
                                                bass.IndirectOffsetOnAxis(ap=slots[:, n, k:k + 1], axis=0),
                                                bounds_check=MAXT * P - 1, oob_is_err=False).then_inc(s_got[n % 4], 16)

                for n in range(3):
                    gather(n)
                for n in range(NT):
                    if n + 3 < NT:
                        gather(n + 3)
                    pool.wait_ge(s_eps, n + 1)
                    pool.tensor_tensor(rstd[:, n:n + 1], rstd[:, n:n + 1], neghalf[:, 0:1], ALU.pow).then_inc(s_pow, 1)

            @block.vector
            def _(dve):
                def normed(n):
                    dve.wait_ge(s_pow, n + 1)
                    dve.tensor_scalar(acc[:, n, :], acc[:, n, :], mv[:, n, 0:1], rstd[:, n:n + 1],
                                      ALU.subtract, ALU.mult).then_inc(s_done, 1)

                for n in range(NT):
                    dve.wait_ge(s_got[n % 4], 16 * PICK * (n // 4 + 1))
                    for k in range(PICK):
                        if k:
                            dve.wait_ge(s_sum, PICK * n + k)
                        dve.scalar_tensor_tensor(acc[:, n, :], got[n % 4][:, k, :], pick_w[:, n, k:k + 1],
                                                 acc[:, n, :], ALU.mult, ALU.add).then_inc(s_sum, 1)
                    dve.wait_ge(s_sum, PICK * (n + 1))
                    dve.bn_stats(stats[:, n % 2, :], acc[:, n, :]).then_inc(s_st, 1)
                    dve.wait_ge(s_st, n + 1)
                    dve.bn_aggr(mv[:, n, :], stats[:, n % 2, :]).then_inc(s_mv, 1)
                    dve.wait_ge(s_mv, n + 1)
                    dve.tensor_scalar(rstd[:, n:n + 1], mv[:, n, 1:2], LN_EPS, None, ALU.add).then_inc(s_eps, 1)
                    if n:
                        normed(n - 1)
                normed(NT - 1)

            @block.sync
            def _(sp):
                for n in range(NT):
                    sp.wait_ge(s_done, n + 1)
                    sp.dma_start(t["out"][n * P:(n + 1) * P, :], acc[:, n, :]).then_inc(s_store, 16)
                sp.wait_ge(s_store, 16 * NT)


def kernel(**inputs):
    import concourse.bacc as bacc
    from concourse.bass_utils import run_bass_kernel_spmd as run

    a = {n.replace("L0_attn_", "").replace("L0_ffn_", "f_"): np.ascontiguousarray(x) for n, x in inputs.items()}
    x = a["hidden_states"][0]
    def by_head(w):
        return w.reshape(KC, P, NH, D).transpose(2, 1, 0, 3).reshape(NH, P, KC * D)
    wh = np.concatenate([
        by_head(a["Wq"]), by_head(a["Wlk"]), by_head(a["Wlv"]),
        a["bq"].reshape(NH, D, 1), a["blk"].reshape(NH, D, 1),
        np.broadcast_to(a["blv"].reshape(NH, 1, D), (NH, P, D)),
    ], axis=2)
    sh = NSH * INTER
    w1 = np.concatenate([a["f_w1"], a["f_sw1"].reshape(HID, NSH, INTER).transpose(1, 0, 2)])
    w3 = np.concatenate([a["f_w3"], a["f_sw3"].reshape(HID, NSH, INTER).transpose(1, 0, 2)])
    w2 = np.concatenate([a["f_w2"], a["f_sw2"].reshape(NSH, INTER, HID)])
    ne = E + NSH
    w2 = np.concatenate([w2, np.zeros((ne, HB * P - INTER, HID), np.float32)], axis=1)
    w13 = np.stack([w1, w3], axis=1).reshape(ne, 2, KC, P, INTER).transpose(0, 3, 1, 2, 4).reshape(ne, P, -1)
    wexp = np.concatenate([w13, w2.reshape(ne, HB, P, HID).transpose(0, 2, 1, 3).reshape(ne, P, -1)], axis=2)
    inv = np.float32(1.0) / np.float32(10000.0) ** (np.arange(ROT, dtype=np.float32) * np.float32(2.0 / (2 * ROT)))
    ang = np.arange(S, dtype=np.float32)[None, :] * inv.astype(np.float32)[:, None]
    cos, sin = np.cos(ang).astype(np.float32), np.sin(ang).astype(np.float32)
    cos_t = np.concatenate([cos, cos, np.ones((P - 2 * ROT, S), np.float32)])
    sin_t = np.concatenate([sin, -sin])
    q, k = np.arange(P)[:, None], np.arange(2 * P)[None, :]
    rel = q + P - k
    band = np.where((rel >= 0) & (rel <= P), 0.0, NEG).astype(np.float32)
    diag = np.where(np.arange(EPT)[None, :] * RATIO + RATIO - 1 <= q, 0.0, NEG).astype(np.float32)
    arrays = {
        "x": x, "xT": x.T, "Wcmp": a["Wcmp"].reshape(KC, P).T, "bcmp": a["bcmp"].reshape(1, 1), "Wk": a["Wk"], "Wv": a["Wv"],
        "norm_w": np.stack([a["kn_w"], a["qn_w"]], axis=1), "bk": a["bk"].reshape(D, 1), "bv": a["bv"].reshape(1, D),
        "bo": a["bo"].reshape(1, HID), "wh": wh, "Wo": a["Wo"], "gateT": a["f_gate_w"].T,
        "ebias": a["f_expert_bias"].reshape(1, E), "wexp": wexp,
        "tri": np.stack([np.triu(np.ones((P, P), np.float32), 1), np.ones((P, P), np.float32)], axis=1),
        "ramp": np.arange(MAXT, dtype=np.float32).reshape(1, MAXT),
        "ident": np.eye(P, dtype=np.float32), "cos": cos_t, "sin": sin_t, "band": band, "diag": diag,
    }
    arrays = {n: np.ascontiguousarray(v) for n, v in arrays.items()}
    nc = bacc.Bacc("TRN2", target_bir_lowering=False, num_devices=1)
    t = {n: nc.dram_tensor(f"in_{n}", v.shape, F32, kind="ExternalInput").ap() for n, v in arrays.items()}
    out = nc.dram_tensor("out", [1, S, HID], F32, kind="ExternalOutput").ap()
    t["out"] = out[0, :, :]
    build(nc, t)
    r = run(nc, [{f"in_{n}": v for n, v in arrays.items()}], core_ids=[0])
    return r.results[0]["out"]
```

```python
from contextlib import ExitStack

import numpy as np

import concourse.bass as bass
from concourse import mybir

F32 = mybir.dt.float32
F32R = mybir.dt.float32r
BF16 = mybir.dt.bfloat16
I32 = mybir.dt.int32
U32 = mybir.dt.uint32
ALU = mybir.AluOpType
ACT = mybir.ActivationFunctionType
AX = mybir.AxisListType

P = 128
S = 2048
HID = 512
KC = HID // P
NH = 16
D = 128
NT = S // P
RATIO = 4
C = S // RATIO
CB = C // P
EPT = P // RATIO
TOPK = 8
ROT = D // 4
CH = 512
NCH = S // CH
TPC = CH // P
EPS = 1e-6
LN_EPS = 1e-5
NEG = -1e30
FLOOR = -1e29
TAKEN = 3e38
INTER = 352
HB = 3
E = 16
NSH = 2
EG = 4
G = E // EG
PICK = 4
PICK_G = 2
MAXT = PICK * NT + E + 2
EARLY = NCH - 1
RING = 3
WCOLS = 2 * KC * INTER + HB * HID
HEAD_COLS = 3 * KC * D + 2 + D


def hb_rows(b):
    return min(P, INTER - b * P)


def wait_for(eng, sem, count):
    if isinstance(count, int) and count <= 0:
        return
    eng.wait_ge(sem, count)


def build(nc, t):
    ctx = ExitStack()
    with ctx:
        def sb(name, shape, dt=F32, stack=ctx):
            return stack.enter_context(nc.sbuf_tensor(name, shape, dt))

        def sem(name, stack=ctx):
            return stack.enter_context(nc.semaphore(name))

        bank = [ctx.enter_context(nc.psum_tensor(f"bank{i}", [P, CH], F32)) for i in range(8)]

        acc = sb("acc", [P, NT, HID])
        ident = sb("ident", [P, P])

        xs = nc.dram_tensor("slots_in", [MAXT * P, HID], F32, kind="Internal").ap()
        ys = nc.dram_tensor("slots_out", [MAXT * P, HID], F32, kind="Internal").ap()
        zero_sem = sem("slots_zeroed")
        zero_count = 16 * (MAXT // 2 + (MAXT - PICK * NT) // 2)

        att = ExitStack()
        with att:
            xT = sb("xT", [P, KC, S], F32, att)
            attention(nc, t, bank, xT, acc, ident, (xs, ys), zero_sem, zero_count,
                      lambda n, s, d=F32: sb(n, s, d, att), lambda n: sem(n, att), sb)
        feed_forward(nc, t, bank, acc, ident, xs, ys, [(zero_sem, zero_count)],
                     sb, sem)


def attention(nc, t, bank, xT, acc, ident, slots_dram, zero_sem, zero_count, sb, sem, sb_for):
    cosk = sb("cosk", [P, S])
    cosq = sb("cosq", [P, S])
    sin = sb("sin", [P, S])
    norm_w = sb("norm_w", [P, 3])
    ckT = sb("ckT", [P, C])
    cv = sb("cv", [P, CB, D])
    half = sb("half", [P, NT])
    band = sb("band", [P, 2 * P])
    diag = sb("diag", [P, EPT], BF16)
    identb = sb("identb", [P, P], BF16)
    ones = sb("ones", [P, P])
    wh = [sb(f"wh{i}", [P, HEAD_COLS]) for i in range(2)]
    w_in = [sem("w_in_even"), sem("w_in_odd")]

    s1 = ExitStack()
    with s1:
        compress(nc, t, bank, xT, acc, ident, ones, half, band, diag, identb, cosk, cosq, sin,
                 norm_w, ckT, cv, wh, w_in, lambda n, s, d=F32: sb_for(n, s, d, s1),
                 lambda n: s1.enter_context(nc.semaphore(n)))

    heads(nc, t, bank, xT, acc, ident, slots_dram, zero_sem, zero_count, ones, half, band, diag, identb, cosk, cosq, sin,
          ckT, cv, wh, w_in, sb, sem)


def compress(nc, t, bank, xT, acc, ident, ones, half, band, diag, identb, cosk, cosq, sin,
             norm_w, ckT, cv, wh, w_in, sb, sem):
    wcmp = sb("wcmp", [P, HID])
    product = sb("product", [P, 2, HID])
    sel = sb("sel", [P, TPC, P])
    bcmp = sb("bcmp", [P, 1])
    wk = sb("wk", [P, KC, D])
    wv = sb("wv", [P, KC, D])
    bk = sb("bk", [P, 1])
    bv = sb("bv", [P, D])
    bo = sb("bo", [P, HID])
    logit = sb("logit", [P, NT])
    by_tile = sb("by_tile", [NT, P])
    gmax = sb("gmax", [NT, EPT])
    gsum = sb("gsum", [NT, EPT])
    spread = sb("spread", [P, NT, P])
    rows = sb("entries", [P, CB, HID])
    entT = sb("entT", [P, KC, C])
    square = sb("square", [P, C])
    ms = sb("ms", [P, CB])
    rstd = sb("rstd", [P, CB])
    turned = sb("turned", [2 * ROT, C])
    diag32 = sb("diag32", [P, EPT])
    POOL_TILES = 6

    x_in = [sem(f"x_in{c}") for c in range(NCH)]
    cmp_in, c_in, k_in, tab_in, r_in = (sem(n) for n in ("cmp_in", "c_in", "k_in", "tab_in", "r_in"))
    xturn, xcopy = sem("x_turned"), sem("xT_copied")
    logits, wstep, wexp, wturn, wspread, ent, ent_act, ent_dve = (sem(n) for n in (
        "logits", "softmax_step", "softmax_exp", "weights_turned", "weights_spread", "entries",
        "entT_by_act", "entT_by_dve"))
    step, kproj, ksq, kssq, kms, krstd, vproj = (
        sem(n) for n in ("step", "kproj", "ksq", "kssq", "kms", "krstd", "vproj"))
    ent_rows, ent_turned = sem("entries_copied"), sem("entries_turned")
    b_bytile, b_weight = bank[5], bank[6]

    with nc.Block() as block:
        @block.sync
        def _(sp):
            for c in range(NCH):
                sp.dma_start(acc[:, c * TPC:(c + 1) * TPC, :],
                             t["x"][c * CH:(c + 1) * CH, :].rearrange("(n p) d -> p n d", p=P)).then_inc(x_in[c], 16)
            sp.dma_start(wk[:, :, :], t["Wk"].rearrange("(k p) d -> p k d", p=P)).then_inc(k_in, 16)
            sp.dma_start(wv[:, :, :], t["Wv"].rearrange("(k p) d -> p k d", p=P)).then_inc(k_in, 16)
            sp.dma_start(cosk[:, :], t["cos"]).then_inc(tab_in, 16)
            sp.dma_start(sin[:, :], t["sin"]).then_inc(tab_in, 16)
            sp.dma_start(bo[:, :], t["bo"].broadcast_to([P, HID])).then_inc(r_in, 16)
            for h in range(2):
                sp.dma_start(wh[h][:, :], t["wh"][h, :, :]).then_inc(w_in[h], 16)

        @block.scalar
        def _(act):
            act.dma_start(ident[:, :], t["ident"]).then_inc(cmp_in, 16)
            act.dma_start(wcmp[:, :], t["Wcmp"].broadcast_to([P, HID])).then_inc(cmp_in, 16)
            act.dma_start(bcmp[:, :], t["bcmp"].broadcast_to([P, 1])).then_inc(cmp_in, 16)
            act.dma_start(norm_w[:, :], t["norm_w"]).then_inc(c_in, 16)
            act.dma_start(bk[:, :], t["bk"]).then_inc(c_in, 16)
            act.dma_start(bv[:, :], t["bv"].broadcast_to([P, D])).then_inc(c_in, 16)
            act.dma_start(sel[:, :, :], t["sel"]).then_inc(c_in, 16)
            act.dma_start(band[:, :], t["band"]).then_inc(c_in, 16)
            act.dma_start(diag32[:, :], t["diag"]).then_inc(c_in, 16)
            for c in range(NCH):
                for k in range(KC):
                    act.wait_ge(xturn, c * KC + k + 1)
                    act.copy(xT[:, k, c * CH:(c + 1) * CH], bank[k][:, :]).then_inc(xcopy, 1)
            act.wait_ge(wstep, 4)
            act.activation(by_tile[:, :], by_tile[:, :], ACT.Exp).then_inc(wexp, 1)
            for b in range(CB):
                act.wait_ge(ent, b + 1)
                act.copy(rows[:, b, :], bank[b][:, :]).then_inc(ent_rows, 1)
            for k in range(0, KC, 2):
                act.wait_ge(ent_turned, k + 1)
                act.copy(entT[:, k, :], bank[k][:, :]).then_inc(ent_act, 1)
            act.wait_ge(c_in, 16 * 6)
            act.wait_ge(kproj, 1)
            act.activation(square[:, :], bank[4][:, :], ACT.Square, bias=bk[:, 0:1]).then_inc(ksq, 1)

        @block.tensor
        def _(pe):
            def turn(c):
                pe.wait_ge(x_in[c], 16)
                for k in range(KC):
                    wait_for(pe, xcopy, (c - 1) * KC + k + 1)
                    for i in range(TPC):
                        mm = pe.transpose(bank[k][:, i * P:(i + 1) * P], acc[:, c * TPC + i, k * P:(k + 1) * P],
                                          ident[:, :])
                    mm.then_inc(xturn, 1)

            pe.wait_ge(cmp_in, 48)
            for c in range(NCH):
                turn(c)
            pe.wait_ge(wstep, 1)
            pe.transpose(b_bytile[0:NT, 0:P], logit[:, :], ident[:, :]).then_inc(wturn, 1)
            pe.wait_ge(wstep, 7)
            pe.transpose(b_weight[:, 0:NT], by_tile[:, :], ident[0:NT, 0:NT]).then_inc(wturn, 1)
            pe.wait_ge(xcopy, NCH * KC)
            for b in range(CB):
                pe.wait_ge(wspread, b + 1)
                for j in range(TPC):
                    n = b * TPC + j
                    mm = pe.matmul(bank[b][:, :], spread[:, n, :], acc[:, n, :], start=(j == 0), stop=(j == TPC - 1))
                mm.then_inc(ent, 1)
            pe.wait_ge(ent_rows, CB)
            for k in range(KC):
                for b in range(CB):
                    mm = pe.transpose(bank[k][:, b * P:(b + 1) * P], rows[:, b, k * P:(k + 1) * P], ident[:, :])
                mm.then_inc(ent_turned, 1)
            pe.wait_ge(k_in, 32)
            pe.wait_ge(ent_act, KC // 2)
            pe.wait_ge(ent_dve, KC // 2)
            for k in range(KC):
                mm = pe.matmul(bank[4][:, :], wk[:, k, :], entT[:, k, :], start=(k == 0), stop=(k == KC - 1))
            mm.then_inc(kproj, 1)
            for b in range(CB):
                for k in range(KC):
                    mm = pe.matmul(bank[5][:, b * D:(b + 1) * D], entT[:, k, b * P:(b + 1) * P], wv[:, k, :],
                                   start=(k == 0), stop=(k == KC - 1))
            mm.then_inc(vproj, 1)
            pe.wait_ge(ksq, 1)
            for b in range(CB):
                mm = pe.matmul(bank[6][:, b:b + 1], square[:, b * P:(b + 1) * P], ones[:, 0:1], start=True, stop=True)
            mm.then_inc(kssq, 1)
            pe.wait_ge(krstd, 2)
            for b in range(CB):
                mm = pe.transpose(bank[7][:, b * P:(b + 1) * P], rstd[:, b:b + 1].to_broadcast([P, P]), ident[:, :])
            mm.then_inc(kssq, 1)

        @block.gpsimd
        def _(pool):
            pool.memset(half[:, :], -0.5).then_inc(krstd, 1)
            pool.wait_ge(ent, CB)
            pool.wait_ge(r_in, 16)
            pool.tensor_tensor(acc[:, 0:POOL_TILES, :], acc[:, 0:POOL_TILES, :],
                               bo[:, :].unsqueeze(1).to_broadcast([P, POOL_TILES, HID]), ALU.add)
            pool.wait_ge(kms, 1)
            pool.wait_ge(krstd, 1)
            pool.tensor_tensor(rstd[:, :], ms[:, :], half[:, 0:CB], ALU.pow).then_inc(krstd, 1)

        @block.vector
        def _(dve):
            dve.memset(ones[:, :], 1.0)
            dve.wait_ge(cmp_in, 48)
            for n in range(NT):
                if n % TPC == 0:
                    dve.wait_ge(x_in[n // TPC], 16)
                wait_for(dve, logits, n - 1)
                dve.scalar_tensor_tensor(product[:, n % 2, :], acc[:, n, :], 1.0, wcmp[:, :], ALU.mult, ALU.mult,
                                         accum_out=logit[:, n:n + 1]).then_inc(logits, 1)
            dve.wait_ge(logits, NT)
            dve.tensor_scalar(logit[:, :], logit[:, :], bcmp[:, 0:1], None, ALU.add).then_inc(wstep, 1)
            dve.wait_ge(wturn, 1)
            dve.tensor_copy(by_tile[:, :], b_bytile[0:NT, 0:P]).then_inc(wstep, 1)
            dve.wait_ge(wstep, 2)
            w4 = by_tile[:, :].rearrange("n (c r) -> n c r", r=RATIO)
            dve.tensor_reduce(gmax[:, :], w4, AX.X, ALU.max).then_inc(wstep, 1)
            dve.wait_ge(wstep, 3)
            dve.tensor_tensor(w4, w4, gmax[:, :].unsqueeze(2).to_broadcast([NT, EPT, RATIO]), ALU.subtract).then_inc(wstep, 1)
            dve.wait_ge(wexp, 1)
            dve.tensor_reduce(gsum[:, :], w4, AX.X, ALU.add).then_inc(wstep, 1)
            dve.wait_ge(wstep, 5)
            dve.reciprocal(gsum[:, :], gsum[:, :]).then_inc(wstep, 1)
            dve.wait_ge(wstep, 6)
            dve.tensor_tensor(w4, w4, gsum[:, :].unsqueeze(2).to_broadcast([NT, EPT, RATIO]), ALU.mult).then_inc(wstep, 1)
            dve.wait_ge(c_in, 16 * 6)
            dve.wait_ge(wturn, 2)
            for b in range(CB):
                tiles = slice(b * TPC, (b + 1) * TPC)
                dve.tensor_tensor(spread[:, tiles, :], b_weight[:, tiles].unsqueeze(2).to_broadcast([P, TPC, P]),
                                  sel[:, :, :], ALU.mult).then_inc(wspread, 1)
            dve.wait_ge(tab_in, 32)
            dve.tensor_copy(identb[:, :], ident[:, :])
            dve.tensor_copy(diag[:, :], diag32[:, :])
            dve.tensor_scalar(cosq[:, :], cosk[:, :], norm_w[:, 1:2], None, ALU.mult).then_inc(step, 1)
            dve.tensor_scalar(sin[:, :], sin[:, :], norm_w[:, 2:3], None, ALU.mult).then_inc(step, 1)
            dve.wait_ge(step, 1)
            dve.tensor_scalar(cosk[:, :], cosk[:, :], norm_w[:, 0:1], None, ALU.mult).then_inc(step, 1)
            for k in range(1, KC, 2):
                dve.wait_ge(ent_turned, k + 1)
                dve.tensor_copy(entT[:, k, :], bank[k][:, :]).then_inc(ent_dve, 1)
            dve.wait_ge(r_in, 16)
            dve.tensor_tensor(acc[:, POOL_TILES:NT, :], acc[:, POOL_TILES:NT, :],
                              bo[:, :].unsqueeze(1).to_broadcast([P, NT - POOL_TILES, HID]), ALU.add)
            dve.wait_ge(step, 3)
            dve.wait_ge(kproj, 1)
            dve.wait_ge(ksq, 1)
            ends = slice(RATIO - 1, S, RATIO)
            dve.scalar_tensor_tensor(turned[0:ROT, :], bank[4][ROT:2 * ROT, :], bk[ROT:2 * ROT, 0:1],
                                     sin[ROT:2 * ROT, ends], ALU.add, ALU.mult)
            dve.scalar_tensor_tensor(turned[ROT:2 * ROT, :], bank[4][0:ROT, :], bk[0:ROT, 0:1],
                                     sin[0:ROT, ends], ALU.add, ALU.mult).then_inc(step, 1)
            dve.scalar_tensor_tensor(ckT[:, :], bank[4][:, :], bk[:, 0:1], cosk[:, ends],
                                     ALU.add, ALU.mult).then_inc(step, 1)
            dve.wait_ge(step, 5)
            dve.tensor_tensor(ckT[0:2 * ROT, :], ckT[0:2 * ROT, :], turned[:, :], ALU.add).then_inc(step, 1)
            dve.wait_ge(kssq, 1)
            dve.tensor_scalar(ms[:, :], bank[6][:, 0:CB], 1.0 / D, EPS, ALU.mult, ALU.add).then_inc(kms, 1)
            dve.wait_ge(kssq, 2)
            dve.wait_ge(step, 6)
            dve.tensor_tensor(ckT[:, :], ckT[:, :], bank[7][:, :], ALU.mult)
            dve.wait_ge(vproj, 1)
            dve.tensor_tensor(cv[:, :, :], bank[5][:, :].rearrange("p (b d) -> p b d", b=CB),
                              bv[:, :].unsqueeze(1).to_broadcast([P, CB, D]), ALU.add)


def heads(nc, t, bank, xT, acc, ident, slots_dram, zero_sem, zero_count, ones, half, band, diag, identb, cosk, cosq, sin,
          ckT, cv, wh, w_in, sb, sem):
    wo = sb("wo", [P, 2, HID])
    wo_hi = sb("wo_hi", [P, 2, HID], F32R)
    wo_lo = sb("wo_lo", [P, 2, HID], F32R)
    kT = [sb(f"kT{i}", [P, S]) for i in range(2)]
    qT = [sb(f"qT{i}", [P, S]) for i in range(2)]
    v = [sb(f"v{i}", [P, NT, D]) for i in range(2)]
    turned = [sb(f"turned{i}", [2 * ROT, CH]) for i in range(2)]
    square = [sb(f"square{i}", [P, CH]) for i in range(2)]
    kms = sb("kms", [P, NT])
    qms = sb("qms", [P, NT])
    krstd = [sb(f"krstd{i}", [P, NT]) for i in range(2)]
    qfac = [sb(f"qfac{i}", [P, NT]) for i in range(2)]
    nfac = [sb(f"nfac{i}", [P, NT]) for i in range(2)]
    top = [sb(f"top{i}", [P, TOPK + 1]) for i in range(2)]
    nbias = [sb(f"nbias{i}", [P, 2]) for i in range(2)]
    total = [sb(f"total{i}", [P, 2]) for i in range(2)]
    share = [sb(f"share{i}", [P, 2]) for i in range(2)]
    taken = sb("taken", [P, C])
    prob = [sb(f"prob{i}", [P, C + 2 * P]) for i in range(2)]
    probT = sb("probT", [P, C + 2 * P])
    even_hi = sb("even_hi", [P, S], F32R)
    even_lo = sb("even_lo", [P, S], F32R)
    odd_hi = sb("odd_hi", [P, 2, P], F32R)
    odd_lo = sb("odd_lo", [P, 2, P], F32R)

    b_score, b_local, b_turn_s, b_turn_l, b_unit, b_ctx, b_out = (
        bank[0], bank[1], bank[2], bank[3], (bank[4], bank[5]), bank[6], bank[7])
    SSQ = 2 * P

    zeros = wo[:, :, :].rearrange("p a n -> p (a n)")
    xs, ys = slots_dram
    s_zero = sem("zeros_made")
    wo_in = sem("wo_in")
    s_scores = sem("scores_done")
    s_ssq = sem("ssq_done")
    s_turn = sem("turn_done")
    s_unit = sem("unit_done")
    s_ctx = sem("ctx_done")
    s_out = sem("out_done")
    s_top = sem("top_done")
    s_bias = sem("bias_done")
    s_taken = sem("taken_done")
    s_total = sem("total_done")
    s_share = sem("share_done")
    s_uvec = sem("unit_vector")
    s_ms = sem("ms_done")
    s_nfac = sem("nfac_done")
    s_acc = sem("acc_done")
    s_exp = sem("exp_done")
    s_probT = sem("probT_done")
    s_square = sem("square_done")
    s_ctxc = sem("ctx_high")
    s_ctxl = sem("ctx_low")
    s_woh = sem("wo_high")
    s_wol = sem("wo_low")
    s_prob = sem("prob_done")
    s_rope = sem("rope_done")
    s_rstd = sem("rstd_done")

    def weight(par, which, k):
        return wh[par][:, (which * KC + k) * D:(which * KC + k + 1) * D]

    def bias_col(par, which, rows=slice(0, P)):
        col = 3 * KC * D + which
        return wh[par][rows, col:col + 1]

    def blocks(tile):
        return tile // TPC + 1

    def width(tile):
        return EPT * (tile + 1)

    def local_cols(tile):
        return slice(0 if tile else P, 2 * P)

    def chunk(c):
        return slice(c * CH, (c + 1) * CH)

    def value_tiles(u):
        return range((u - 8) * 2, (u - 7) * 2)

    def ctx_half(even, odd, par, tile):
        return odd[:, tile % 2, :] if par else even[:, tile * P:(tile + 1) * P]

    def pe_unit(pe, h, par, u, of_kind):
        n = h * 16 + u
        dst = b_unit[u % 2]
        if u == 0:
            pe.wait_ge(w_in[par], of_kind * 16 + 16)
        wait_for(pe, s_uvec, n - 1)
        if u < 8:
            which, c = (1, u) if u < 4 else (0, u - 4)
            for k in range(KC):
                mm = pe.matmul(dst[:, :], weight(par, which, k), xT[:, k, chunk(c)],
                               start=(k == 0), stop=(k == KC - 1))
        else:
            if u == 8:
                pe.wait_ge(s_rstd, h * 2 + 1)
            for i, tile in enumerate(value_tiles(u)):
                for k in range(KC):
                    pe.matmul(dst[:, i * D:(i + 1) * D], xT[:, k, tile * P:(tile + 1) * P],
                              weight(par, 2, k), start=(k == 0), stop=(k == KC - 1))
                mm = pe.transpose(dst[:, (2 + i) * P:(3 + i) * P],
                                  krstd[par][:, tile:tile + 1].to_broadcast([P, P]), ident[:, :])
        mm.then_inc(s_unit, 1)

    def pe_ssq(pe, h, u):
        pe.wait_ge(s_square, h * 8 + (u + 1))
        for i in range(TPC):
            col = SSQ + TPC * u + i
            mm = pe.matmul(b_local[:, col:col + 1], square[u % 2][:, i * P:(i + 1) * P], ones[:, 0:1],
                           start=True, stop=True)
        if u % 4 == 3:
            mm.then_inc(s_ssq, 1)

    def pe_scores(pe, n, h, par, tile):
        if tile == 0:
            pe.wait_ge(s_uvec, n + 16)
            pe.wait_ge(s_rope, h * 8 + 8)
        w = width(tile)
        q = qT[par][:, tile * P:(tile + 1) * P]
        pe.matmul(b_score[:, 0:w], q, ckT[:, 0:w], start=True, stop=False)
        pe.matmul(b_score[:, w - EPT:w], identb[:, :], diag[:, :], start=False, stop=True)
        pe.matmul(b_local[:, local_cols(tile)], q, kT[par][:, max(tile - 1, 0) * P:(tile + 1) * P],
                  start=True, stop=True).then_inc(s_scores, 1)

    def pe_turn(pe, n, tile):
        pe.wait_ge(s_prob, n + 1)
        wait_for(pe, s_probT, n)
        pr = prob[tile % 2]
        for b in range(blocks(tile)):
            pe.transpose(b_turn_s[:, b * P:(b + 1) * P], pr[:, b * P:(b + 1) * P], ident[:, :])
        for b in ((0, 1) if tile else (1,)):
            mm = pe.transpose(b_turn_l[:, b * P:(b + 1) * P], pr[:, C + b * P:C + (b + 1) * P], ident[:, :])
        mm.then_inc(s_turn, 1)

    def pe_context(pe, n, par, tile):
        pe.wait_ge(s_probT, n + 1)
        wait_for(pe, s_ctxl, n)
        parts = [(cv[:, b, :], probT[:, b * P:(b + 1) * P]) for b in range(blocks(tile))]
        if tile:
            parts.append((v[par][:, tile - 1, :], probT[:, C:C + P]))
        parts.append((v[par][:, tile, :], probT[:, C + P:C + 2 * P]))
        for m, (val, pt) in enumerate(parts):
            mm = pe.matmul(b_ctx[:, 0:P], val, pt, start=(m == 0), stop=(m == len(parts) - 1))
        mm.then_inc(s_ctx, 1)

    def pe_out(pe, i, n, tile):
        if tile == 0:
            pe.wait_ge(s_wol, i + 1)
        pe.wait_ge(s_ctxl, n + 1)
        wait_for(pe, s_acc, i * 16 + tile)
        cols = slice(tile * P, (tile + 1) * P)
        three_products(pe, b_out[:, :], (even_hi[:, cols], even_lo[:, cols]), (wo_hi[:, 0, :], wo_lo[:, 0, :]),
                       True, False)
        three_products(pe, b_out[:, :], (odd_hi[:, tile % 2, :], odd_lo[:, tile % 2, :]),
                       (wo_hi[:, 1, :], wo_lo[:, 1, :]), False, True).then_inc(s_out, 1)

    def pe_pair(pe, i, first=False, last=False):
        for j in range(2 * NT):
            n, par, tile = i * 32 + j, j // NT, j % NT
            nxt = i * 2 + (par + 1)
            units = not (last and par == 1)
            wait_for(pe, s_taken, n)
            wait_for(pe, s_exp, n)
            if units and 1 <= tile <= 8:
                pe_ssq(pe, nxt, tile - 1)
            pe_scores(pe, n, i * 2 + par, par, tile)
            if j or not first:
                pe_turn(pe, n - 1, (tile - 1) % NT)
            if units:
                pe_unit(pe, nxt, 1 - par, tile, i + par)
            if j >= NT + 2:
                pe_out(pe, i, n - 2, tile - 2)
            elif j < 2 and not first:
                pe_out(pe, i - 1, n - 2, NT - 2 + j)
            if j or not first:
                pe_context(pe, n - 1, par if tile else 1 - par, (tile - 1) % NT)

    def dve_ms(dve, h, which):
        dve.wait_ge(s_ssq, h * 2 + (which + 1))
        cols = slice(SSQ + NT * which, SSQ + NT * (which + 1))
        if which == 0:
            dve.tensor_scalar(kms[:, :], b_local[:, cols], 1.0 / D, EPS, ALU.mult, ALU.add).then_inc(s_ms, 1)
        else:
            dve.tensor_scalar(qms[:, :], b_local[:, cols], D * EPS, None, ALU.add).then_inc(s_ms, 1)

    def dve_unit(dve, h, par, u):
        n = h * 16 + u
        src = b_unit[u % 2]
        if u < 8:
            dve.wait_ge(s_square, h * 8 + (u + 1))
            which, c, cos, row, dst = (1, u, cosk, 0, kT) if u < 4 else (0, u - 4, cosq, 2 * ROT, qT)
            wait_for(dve, s_rope, h * 8 + (u - 1))
            lo, hi = slice(0, ROT), slice(ROT, 2 * ROT)
            dve.scalar_tensor_tensor(turned[u % 2][lo, :], src[hi, :], bias_col(par, which, hi),
                                     sin[row + ROT:row + 2 * ROT, chunk(c)], ALU.add, ALU.mult)
            dve.scalar_tensor_tensor(turned[u % 2][hi, :], src[lo, :], bias_col(par, which, lo),
                                     sin[row:row + ROT, chunk(c)], ALU.add, ALU.mult)
            dve.scalar_tensor_tensor(dst[par][:, chunk(c)], src[:, :], bias_col(par, which),
                                     cos[:, chunk(c)], ALU.add, ALU.mult).then_inc(s_uvec, 1)
        else:
            dve.wait_ge(s_unit, n + 1)
            if u == 8:
                dve.wait_ge(s_rope, h * 8 + 4)
            tiles = value_tiles(u)
            blv = wh[par][:, 3 * KC * D + 2:HEAD_COLS]
            dve.tensor_tensor(v[par][:, tiles.start:tiles.stop, :], src[:, 0:2 * D].rearrange("p (a d) -> p a d", a=2),
                              blv.unsqueeze(1).to_broadcast([P, 2, D]), ALU.add)
            keys = kT[par][:, tiles.start * P:tiles.stop * P]
            dve.tensor_tensor(keys, keys, src[:, 2 * P:4 * P], ALU.mult).then_inc(s_uvec, 1)

    def dve_nfac(dve, h, par):
        dve.wait_ge(s_rstd, h * 2 + 2)
        dve.tensor_scalar(nfac[par][:, :], qfac[par][:, :], -1.0, None, ALU.mult).then_inc(s_nfac, 1)

    def dve_ctx(dve, n, par, tile):
        dve.wait_ge(s_ctxc, n + 1)
        dve.tensor_tensor(ctx_half(even_lo, odd_lo, par, tile), b_ctx[:, 0:P],
                          ctx_half(even_hi, odd_hi, par, tile).bitcast(F32), ALU.subtract).then_inc(s_ctxl, 1)

    def dve_wo(dve, i):
        dve.wait_ge(s_woh, i + 1)
        dve.tensor_tensor(wo_lo[:, :, :], wo[:, :, :], wo_hi[:, :, :].bitcast(F32), ALU.subtract).then_inc(s_wol, 1)

    def dve_step(dve, i, n, par, tile, ms_of):
        b, w, lc = tile % 2, width(tile), local_cols(tile)
        dve.wait_ge(s_scores, n + 1)
        wait_for(dve, s_turn, n - 1)
        dve.memset(prob[b][:, w:blocks(tile) * P] if w < blocks(tile) * P else total[b][:, :], 0.0)
        if ms_of is not None:
            dve_ms(dve, ms_of, tile // 8)
        pl = prob[b][:, C:C + 2 * P]
        dve.tensor_tensor_reduce(pl[:, lc], b_local[:, lc], band[:, lc], 1.0, NEG, ALU.add, ALU.max,
                                 top[b][:, TOPK:TOPK + 1]).then_inc(s_top, 1)
        dve.max(top[b][:, 0:TOPK], b_score[:, 0:w]).then_inc(s_top, 1)
        dve.wait_ge(s_top, n * 2 + 2)
        if tile == 0:
            dve.wait_ge(s_nfac, i * 2 + (par + 1))
        dve.tensor_scalar(nbias[b][:, :], top[b][:, 0:TOPK + 1:TOPK], FLOOR, nfac[par][:, tile:tile + 1],
                          ALU.max, ALU.mult).then_inc(s_bias, 1)
        dve.match_replace(taken[:, 0:w], top[b][:, 0:TOPK], b_score[:, 0:w], TAKEN).then_inc(s_taken, 1)
        dve.wait_ge(s_exp, n + 1)
        dve.wait_ge(s_taken, n + 1)
        dve.scalar_tensor_tensor(prob[b][:, 0:w], taken[:, 0:w], TAKEN / 2, prob[b][:, 0:w], ALU.is_ge, ALU.mult,
                                 accum_out=total[b][:, 0:1]).then_inc(s_total, 1)
        dve.wait_ge(s_total, n * 2 + 1)
        dve.tensor_scalar(total[b][:, :], total[b][:, :], 1e-9, 2.0, ALU.max, ALU.mult).then_inc(s_total, 1)
        dve.wait_ge(s_total, n * 2 + 2)
        dve.reciprocal(share[b][:, :], total[b][:, :]).then_inc(s_share, 1)

    def dve_acc(dve, i, tile):
        dve.wait_ge(s_out, i * 16 + (tile + 1))
        dve.tensor_tensor(acc[:, tile, :], acc[:, tile, :], b_out[:, :], ALU.add).then_inc(s_acc, 1)

    def dve_pair(dve, i, first=False, last=False):
        for j in range(2 * NT):
            n, par, tile = i * 32 + j, j // NT, j % NT
            nxt = i * 2 + (par + 1)
            units = not (last and par == 1)
            before = (n - 2, par if tile >= 2 else 1 - par, (tile - 2) % NT)
            if j >= 2 or not first:
                dve_ctx(dve, *before)
            dve_step(dve, i, n, par, tile, nxt if units and tile in (4, 8) else None)
            if units:
                dve_unit(dve, nxt, 1 - par, tile)
                if tile == 11:
                    dve_nfac(dve, nxt, 1 - par)
            if j == NT - 1:
                dve_wo(dve, i)
            if j >= NT + 2:
                dve_acc(dve, i, tile - 2)
            elif j < 2 and not first:
                dve_acc(dve, i - 1, NT - 2 + j)

    def act_square(act, h, par, u):
        act.wait_ge(s_unit, h * 16 + (u + 1))
        act.activation(square[u % 2][:, :], b_unit[u % 2][:, :], ACT.Square,
                       bias=bias_col(par, 1 if u < 4 else 0)).then_inc(s_square, 1)

    def act_probT(act, n, tile):
        act.wait_ge(s_turn, n + 1)
        w = blocks(tile) * P
        act.copy(probT[:, 0:w], b_turn_s[:, 0:w])
        lc = local_cols(tile)
        act.copy(probT[:, C:C + 2 * P][:, lc], b_turn_l[:, lc]).then_inc(s_probT, 1)

    def act_exp(act, n, par, tile):
        b, w = tile % 2, width(tile)
        act.wait_ge(s_bias, n + 1)
        pl = prob[b][:, C:C + 2 * P][:, local_cols(tile)]
        act.activation(pl, pl, ACT.Exp, bias=nbias[b][:, 1:2], scale=qfac[par][:, tile:tile + 1],
                       accum_out=total[b][:, 1:2])
        act.wait_ge(s_taken, n + 1)
        act.activation(prob[b][:, 0:w], b_score[:, 0:w], ACT.Exp, bias=nbias[b][:, 0:1],
                       scale=qfac[par][:, tile:tile + 1]).then_inc(s_exp, 1)

    def act_ctx(act, n, par, tile):
        act.wait_ge(s_ctx, n + 1)
        act.copy(ctx_half(even_hi, odd_hi, par, tile), b_ctx[:, 0:P]).then_inc(s_ctxc, 1)

    def act_wo(act, i):
        act.wait_ge(wo_in, i * 16 + 16)
        wait_for(act, s_out, i * 16)
        act.copy(wo_hi[:, :, :], wo[:, :, :]).then_inc(s_woh, 1)

    def act_pair(act, i, first=False, last=False):
        for j in range(2 * NT):
            n, par, tile = i * 32 + j, j // NT, j % NT
            if j or not first:
                act_probT(act, n - 1, (tile - 1) % NT)
            act_exp(act, n, par, tile)
            if tile < 8 and not (last and par == 1):
                act_square(act, i * 2 + (par + 1), 1 - par, tile)
            if j or not first:
                act_ctx(act, n - 1, par if tile else 1 - par, (tile - 1) % NT)
            if j == NT - 2:
                act_wo(act, i)

    def pool_rope(pool, h, par, u):
        pool.wait_ge(s_uvec, h * 16 + (u + 1))
        dst = kT[par] if u < 4 else qT[par]
        part = dst[0:2 * ROT, chunk(u % 4)]
        pool.tensor_tensor(part, part, turned[u % 2][:, :], ALU.add).then_inc(s_rope, 1)

    def pool_rstd(pool, h, par, which):
        pool.wait_ge(s_ms, h * 2 + (which + 1))
        src, dst = (kms, krstd) if which == 0 else (qms, qfac)
        pool.tensor_tensor(dst[par][:, :], src[:, :], half[:, 0:NT], ALU.pow).then_inc(s_rstd, 1)

    def pool_prob(pool, n, tile):
        b, w = tile % 2, width(tile)
        pool.wait_ge(s_share, n + 1)
        pl = prob[b][:, C:C + 2 * P][:, local_cols(tile)]
        pool.tensor_tensor(pl, pl, share[b][:, 1:2].to_broadcast(list(pl.shape)), ALU.mult)
        pool.tensor_scalar(prob[b][:, 0:w], prob[b][:, 0:w], share[b][:, 0:1], 1.0, ALU.mult,
                           ALU.mult).then_inc(s_prob, 1)

    def pool_pair(pool, i, first=False, last=False):
        for j in range(2 * NT):
            n, par, tile = i * 32 + j, j // NT, j % NT
            nxt = i * 2 + (par + 1)
            units = not (last and par == 1)
            if units and tile in (4, 8):
                pool_rstd(pool, nxt, 1 - par, tile // 8)
            pool_prob(pool, n, tile)
            if units and tile < 8:
                pool_rope(pool, nxt, 1 - par, tile)

    NP = NH // 2
    with nc.Block() as block:
        @block.sync
        def _(sp):
            def load_head(h, par):
                wait_for(sp, s_uvec, h * 16 - 16)
                sp.dma_start(wh[par][:, :], t["wh"][h, :, :] if isinstance(h, int)
                             else t["wh"][bass.ds(h, 1), :, :].rearrange("o p c -> (o p) c")).then_inc(w_in[par], 16)

            def load_wo(i):
                wait_for(sp, s_wol, i)
                rows = t["Wo"][0:2 * D, :] if isinstance(i, int) and i == 0 else t["Wo"][bass.ds(i * (2 * D), 2 * D), :]
                sp.dma_start(wo[:, :, :], rows.rearrange("(a d) n -> d a n", a=2)).then_inc(wo_in, 16)

            sp.wait_ge(s_zero, 1)
            for n in range(MAXT // 2):
                sp.dma_start(xs[n * 2 * P:(n + 1) * 2 * P, :].rearrange("(p a) d -> p (a d)", a=2),
                             zeros).then_inc(zero_sem, 16)
            for n in range(PICK * NT // 2, MAXT // 2):
                sp.dma_start(ys[n * 2 * P:(n + 1) * 2 * P, :].rearrange("(p a) d -> p (a d)", a=2),
                             zeros).then_inc(zero_sem, 16)
            sp.wait_ge(zero_sem, zero_count)
            load_wo(0)
            with sp.Fori(1, NP) as i:
                load_head(i * 2, 0)
                load_head(i * 2 + 1, 1)
                load_wo(i)

        @block.tensor
        def _(pe):
            for u in range(NT):
                pe_unit(pe, 0, 0, u, 0)
                if 1 <= u <= 8:
                    if u == 5:
                        pe.wait_ge(s_ms, 1)
                    pe_ssq(pe, 0, u - 1)
            pe.wait_ge(s_ms, 2)
            pe_pair(pe, 0, first=True)
            with pe.Fori(1, NP - 1) as i:
                pe_pair(pe, i)
            pe_pair(pe, NP - 1, last=True)
            n = NH * NT
            pe_turn(pe, n - 1, NT - 1)
            pe_out(pe, NP - 1, n - 2, NT - 2)
            pe_context(pe, n - 1, 1, NT - 1)
            pe_out(pe, NP - 1, n - 1, NT - 1)

        @block.vector
        def _(dve):
            for u in range(NT):
                dve_unit(dve, 0, 0, u)
                if u in (4, 8):
                    dve_ms(dve, 0, u // 8)
            dve_nfac(dve, 0, 0)
            dve_pair(dve, 0, first=True)
            with dve.Fori(1, NP - 1) as i:
                dve_pair(dve, i)
            dve_pair(dve, NP - 1, last=True)
            dve_ctx(dve, NH * NT - 2, 1, NT - 2)
            dve_acc(dve, NP - 1, NT - 2)
            dve_ctx(dve, NH * NT - 1, 1, NT - 1)
            dve_acc(dve, NP - 1, NT - 1)

        @block.scalar
        def _(act):
            for u in range(8):
                act_square(act, 0, 0, u)
            act_pair(act, 0, first=True)
            with act.Fori(1, NP - 1) as i:
                act_pair(act, i)
            act_pair(act, NP - 1, last=True)
            n = NH * NT
            act_probT(act, n - 1, NT - 1)
            act_ctx(act, n - 1, 1, NT - 1)

        @block.gpsimd
        def _(pool):
            pool.memset(wo[:, :, :], 0.0).then_inc(s_zero, 1)
            for u in range(8):
                pool_rope(pool, 0, 0, u)
                if u == 4:
                    pool_rstd(pool, 0, 0, 0)
            pool_rstd(pool, 0, 0, 1)
            pool_pair(pool, 0, first=True)
            with pool.Fori(1, NP - 1) as i:
                pool_pair(pool, i)
            pool_pair(pool, NP - 1, last=True)


def feed_forward(nc, t, bank, acc, ident, xs, ys, zeroed, sb_in, sem_in):
    whole = ExitStack()

    def sb(name, shape, dt=F32, stack=whole):
        return sb_in(name, shape, dt, stack)

    def sem(name, stack=whole):
        return sem_in(name, stack)

    with whole:
        slots = sb("slots", [P, NT, PICK], U32)
        pick_w = sb("pick_w", [P, NT, PICK])
        tile_expert = sb("tile_expert", [P, MAXT], I32)
        first_tile = sb("first_tile", [P, E + 1], I32)
        mv = sb("mv", [P, NT, 2])
        rstd = sb("rstd2", [P, NT])
        neghalf = sb("neghalf", [P, NT])
        stats = sb("stats", [P, 4, 6])

        mid = ExitStack()
        with mid:
            whi = sb("whi", [P, 2, WCOLS], F32R, mid)
            wlo = sb("wlo", [P, 2, WCOLS], F32R, mid)
            first_norm_and_split(nc, t, acc, mv, rstd, neghalf, stats, whi, wlo,
                                 sb, sem)
            route_and_shared(nc, t, bank, acc, ident, xs, zeroed, mv, rstd, slots, pick_w, tile_expert, first_tile,
                             whi, wlo, sb, sem)
        ring_hi = sb("ring_hi", [P, RING, WCOLS], F32R)
        ring_lo = sb("ring_lo", [P, RING, WCOLS], F32R)
        routed(nc, t, bank, ident, xs, ys, tile_expert, first_tile, ring_hi, ring_lo, sb, sem)
        combine(nc, t, bank, acc, ident, ys, slots, pick_w, mv, rstd, neghalf, stats, ring_hi, ring_lo, sb, sem)


def first_norm_and_split(nc, t, acc, mv, rstd, neghalf, stats, whi, wlo, sb, sem):
    st = ExitStack()
    with st:
        PARTS = 4
        NP = NSH * PARTS
        pc = WCOLS // PARTS
        staged = sb("staged_shared", [P, NP, pc], F32, st)
        s_in = [sem(f"shared_in{i}", st) for i in range(NP)]
        s_hi, s_st, s_mv, s_eps, s_half = (sem(x, st) for x in (
            "shared_hi", "ln1_stats", "ln1_mv", "ln1_eps", "ln1_half"))

        def cols(i):
            return slice(i % PARTS * pc, (i % PARTS + 1) * pc)

        with nc.Block() as block:
            @block.sync
            def _(sp):
                for i in range(NP):
                    sp.dma_start(staged[:, i, :], t["wexp"][E + i // PARTS, :, cols(i)]).then_inc(s_in[i], 16)

            @block.scalar
            def _(act):
                for i in range(NP):
                    act.wait_ge(s_in[i], 16)
                    act.copy(whi[:, i // PARTS, cols(i)], staged[:, i, :]).then_inc(s_hi, 1)

            @block.gpsimd
            def _(pool):
                pool.memset(neghalf[:, :], -0.5).then_inc(s_half, 1)
                pool.wait_ge(s_half, 1)
                pool.wait_ge(s_eps, 1)
                pool.tensor_tensor(rstd[:, :], rstd[:, :], neghalf[:, :], ALU.pow)

            @block.vector
            def _(dve):
                for n in range(NT + 2):
                    if n < NT:
                        wait_for(dve, s_mv, n - 3)
                        dve.bn_stats(stats[:, n % 4, :], acc[:, n, :]).then_inc(s_st, 1)
                    if n >= 2:
                        dve.wait_ge(s_st, n - 1)
                        dve.bn_aggr(mv[:, n - 2, :], stats[:, (n - 2) % 4, :]).then_inc(s_mv, 1)
                dve.wait_ge(s_mv, NT)
                dve.tensor_scalar(rstd[:, :], mv[:, :, 1], LN_EPS, None, ALU.add).then_inc(s_eps, 1)
                for i in range(NP):
                    dve.wait_ge(s_hi, i + 1)
                    dve.tensor_tensor(wlo[:, i // PARTS, cols(i)], staged[:, i, :],
                                      whi[:, i // PARTS, cols(i)].bitcast(F32), ALU.subtract)


def three_products(pe, out, hi_lo_w, hi_lo_x, first, last):
    (wh_, wl_), (xh_, xl_) = hi_lo_w, hi_lo_x
    pe.matmul(out, wl_, xh_, start=first, stop=False)
    pe.matmul(out, wh_, xl_, start=False, stop=False)
    return pe.matmul(out, wh_, xh_, start=False, stop=last)


def w13_cols(w, k):
    at = (w * KC + k) * INTER
    return at, at + INTER


def w2_cols(b):
    at = 2 * KC * INTER + b * HID
    return at, at + HID


def route_and_shared(nc, t, bank, acc, ident, xs, zeroed, mv, rstd, slots, pick_w, tile_expert, first_tile,
                     whi, wlo, sb, sem):
    DVE_FROM = 2
    AT_ONCE = 3
    st = ExitStack()
    with st:
        raw = [sb(f"raw{i}", [P, CH], F32, st) for i in range(3)]
        up3 = [sb(f"up3_{i}", [P, CH], F32, st) for i in range(2)]
        shared = sb("shared", [P, DVE_FROM * TPC, HID], F32, st)
        gateT = sb("gateT", [P, KC, E], F32, st)
        ebias = sb("ebias", [P, E], F32, st)
        sig = sb("sig", [P, NT, E], F32, st)
        choice = sb("choice", [P, NT, E], F32, st)
        gbest = sb("gbest", [P, NT, G], F32, st)
        cmp = sb("cmp", [P, NT, E], F32, st)
        grank = sb("grank", [P, NT, G], F32, st)
        rank = sb("rank", [P, NT, E], F32, st)
        picked = sb("picked", [P, NT, E], F32, st)
        pickedb = sb("pickedb", [P, NT, E], BF16, st)
        trib = sb("trib", [P, 2, P], BF16, st)
        tri = sb("tri", [P, 2, P], F32, st)
        before = [sb(f"before{i}", [P, NT, E], F32, st) for i in range(2)]
        slotf = sb("slotf", [P, NT, E], F32, st)
        load = sb("load", [P, E], F32, st)
        ramp = sb("ramp", [P, MAXT], F32, st)
        tiles = [sb(f"tiles{i}", [P, E], F32, st) for i in range(2)]
        by16 = sb("by16", [P, E, E], F32, st)
        byt = sb("byt", [P, MAXT, E], F32, st)
        texp = sb("texp", [P, MAXT], F32, st)
        slot4 = sb("slot4", [P, NT, PICK], F32, st)
        csum = sb("csum", [P, NT], F32, st)
        xhi = sb("xhi", [P, KC, CH], F32R, st)
        xlo = sb("xlo", [P, KC, CH], F32R, st)
        gate = [sb(f"gate{i}", [P, CH], F32, st) for i in range(2)]
        hid = [sb(f"hid{i}", [P, CH], F32, st) for i in range(2)]
        hhi = sb("hhi", [P, NSH * HB, CH], F32R, st)
        hlo = sb("hlo", [P, NSH * HB, CH], F32R, st)

        g_in, s_turned, s_raw, s_logits, s_sig, s_r, s_pick, s_count, s_slots, s_scat = (sem(x, st) for x in (
            "gate_in", "x1_turned", "x1_raw", "gate_done", "sig_done", "router_step", "picked_done",
            "counts_done", "slots_done", "scatter_done"))
        s_xt, s_xhi, s_xlo, s_up, s_silu, s_hid, s_hhi, s_hlo, s_y = (sem(x, st) for x in (
            "sh_xt", "sh_xhi", "sh_xlo", "sh_up", "sh_silu", "sh_hid", "sh_hhi", "sh_hlo", "sh_y"))
        s_norm, s_yc, s_hlo_dve = sem("ln1_done", st), sem("sh_y_copied", st), sem("sh_hlo_dve", st)
        NB = NSH * HB
        POOL_BLOCKS = DVE_FROM * NB - 2

        gate_bank = (bank[0], bank[1], bank[6])

        def gate_group(q):
            return range(max(q, 0) * AT_ONCE, min((q + 1) * AT_ONCE, NT))

        def y_bank(m):
            return bank[6 + m % 2] if m < DVE_FROM * TPC else (bank[6], bank[7], bank[0], bank[1])[m % TPC]

        def low_of_x(eng, c, k):
            eng.wait_ge(s_xhi, c * KC + k + 1)
            src = bank[k % 2] if c >= DVE_FROM else raw[k % 2]
            eng.tensor_tensor(xlo[:, k, :], src[:, :], xhi[:, k, :].bitcast(F32), ALU.subtract).then_inc(s_xlo, 1)

        def hidden(eng, n, q):
            rows = hb_rows(q % HB)
            eng.wait_ge(s_silu, n + 1)
            src = bank[4 + q % 2] if n >= POOL_BLOCKS else up3[n % 2]
            if n == POOL_BLOCKS:
                eng.wait_ge(s_hlo, n)
            eng.tensor_tensor(hid[n % 2][0:rows, :], gate[n % 2][0:rows, :], src[0:rows, :], ALU.mult).then_inc(s_hid, 1)

        def low_of_hidden(eng, n, q):
            rows = hb_rows(q % HB)
            eng.wait_ge(s_hhi, n + 1)
            eng.tensor_tensor(hlo[0:rows, q, :], hid[n % 2][0:rows, :], hhi[0:rows, q, :].bitcast(F32),
                              ALU.subtract).then_inc(s_hlo if n < POOL_BLOCKS else s_hlo_dve, 1)

        def hidden_blocks(eng, first, end):
            for n in range(first, end):
                hidden(eng, n, n % NB)
                low_of_hidden(eng, n, n % NB)

        def chunk_halves(eng, c, end):
            for k in range(KC):
                low_of_x(eng, c, k)
            hidden_blocks(eng, c * NB, end)

        with nc.Block() as block:
            @block.sync
            def _(sp):
                sp.dma_start(gateT[:, :, :], t["gateT"].rearrange("(k p) e -> p k e", p=P)).then_inc(g_in, 16)
                sp.dma_start(ebias[:, :], t["ebias"].broadcast_to([P, E])).then_inc(g_in, 16)
                sp.dma_start(tri[:, :, :], t["tri"]).then_inc(g_in, 16)
                sp.dma_start(ramp[:, :], t["ramp"].broadcast_to([P, MAXT])).then_inc(g_in, 16)

            @block.tensor
            def _(pe):
                def gate_logits(n):
                    pe.wait_ge(s_raw, n + 1)
                    for k in range(KC):
                        mm = pe.matmul(bank[7][:, n * E:(n + 1) * E], raw[n % 3][:, k * P:(k + 1) * P], gateT[:, k, :],
                                       start=(k == 0), stop=(k == KC - 1))
                    return mm

                def gate_turn(n):
                    pe.wait_ge(s_norm, n + 1)
                    wait_for(pe, s_raw, n - 2)
                    for k in range(KC):
                        mm = pe.transpose(gate_bank[n % 3][:, k * P:(k + 1) * P], acc[:, n, k * P:(k + 1) * P], ident[:, :])
                    mm.then_inc(s_turned, 1)

                def turn(c, k):
                    if c < DVE_FROM:
                        wait_for(pe, s_xhi, c * KC + k)
                    else:
                        pe.wait_ge(s_xlo, c * KC + k - 1)
                    b = k % 2 if c >= DVE_FROM else 0
                    pe.wait_ge(s_norm, (c + 1) * TPC)
                    for i in range(TPC):
                        mm = pe.transpose(bank[b][:, i * P:(i + 1) * P], acc[:, c * TPC + i, k * P:(k + 1) * P],
                                          ident[:, :])
                    mm.then_inc(s_xt, 1)

                def up(c, q):
                    n = c * NB + q
                    s, b = divmod(q, HB)
                    rows = hb_rows(b)
                    if q == 0:
                        pe.wait_ge(s_xlo, (c + 1) * KC)
                    wait_for(pe, s_hid, n - 1)
                    for w in range(2):
                        for k in range(KC):
                            at = w13_cols(w, k)[0] + b * P
                            mm = three_products(pe, bank[2 + 2 * w + q % 2][0:rows, :],
                                                (whi[:, s, at:at + rows], wlo[:, s, at:at + rows]),
                                                (xhi[:, k, :], xlo[:, k, :]), k == 0, k == KC - 1)
                    mm.then_inc(s_up, 1)

                def down(c):
                    pe.wait_ge(s_hlo, min((c + 1) * NB, POOL_BLOCKS))
                    wait_for(pe, s_hlo_dve, (c + 1) * NB - POOL_BLOCKS)
                    for i in range(TPC):
                        m = c * TPC + i
                        wait_for(pe, s_yc, min(m - 1, DVE_FROM * TPC))
                        for q in range(NB):
                            s, b = divmod(q, HB)
                            rows = hb_rows(b)
                            lo_, hi_ = w2_cols(b)
                            cols = slice(i * P, (i + 1) * P)
                            mm = three_products(pe, y_bank(m)[:, :],
                                                (hhi[0:rows, q, cols], hlo[0:rows, q, cols]),
                                                (whi[0:rows, s, lo_:hi_], wlo[0:rows, s, lo_:hi_]),
                                                q == 0, q == NB - 1)
                        mm.then_inc(s_y, 1)

                for k in range(KC):
                    turn(0, k)
                pe.wait_ge(g_in, 64)
                for c in range(EARLY):
                    for q in range(NB):
                        up(c, q)
                        if c == 0:
                            for n in gate_group(q - 1):
                                last = gate_logits(n)
                            for n in gate_group(q):
                                gate_turn(n)
                    if c == 0:
                        for n in gate_group(NB - 1):
                            last = gate_logits(n)
                        last.then_inc(s_logits, 1)
                    if c + 1 == DVE_FROM:
                        pe.wait_ge(s_count, 2)
                    if c + 1 < EARLY:
                        for k in range(KC):
                            turn(c + 1, k)
                    if c == 0:
                        pe.wait_ge(s_sig, 1)
                    down(c)
                    if c == 0:
                        pe.wait_ge(s_pick, 1)
                        picks = pickedb[:, :, :].rearrange("p n e -> p (n e)")
                        pe.matmul(bank[1][:, 0:NT * E], trib[:, 0, :], picks, start=True, stop=True)
                        pe.matmul(bank[1][:, NT * E:2 * NT * E], trib[:, 1, :], picks,
                                  start=True, stop=True).then_inc(s_count, 1)

            @block.scalar
            def _(act):
                def x_high(c):
                    for k in range(KC):
                        act.wait_ge(s_xt, c * KC + k + 1)
                        wait_for(act, s_up, c * NB)
                        b = k % 2 if c >= DVE_FROM else 0
                        if c < DVE_FROM:
                            wait_for(act, s_xlo, c * KC + k - 1)
                            act.copy(raw[k % 2][:, :], bank[b][:, :])
                        act.copy(xhi[:, k, :], bank[b][:, :]).then_inc(s_xhi, 1)

                x_high(0)
                for c in range(EARLY):
                    for q in range(NB):
                        n = c * NB + q
                        rows = hb_rows(q % HB)
                        act.wait_ge(s_up, n + 1)
                        if n < POOL_BLOCKS:
                            act.copy(up3[n % 2][0:rows, :], bank[4 + q % 2][0:rows, :])
                        act.activation(gate[n % 2][0:rows, :], bank[2 + q % 2][0:rows, :], ACT.Silu).then_inc(s_silu, 1)
                        act.wait_ge(s_hid, n + 1)
                        wait_for(act, s_y, c * TPC)
                        act.copy(hhi[0:rows, q, :], hid[n % 2][0:rows, :]).then_inc(s_hhi, 1)
                        if c == 0:
                            for m in gate_group(q):
                                act.wait_ge(s_turned, m + 1)
                                act.copy(raw[m % 3][:, :], gate_bank[m % 3][:, :]).then_inc(s_raw, 1)
                    if c == 0:
                        act.wait_ge(s_logits, 1)
                        act.activation(sig[:, :, :], bank[7][:, 0:NT * E].rearrange("p (n e) -> p n e", e=E),
                                       ACT.Sigmoid).then_inc(s_sig, 1)
                    if c + 1 < EARLY:
                        x_high(c + 1)
                    if c < DVE_FROM:
                        for m in range(c * TPC, (c + 1) * TPC):
                            act.wait_ge(s_y, m + 1)
                            act.copy(shared[:, m, :], y_bank(m)[:, :]).then_inc(s_yc, 1)

            @block.gpsimd
            def _(pool):
                for c in range(DVE_FROM):
                    chunk_halves(pool, c, min((c + 1) * NB, POOL_BLOCKS))
                pool.wait_ge(s_slots, 1)
                for z in zeroed:
                    pool.wait_ge(*z)
                for n in range(NT):
                    for k in range(PICK):
                        pool.indirect_dma_start(xs[:, :], bass.IndirectOffsetOnAxis(ap=slots[:, n, k:k + 1], axis=0),
                                                acc[:, n, :], None, bounds_check=MAXT * P - 1,
                                                oob_is_err=False).then_inc(s_scat, 16)
                pool.wait_ge(s_scat, 16 * NT * PICK)

            @block.vector
            def _(dve):
                count = [0]

                def then(ins):
                    count[0] += 1
                    ins.then_inc(s_r, 1)
                    dve.wait_ge(s_r, count[0])

                def prefix(bufs, total, axis_view):
                    a, shift = 0, 1
                    while shift < total:
                        x, y = axis_view(bufs[a]), axis_view(bufs[1 - a])
                        then(dve.tensor_copy(y[:, 0:shift, :], x[:, 0:shift, :]))
                        then(dve.tensor_tensor(y[:, shift:total, :], x[:, shift:total, :], x[:, 0:total - shift, :], ALU.add))
                        a, shift = 1 - a, 2 * shift
                    return bufs[a]

                for n in range(NT):
                    dve.tensor_scalar(acc[:, n, :], acc[:, n, :], mv[:, n, 0:1], rstd[:, n:n + 1],
                                      ALU.subtract, ALU.mult).then_inc(s_norm, 1)
                dve.wait_ge(g_in, 64)
                then(dve.tensor_copy(trib[:, :, :], tri[:, :, :]))
                dve.wait_ge(s_sig, 1)
                then(dve.tensor_tensor(choice[:, :, :], sig[:, :, :], ebias[:, :].unsqueeze(1).to_broadcast([P, NT, E]),
                                       ALU.add))
                then(dve.tensor_reduce(gbest[:, :, :], choice[:, :, :].rearrange("p n (g e) -> p n g e", e=EG),
                                       AX.X, ALU.max))
                then(dve.memset(grank[:, :, :], 0.0))
                for o in range(G):
                    other = gbest[:, :, o:o + 1]
                    if o + 1 < G:
                        then(dve.tensor_tensor(cmp[:, :, o + 1:G], other.to_broadcast([P, NT, G - o - 1]),
                                               gbest[:, :, o + 1:G], ALU.is_ge))
                        then(dve.tensor_tensor(grank[:, :, o + 1:G], grank[:, :, o + 1:G], cmp[:, :, o + 1:G], ALU.add))
                    if o:
                        then(dve.tensor_tensor(cmp[:, :, 0:o], other.to_broadcast([P, NT, o]), gbest[:, :, 0:o], ALU.is_gt))
                        then(dve.tensor_tensor(grank[:, :, 0:o], grank[:, :, 0:o], cmp[:, :, 0:o], ALU.add))
                then(dve.tensor_scalar(grank[:, :, :], grank[:, :, :], float(PICK_G), None, ALU.is_lt))
                gm = grank[:, :, :].unsqueeze(3).to_broadcast([P, NT, G, EG])
                c4 = choice[:, :, :].rearrange("p n (g e) -> p n g e", e=EG)
                then(dve.tensor_tensor(c4, c4, gm, ALU.mult))
                then(dve.tensor_scalar(grank[:, :, :], grank[:, :, :], -1.0, -NEG, ALU.add, ALU.mult))
                then(dve.tensor_tensor(c4, c4, gm, ALU.add))
                then(dve.memset(rank[:, :, :], 0.0))
                for o in range(E):
                    other = choice[:, :, o:o + 1]
                    if o + 1 < E:
                        dve.tensor_tensor(cmp[:, :, o + 1:E], other.to_broadcast([P, NT, E - o - 1]),
                                          choice[:, :, o + 1:E], ALU.is_ge).then_inc(s_r, 1)
                        count[0] += 1
                    if o:
                        dve.tensor_tensor(cmp[:, :, 0:o], other.to_broadcast([P, NT, o]),
                                          choice[:, :, 0:o], ALU.is_gt).then_inc(s_r, 1)
                        count[0] += 1
                    dve.memset(cmp[:, :, o:o + 1], 0.0).then_inc(s_r, 1)
                    count[0] += 1
                    dve.wait_ge(s_r, count[0])
                    then(dve.tensor_tensor(rank[:, :, :], rank[:, :, :], cmp[:, :, :], ALU.add))
                then(dve.tensor_scalar(picked[:, :, :], rank[:, :, :], float(PICK), None, ALU.is_lt))
                dve.tensor_copy(pickedb[:, :, :], picked[:, :, :]).then_inc(s_pick, 1)
                then(dve.tensor_tensor(sig[:, :, :], sig[:, :, :], picked[:, :, :], ALU.mult))
                then(dve.tensor_reduce(csum[:, :], sig[:, :, :], AX.X, ALU.add))
                then(dve.reciprocal(csum[:, :], csum[:, :]))
                then(dve.tensor_tensor(sig[:, :, :], sig[:, :, :], csum[:, :].unsqueeze(2).to_broadcast([P, NT, E]),
                                       ALU.mult))
                dve.wait_ge(s_count, 1)
                ne = lambda b: b[:, :, :]
                within, sums = (bank[1][:, x * NT * E:(x + 1) * NT * E].rearrange("p (n e) -> p n e", e=E) for x in range(2))
                then(dve.tensor_copy(before[0][:, :, :], sums))
                full = prefix(before, NT, ne)
                then(dve.tensor_copy(load[:, :], full[:, NT - 1, :]))
                then(dve.tensor_tensor(full[:, :, :], full[:, :, :], sums, ALU.subtract))
                then(dve.tensor_tensor(full[:, :, :], full[:, :, :], within, ALU.add))
                dve.nop().then_inc(s_count, 1)
                then(dve.tensor_scalar(texp[:, 0:E], ramp[:, 0:E], float(P), None, ALU.mult))
                then(dve.tensor_tensor(by16[:, :, :], load[:, :].unsqueeze(2).to_broadcast([P, E, E]),
                                       texp[:, 0:E].unsqueeze(1).to_broadcast([P, E, E]), ALU.is_gt))
                then(dve.tensor_reduce(tiles[0][:, :], by16[:, :, :], AX.X, ALU.add))
                then(dve.tensor_scalar(tiles[0][:, :], tiles[0][:, :], 1.0, None, ALU.max))
                then(dve.tensor_copy(load[:, :], tiles[0][:, :]))
                upto = prefix(tiles, E, lambda b: b[:, :].unsqueeze(2))
                then(dve.tensor_scalar(upto[:, :], upto[:, :], 1.0, None, ALU.add))
                then(dve.tensor_copy(first_tile[:, E:E + 1], upto[:, E - 1:E]))
                then(dve.tensor_tensor(upto[:, :], upto[:, :], load[:, :], ALU.subtract))
                then(dve.tensor_copy(first_tile[:, 0:E], upto[:, :]))
                then(dve.tensor_tensor(byt[:, :, :], ramp[:, :].unsqueeze(2).to_broadcast([P, MAXT, E]),
                                       upto[:, :].unsqueeze(1).to_broadcast([P, MAXT, E]), ALU.is_ge))
                then(dve.tensor_reduce(texp[:, :], byt[:, :, :], AX.X, ALU.add))
                then(dve.tensor_scalar(texp[:, :], texp[:, :], -1.0, 0.0, ALU.add, ALU.max))
                then(dve.tensor_copy(tile_expert[:, :], texp[:, :]))
                then(dve.tensor_scalar(upto[:, :], upto[:, :], float(P), None, ALU.mult))
                then(dve.tensor_tensor(slotf[:, :, :], full[:, :, :], upto[:, :].unsqueeze(1).to_broadcast([P, NT, E]),
                                       ALU.add))
                for k in range(PICK):
                    then(dve.tensor_scalar(cmp[:, :, :], rank[:, :, :], float(k), None, ALU.is_equal))
                    dve.tensor_tensor(choice[:, :, :], cmp[:, :, :], sig[:, :, :], ALU.mult)
                    then(dve.tensor_tensor(picked[:, :, :], cmp[:, :, :], slotf[:, :, :], ALU.mult))
                    dve.tensor_reduce(slot4[:, :, k:k + 1], picked[:, :, :], AX.X, ALU.add)
                    then(dve.tensor_reduce(pick_w[:, :, k:k + 1], choice[:, :, :], AX.X, ALU.add))
                dve.tensor_copy(slots[:, :, :], slot4[:, :, :]).then_inc(s_slots, 1)

                hidden_blocks(dve, POOL_BLOCKS, DVE_FROM * NB)
                for c in range(DVE_FROM, EARLY):
                    chunk_halves(dve, c, (c + 1) * NB)
                dve.wait_ge(s_scat, 16 * NT * PICK)
                dve.wait_ge(s_yc, DVE_FROM * TPC)
                dve.tensor_tensor(acc[:, 0:DVE_FROM * TPC, :], acc[:, 0:DVE_FROM * TPC, :], shared[:, :, :], ALU.add)
                for m in range(DVE_FROM * TPC, EARLY * TPC):
                    dve.wait_ge(s_y, m + 1)
                    dve.tensor_tensor(acc[:, m, :], acc[:, m, :], y_bank(m)[:, :], ALU.add)


def routed(nc, t, bank, ident, xs, ys, tile_expert, first_tile, whi, wlo, sb, sem):
    st = ExitStack()
    with st:
        staged = [sb(f"staged{i}", [P, WCOLS], F32, st) for i in range(2)]
        x = sb("xslot", [P, HID], F32, st)
        xhi = sb("xshi", [P, KC, P], F32R, st)
        xlo = sb("xslo", [P, KC, P], F32R, st)
        gate = sb("sgate", [P, INTER], F32, st)
        hid = sb("shid", [P, INTER], F32, st)
        hhi = sb("shhi", [P, HB, P], F32R, st)
        hlo = sb("shlo", [P, HB, P], F32R, st)
        y = sb("yslot", [P, HID], F32, st)

        st_in = [sem("staged_even", st), sem("staged_odd", st)]
        st_first = [sem("staged_first", st), sem("staged_second", st)]
        s_w_dve = sem("w_ready_dve", st)
        x_in, y_out = sem("xslot_in", st), sem("yslot_out", st)
        s_hi_act, s_hi_dve, s_w, s_xt, s_u1, s_u3, s_ht, s_dn, s_xhi, s_silu, s_hhi, s_y, s_xlo, s_h, s_hlo = (
            sem(n, st) for n in ("w_hi_act", "w_hi_dve", "w_ready", "m_xt", "m_up1", "m_up3", "m_ht", "m_down",
                                 "m_xhi", "m_silu", "m_hhi", "m_y", "m_xlo", "m_h", "m_hlo"))
        b_xt, b_ht, b_u1, b_u3, b_dn = bank[0], bank[1], bank[2], bank[3], bank[4]
        parts = {"act": slice(0, WCOLS // 2), "dve": slice(WCOLS // 2, WCOLS)}

        QUARTERS = 4
        LAST = E + NSH - 1
        s_last = sem("w_last_high", st)

        def quarter(q):
            return slice(q * WCOLS // QUARTERS, (q + 1) * WCOLS // QUARTERS)

        def first_of(eng, e):
            return eng.value_load(first_tile[0:1, e:e + 1], min_val=e + 1, max_val=MAXT - 1)

        def staged_in(eng, e):
            if e < 2:
                eng.wait_ge(st_first[e], 16 * QUARTERS)
            else:
                eng.wait_ge(st_in[e % 2], 16 * QUARTERS * (e // 2))

        def split_high(eng, copy, e, which, s_hi):
            if e >= RING:
                free_at = first_of(eng, e - RING + 1)
                eng.wait_ge(s_dn, free_at)
            staged_in(eng, e)
            copy(whi[:, e % RING, parts[which]], staged[e % 2][:, parts[which]]).then_inc(s_hi, 1)

        def split_last(dve, e):
            dve.wait_ge(s_hi_dve, e + 1)
            cols = quarter(QUARTERS - 1)
            dve.tensor_tensor(wlo[:, e % RING, cols], staged[e % 2][:, cols], whi[:, e % RING, cols].bitcast(F32),
                              ALU.subtract).then_inc(s_w_dve, 1)

        def flat(w):
            return w[:, :, :].rearrange("p s c -> p (s c)")

        with nc.Block() as block:
            @block.sync
            def _(sp):
                def load(g):
                    r = g * P if isinstance(g, int) else sp.snap(g * P)
                    if not isinstance(g, int):
                        sp.wait_ge(s_xt, g - 1)
                    sp.dma_start(x[:, :], xs[bass.ds(r, P), :]).then_inc(x_in, 16)

                load(1)
                for e in range(2):
                    for q in range(QUARTERS):
                        sp.dma_start(staged[e % 2][:, quarter(q)],
                                     t["wexp"][e, :, quarter(q)]).then_inc(st_first[e], 16)
                with sp.Fori(1, first_of(sp, E)) as g:
                    load(g + 1)

            @block.gpsimd
            def _(pool):
                def stage(e, q):
                    pool.dma_start(staged[e % 2][:, quarter(q)],
                                   t["wexp"][e, :, quarter(q)]).then_inc(st_in[e % 2], 16)

                for e in range(E + 1):
                    pool.wait_ge(s_hi_act, e + 1)
                    pool.wait_ge(s_hi_dve, e + 1)
                    for q in range(QUARTERS - 1):
                        pool.tensor_tensor(wlo[:, e % RING, quarter(q)], staged[e % 2][:, quarter(q)],
                                           whi[:, e % RING, quarter(q)].bitcast(F32), ALU.subtract).then_inc(s_w, 1)
                        if q and e + 2 < E + NSH:
                            pool.wait_ge(s_w, e * (QUARTERS - 1) + q)
                            stage(e + 2, q - 1)
                    if e + 2 < E + NSH:
                        pool.wait_ge(s_w, (e + 1) * (QUARTERS - 1))
                        stage(e + 2, QUARTERS - 2)
                        pool.wait_ge(s_w_dve, e + 1)
                        stage(e + 2, QUARTERS - 1)
                end = first_of(pool, E)
                pool.wait_ge(y_out, end * 16 + 16)
                pool.wait_ge(x_in, end * 16)

            @block.tensor
            def _(pe):
                def turn(g):
                    pe.wait_ge(x_in, g * 16)
                    if not isinstance(g, int):
                        pe.wait_ge(s_xlo, g - 1)
                    for k in range(KC):
                        mm = pe.transpose(b_xt[:, k * P:(k + 1) * P], x[:, k * P:(k + 1) * P], ident[:, :])
                    mm.then_inc(s_xt, 1)

                def up(g, w, slot):
                    if w == 0:
                        pe.wait_ge(s_xlo, g)
                    else:
                        pe.wait_ge(s_h, g)
                    dst = (b_u1, b_u3)[w][:, 0:INTER]
                    for k in range(KC):
                        lo_, hi_ = w13_cols(w, k)
                        mm = three_products(pe, dst, (xhi[:, k, :], xlo[:, k, :]),
                                            (whi[:, slot, lo_:hi_], wlo[:, slot, lo_:hi_]), k == 0, k == KC - 1)
                    mm.then_inc((s_u1, s_u3)[w], 1)

                def turn_hidden(g):
                    pe.wait_ge(s_h, g)
                    for b in range(HB):
                        rows = hb_rows(b)
                        mm = pe.transpose(b_ht[0:rows, b * P:(b + 1) * P], hid[:, b * P:b * P + rows], ident[:, :])
                    mm.then_inc(s_ht, 1)

                def down(g):
                    e = pe.value_load(tile_expert[0:1, bass.ds(g - 1, 1)], min_val=0, max_val=E - 1)
                    at = pe.snap((e % RING) * WCOLS)
                    pe.wait_ge(s_hlo, g)
                    for b in range(HB):
                        rows = hb_rows(b)
                        cols = bass.ds(at + w2_cols(b)[0], HID)
                        mm = three_products(pe, b_dn[:, :], (hhi[0:rows, b, :], hlo[0:rows, b, :]),
                                            (flat(whi)[0:rows, cols], flat(wlo)[0:rows, cols]), b == 0, b == HB - 1)
                    mm.then_inc(s_dn, 1)

                turn(1)
                for e in range(E):
                    pe.wait_ge(s_w, (e + 1) * (QUARTERS - 1))
                    pe.wait_ge(s_w_dve, e + 1)
                    with pe.Fori(first_of(pe, e), first_of(pe, e + 1)) as g:
                        up(g, 0, e % RING)
                        turn_hidden(g)
                        up(g, 1, e % RING)
                        turn(g + 1)
                        down(g)
                end = first_of(pe, E)
                turn_hidden(end)
                down(end)

            @block.scalar
            def _(act):
                def x_high(g):
                    act.wait_ge(s_xt, g)
                    act.copy(xhi[:, :, :], b_xt[:, :].rearrange("p (k t) -> p k t", k=KC)).then_inc(s_xhi, 1)

                def h_high(g):
                    act.wait_ge(s_ht, g)
                    act.copy(hhi[:, 0:2, :], b_ht[:, 0:2 * P].rearrange("p (b t) -> p b t", b=2))
                    rows = hb_rows(2)
                    act.copy(hhi[0:rows, 2, :], b_ht[0:rows, 2 * P:3 * P]).then_inc(s_hhi, 1)

                def y_store(g):
                    r = act.snap((g - 1) * P)
                    act.wait_ge(s_dn, g)
                    act.wait_ge(y_out, g * 16)
                    act.copy(y[:, :], b_dn[:, :]).then_inc(s_y, 1)
                    act.wait_ge(s_y, g)
                    act.dma_start(ys[bass.ds(r, P), :], y[:, :]).then_inc(y_out, 16)

                split_high(act, act.copy, 0, "act", s_hi_act)
                x_high(1)
                for e in range(E):
                    split_high(act, act.copy, e + 1, "act", s_hi_act)
                    with act.Fori(first_of(act, e), first_of(act, e + 1)) as g:
                        act.wait_ge(s_u1, g)
                        act.activation(gate[:, :], b_u1[:, 0:INTER], ACT.Silu).then_inc(s_silu, 1)
                        h_high(g)
                        x_high(g + 1)
                        y_store(g)
                end = first_of(act, E)
                h_high(end)
                y_store(end)
                staged_in(act, LAST)
                for q in range(QUARTERS):
                    act.copy(whi[:, LAST % RING, quarter(q)], staged[LAST % 2][:, quarter(q)]).then_inc(s_last, 1)

            @block.vector
            def _(dve):
                def x_low(g):
                    dve.wait_ge(s_xhi, g)
                    dve.tensor_tensor(xlo[:, :, :], b_xt[:, :].rearrange("p (k t) -> p k t", k=KC),
                                      xhi[:, :, :].bitcast(F32), ALU.subtract).then_inc(s_xlo, 1)

                def h_low(g):
                    dve.wait_ge(s_hhi, g)
                    dve.tensor_tensor(hlo[:, 0:2, :], b_ht[:, 0:2 * P].rearrange("p (b t) -> p b t", b=2),
                                      hhi[:, 0:2, :].bitcast(F32), ALU.subtract)
                    rows = hb_rows(2)
                    dve.tensor_tensor(hlo[0:rows, 2, :], b_ht[0:rows, 2 * P:3 * P],
                                      hhi[0:rows, 2, :].bitcast(F32), ALU.subtract).then_inc(s_hlo, 1)

                dve.memset(hid[:, :], 0.0).then_inc(s_h, 1)
                dve.memset(y[:, :], 0.0).then_inc(y_out, 16)
                split_high(dve, dve.tensor_copy, 0, "dve", s_hi_dve)
                split_last(dve, 0)
                x_low(1)
                for e in range(E):
                    split_high(dve, dve.tensor_copy, e + 1, "dve", s_hi_dve)
                    split_last(dve, e + 1)
                    with dve.Fori(first_of(dve, e), first_of(dve, e + 1)) as g:
                        h_low(g)
                        dve.wait_ge(s_silu, g)
                        dve.wait_ge(s_u3, g)
                        dve.tensor_tensor(hid[:, :], gate[:, :], b_u3[:, 0:INTER], ALU.mult).then_inc(s_h, 1)
                        x_low(g + 1)
                h_low(first_of(dve, E))
                for q in range(QUARTERS):
                    dve.wait_ge(s_last, q + 1)
                    dve.tensor_tensor(wlo[:, LAST % RING, quarter(q)], staged[LAST % 2][:, quarter(q)],
                                      whi[:, LAST % RING, quarter(q)].bitcast(F32), ALU.subtract)


def combine(nc, t, bank, acc, ident, ys, slots, pick_w, mv, rstd, neghalf, stats, whi, wlo, sb, sem):
    st = ExitStack()
    with st:
        NG = 3
        NB = NSH * HB
        LATE = EARLY * TPC
        got = [sb(f"got{i}", [P, PICK, HID], F32, st) for i in range(NG)]
        xhi = sb("late_xhi", [P, KC, CH], F32R, st)
        xlo = sb("late_xlo", [P, KC, CH], F32R, st)
        gate = [sb(f"late_gate{i}", [P, CH], F32, st) for i in range(2)]
        hid = [sb(f"late_hid{i}", [P, CH], F32, st) for i in range(2)]
        hhi = sb("late_hhi", [P, NB, CH], F32R, st)
        hlo = sb("late_hlo", [P, NB, CH], F32R, st)
        s_got = [sem(f"got{i}", st) for i in range(NG)]
        s_sum, s_st, s_mv, s_eps, s_pow, s_done, s_store = (sem(x, st) for x in (
            "ln2_sum", "ln2_stats", "ln2_mv", "ln2_eps", "ln2_pow", "ln2_done", "ln2_store"))
        s_xt, s_xhi, s_xlo, s_up, s_silu, s_hid, s_hhi, s_hlo, s_y, s_late = (sem(x, st) for x in (
            "late_xt", "late_xhi", "late_xlo", "late_up", "late_silu", "late_hid", "late_hhi", "late_hlo", "late_y",
            "late_added"))
        s_bias = sem("ln2_bias", st)
        b_y = (bank[6], bank[7], bank[0], bank[1])

        def slot(s):
            return (E + s) % RING

        with nc.Block() as block:
            @block.tensor
            def _(pe):
                for k in range(KC):
                    wait_for(pe, s_xlo, k - 1)
                    for i in range(TPC):
                        mm = pe.transpose(bank[k % 2][:, i * P:(i + 1) * P], acc[:, LATE + i, k * P:(k + 1) * P],
                                          ident[:, :])
                    mm.then_inc(s_xt, 1)
                pe.wait_ge(s_xlo, KC)
                for q in range(NB):
                    s, b = divmod(q, HB)
                    rows = hb_rows(b)
                    wait_for(pe, s_hid, q - 1)
                    for w in range(2):
                        for k in range(KC):
                            at = w13_cols(w, k)[0] + b * P
                            mm = three_products(pe, bank[2 + 2 * w + q % 2][0:rows, :],
                                                (whi[:, slot(s), at:at + rows], wlo[:, slot(s), at:at + rows]),
                                                (xhi[:, k, :], xlo[:, k, :]), k == 0, k == KC - 1)
                    mm.then_inc(s_up, 1)
                pe.wait_ge(s_hlo, NB)
                for i in range(TPC):
                    cols = slice(i * P, (i + 1) * P)
                    for q in range(NB):
                        s, b = divmod(q, HB)
                        rows = hb_rows(b)
                        lo_, hi_ = w2_cols(b)
                        mm = three_products(pe, b_y[i][:, :], (hhi[0:rows, q, cols], hlo[0:rows, q, cols]),
                                            (whi[0:rows, slot(s), lo_:hi_], wlo[0:rows, slot(s), lo_:hi_]),
                                            q == 0, q == NB - 1)
                    mm.then_inc(s_y, 1)

            @block.scalar
            def _(act):
                for k in range(KC):
                    act.wait_ge(s_xt, k + 1)
                    act.copy(xhi[:, k, :], bank[k % 2][:, :]).then_inc(s_xhi, 1)
                def silu(q):
                    rows = hb_rows(q % HB)
                    act.wait_ge(s_up, q + 1)
                    act.activation(gate[q % 2][0:rows, :], bank[2 + q % 2][0:rows, :], ACT.Silu).then_inc(s_silu, 1)

                def normed(n):
                    act.wait_ge(s_bias, n + 1)
                    act.activation(acc[:, n, :], acc[:, n, :], ACT.Identity, bias=mv[:, n, 1:2],
                                   scale=rstd[:, n:n + 1]).then_inc(s_done, 1)

                silu(0)
                for q in range(NB):
                    rows = hb_rows(q % HB)
                    act.wait_ge(s_hid, q + 1)
                    act.copy(hhi[0:rows, q, :], hid[q % 2][0:rows, :]).then_inc(s_hhi, 1)
                    if q + 1 < NB:
                        silu(q + 1)
                    normed(q)
                for n in range(NB, NT):
                    normed(n)

            @block.gpsimd
            def _(pool):
                def gather(n):
                    if n >= NG:
                        pool.wait_ge(s_sum, PICK * (n - NG + 1))
                    for k in range(PICK):
                        pool.indirect_dma_start(got[n % NG][:, k, :], None, ys[:, :],
                                                bass.IndirectOffsetOnAxis(ap=slots[:, n, k:k + 1], axis=0),
                                                bounds_check=MAXT * P - 1, oob_is_err=False).then_inc(s_got[n % NG], 16)

                def power(n):
                    pool.wait_ge(s_eps, n + 1)
                    pool.tensor_tensor(rstd[:, n:n + 1], rstd[:, n:n + 1], neghalf[:, 0:1], ALU.pow).then_inc(s_pow, 1)

                for n in range(NT):
                    gather(n)
                    if n >= NG:
                        power(n - NG)
                for n in range(NT - NG, NT):
                    power(n)

            @block.vector
            def _(dve):
                def less_mean(n):
                    dve.wait_ge(s_pow, n + 1)
                    dve.scalar_tensor_tensor(mv[:, n, 1:2], mv[:, n, 0:1], -1.0, rstd[:, n:n + 1],
                                             ALU.mult, ALU.mult).then_inc(s_bias, 1)

                def late_block(q):
                    rows = hb_rows(q % HB)
                    dve.wait_ge(s_silu, q + 1)
                    dve.tensor_tensor(hid[q % 2][0:rows, :], gate[q % 2][0:rows, :], bank[4 + q % 2][0:rows, :],
                                      ALU.mult).then_inc(s_hid, 1)
                    dve.wait_ge(s_hhi, q + 1)
                    dve.tensor_tensor(hlo[0:rows, q, :], hid[q % 2][0:rows, :], hhi[0:rows, q, :].bitcast(F32),
                                      ALU.subtract).then_inc(s_hlo, 1)

                for k in range(KC):
                    dve.wait_ge(s_xhi, k + 1)
                    dve.tensor_tensor(xlo[:, k, :], bank[k % 2][:, :], xhi[:, k, :].bitcast(F32),
                                      ALU.subtract).then_inc(s_xlo, 1)
                for n in range(NT):
                    if n >= LATE:
                        dve.wait_ge(s_y, n - LATE + 1)
                        dve.tensor_tensor(acc[:, n, :], acc[:, n, :], b_y[n - LATE][:, :], ALU.add).then_inc(s_late, 1)
                        dve.wait_ge(s_late, n - LATE + 1)
                    dve.wait_ge(s_got[n % NG], 16 * PICK * (n // NG + 1))
                    for k in range(PICK):
                        if k:
                            dve.wait_ge(s_sum, PICK * n + k)
                        dve.scalar_tensor_tensor(acc[:, n, :], got[n % NG][:, k, :], pick_w[:, n, k:k + 1],
                                                 acc[:, n, :], ALU.mult, ALU.add).then_inc(s_sum, 1)
                    if 1 <= n <= NB:
                        late_block(n - 1)
                    dve.wait_ge(s_sum, PICK * (n + 1))
                    dve.bn_stats(stats[:, n % 2, :], acc[:, n, :]).then_inc(s_st, 1)
                    dve.wait_ge(s_st, n + 1)
                    dve.bn_aggr(mv[:, n, :], stats[:, n % 2, :]).then_inc(s_mv, 1)
                    dve.wait_ge(s_mv, n + 1)
                    dve.tensor_scalar(rstd[:, n:n + 1], mv[:, n, 1:2], LN_EPS, None, ALU.add).then_inc(s_eps, 1)
                    if n:
                        less_mean(n - 1)
                less_mean(NT - 1)

            @block.sync
            def _(sp):
                for n in range(NT):
                    sp.wait_ge(s_done, n + 1)
                    sp.dma_start(t["out"][n * P:(n + 1) * P, :], acc[:, n, :]).then_inc(s_store, 16)
                sp.wait_ge(s_store, 16 * NT)


def kernel(**inputs):
    import concourse.bacc as bacc
    from concourse.bass_utils import run_bass_kernel_spmd as run

    a = {n.replace("L0_attn_", "").replace("L0_ffn_", "f_"): np.ascontiguousarray(x) for n, x in inputs.items()}
    x = a["hidden_states"][0]
    def by_head(w):
        return w.reshape(KC, P, NH, D).transpose(2, 1, 0, 3).reshape(NH, P, KC * D)
    wh = np.concatenate([
        by_head(a["Wq"]), by_head(a["Wlk"]), by_head(a["Wlv"]),
        a["bq"].reshape(NH, D, 1), a["blk"].reshape(NH, D, 1),
        np.broadcast_to(a["blv"].reshape(NH, 1, D), (NH, P, D)),
    ], axis=2)
    w1 = np.concatenate([a["f_w1"], a["f_sw1"].reshape(HID, NSH, INTER).transpose(1, 0, 2)])
    w3 = np.concatenate([a["f_w3"], a["f_sw3"].reshape(HID, NSH, INTER).transpose(1, 0, 2)])
    w2 = np.concatenate([a["f_w2"], a["f_sw2"].reshape(NSH, INTER, HID)])
    ne = E + NSH
    w2 = np.concatenate([w2, np.zeros((ne, HB * P - INTER, HID), np.float32)], axis=1)
    w13 = np.stack([w1, w3], axis=1).reshape(ne, 2, KC, P, INTER).transpose(0, 3, 1, 2, 4).reshape(ne, P, -1)
    wexp = np.concatenate([w13, w2.reshape(ne, HB, P, HID).transpose(0, 2, 1, 3).reshape(ne, P, -1)], axis=2)
    inv = np.float32(1.0) / np.float32(10000.0) ** (np.arange(ROT, dtype=np.float32) * np.float32(2.0 / (2 * ROT)))
    ang = np.arange(S, dtype=np.float32)[None, :] * inv.astype(np.float32)[:, None]
    cos, sin = np.cos(ang).astype(np.float32), np.sin(ang).astype(np.float32)
    cos_t = np.concatenate([cos, cos, np.ones((P - 2 * ROT, S), np.float32)])
    sin_t = np.concatenate([sin, -sin, sin, -sin])
    q, k = np.arange(P)[:, None], np.arange(2 * P)[None, :]
    sel = np.stack([(k[:, :P] == j * EPT + q // RATIO).astype(np.float32) for j in range(TPC)], axis=1)
    rel = q + P - k
    band = np.where((rel >= 0) & (rel <= P), 0.0, NEG).astype(np.float32)
    diag = np.where(np.arange(EPT)[None, :] * RATIO + RATIO - 1 <= q, 0.0, NEG).astype(np.float32)
    arrays = {
        "x": x, "sel": sel, "Wcmp": a["Wcmp"].reshape(1, HID), "bcmp": a["bcmp"].reshape(1, 1), "Wk": a["Wk"], "Wv": a["Wv"],
        "norm_w": np.stack([a["kn_w"], a["qn_w"], np.concatenate([a["kn_w"][:2 * ROT], a["qn_w"][:2 * ROT]])], axis=1), "bk": a["bk"].reshape(D, 1), "bv": a["bv"].reshape(1, D),
        "bo": a["bo"].reshape(1, HID), "wh": wh, "Wo": a["Wo"], "gateT": a["f_gate_w"].T,
        "ebias": a["f_expert_bias"].reshape(1, E), "wexp": wexp,
        "tri": np.stack([np.triu(np.ones((P, P), np.float32), 1), np.ones((P, P), np.float32)], axis=1),
        "ramp": np.arange(MAXT, dtype=np.float32).reshape(1, MAXT),
        "ident": np.eye(P, dtype=np.float32), "cos": cos_t, "sin": sin_t, "band": band, "diag": diag,
    }
    arrays = {n: np.ascontiguousarray(v) for n, v in arrays.items()}
    nc = bacc.Bacc("TRN2", target_bir_lowering=False, num_devices=1)
    t = {n: nc.dram_tensor(f"in_{n}", v.shape, F32, kind="ExternalInput").ap() for n, v in arrays.items()}
    out = nc.dram_tensor("out", [1, S, HID], F32, kind="ExternalOutput").ap()
    t["out"] = out[0, :, :]
    build(nc, t)
    r = run(nc, [{f"in_{n}": v for n, v in arrays.items()}], core_ids=[0])
    return r.results[0]["out"]
```
